# Optimizing a Trainium2 kernel written in Bass

```python
import numpy as np
import jax
import jax.numpy as jnp

def _softmax(x, axis=-1):
    return jax.nn.softmax(x, axis=axis)

def _gelu(x):
    return jax.nn.gelu(x, approximate=True)

def _silu(x):
    return jax.nn.silu(x)

def _sigmoid(x):
    return jax.nn.sigmoid(x)

def _layernorm(x, axis=-1, eps=1e-05):
    m = jnp.mean(x, axis=axis, keepdims=True)
    v = jnp.var(x, axis=axis, keepdims=True)
    return (x - m) / jnp.sqrt(v + eps)

def _scatter_add(tgt, idx, src, axis=0):
    return tgt.at[idx].add(src)

def _segment_sum(src, seg, n):
    return jax.ops.segment_sum(src, seg, n)
kernel_name = 'mk_gnn_preln_d2_gnn_r32_22181c'

def setup_inputs(seed: int=0):
    np.random.seed(seed)
    _w = jnp.asarray

    def _rec_inputs():
        import jax
        import jax.numpy as jnp
        _gk = jax.random.key(seed)
        x = -0.0005121 + 1.001 * jax.random.normal(jax.random.fold_in(_gk, 1), (3125, 32), jnp.float32)
        src = jax.random.randint(jax.random.fold_in(_gk, 2), (50000,), 0, 3125, jnp.int32)
        dst = jnp.minimum((3125 * jax.random.uniform(jax.random.fold_in(_gk, 3), (50000,)) ** 2.0).astype(jnp.int32), 99999)
        _o = jnp.argsort(dst, stable=True)
        src = src[_o]
        dst = dst[_o]
        edge_attr_32 = 0.000216709 + 1.00012 * jax.random.normal(jax.random.fold_in(_gk, 11), (50000, 32), jnp.float32)
        edge_attr_4 = 0.000714719 + 1.00021 * jax.random.normal(jax.random.fold_in(_gk, 12), (50000, 4), jnp.float32)
        edge_weight1 = 0.000614103 + 0.999867 * jax.random.normal(jax.random.fold_in(_gk, 14), (50000, 1), jnp.float32)
        return (x, src, dst, edge_attr_32, edge_attr_4, edge_weight1)
    x, src, dst, edge_attr_32, edge_attr_4, edge_weight1 = _rec_inputs()

    def _L0_gnn_setup():
        import jax, jax.numpy as jnp
        import numpy as np
        MUL = 8
        N_NODES = 3125
        N_EDGES = 25000
        EDGE_DIM = 32
        MLP_DIM = 64
        W_NUMEL = 4 * MUL * MUL
        ALPHA = 0.25
        C110 = 1.0 / np.sqrt(3.0)
        SI_SCALE = 1.0 / np.sqrt(MUL)
        key = jax.random.key(seed)
        ks = jax.random.split(key, 10)
        node_attr = jax.random.normal(ks[0], (N_NODES, 4 * MUL), dtype=jnp.float32)
        edge_index = jax.random.randint(ks[1], (2, N_EDGES), 0, N_NODES, dtype=jnp.int64)
        edge_sh = jax.random.normal(ks[2], (N_EDGES, 4), dtype=jnp.float32)
        edge_feat = jax.random.normal(ks[3], (N_EDGES, EDGE_DIM), dtype=jnp.float32)
        W1 = jax.random.normal(ks[4], (EDGE_DIM, MLP_DIM), dtype=jnp.float32) / np.sqrt(EDGE_DIM)
        b1 = jnp.zeros((MLP_DIM,), dtype=jnp.float32)
        W2 = jax.random.normal(ks[5], (MLP_DIM, W_NUMEL), dtype=jnp.float32) / np.sqrt(MLP_DIM)
        b2 = jnp.zeros((W_NUMEL,), dtype=jnp.float32)
        si_w0 = jax.random.normal(ks[6], (MUL, MUL), dtype=jnp.float32)
        si_w1 = jax.random.normal(ks[7], (MUL, MUL), dtype=jnp.float32)
        return {'node_attr': node_attr, 'edge_index': edge_index, 'edge_sh': edge_sh, 'edge_feat': edge_feat, 'W1': W1, 'b1': b1, 'W2': W2, 'b2': b2, 'si_w0': si_w0, 'si_w1': si_w1}
    _L0_gnn_all = _L0_gnn_setup()
    _L0_gnn_in = {k: v for k, v in _L0_gnn_all.items() if k in ('W1', 'b1', 'W2', 'b2', 'si_w0', 'si_w1')}
    del _L0_gnn_all

    def _L1_gnn_setup():
        import jax, jax.numpy as jnp
        import numpy as np
        N = 50000
        E = 25000
        H = 8
        C = 32
        L = 3
        NEG_SLOPE = 0.2
        BN_EPS = 1e-05

        def gatv2_layer(x, Wl, bl, Wr, br, att, bias, src, dst, n):
            xl = (x @ Wl + bl).reshape(n, H, C)
            xr = (x @ Wr + br).reshape(n, H, C)
            e = jax.nn.leaky_relu(xl[src] + xr[dst], NEG_SLOPE)
            logits = jnp.einsum('ehc,hc->eh', e, att)
            m = jax.ops.segment_max(logits, dst, num_segments=n)
            m = jnp.where(jnp.isfinite(m), m, 0.0)
            p = jnp.exp(logits - jax.lax.stop_gradient(m)[dst])
            denom = jax.ops.segment_sum(p, dst, num_segments=n)
            alpha = p / (denom[dst] + 1e-16)
            out = jax.ops.segment_sum(xl[src] * alpha[:, :, None], dst, num_segments=n)
            return out.mean(axis=1) + bias

        def batchnorm_train(x, gamma, beta):
            mu = x.mean(axis=0)
            var = x.var(axis=0)
            return (x - mu) * jax.lax.rsqrt(var + BN_EPS) * gamma + beta
        key = jax.random.key(seed)
        ks = jax.random.split(key, 8)
        s = 1.0 / np.sqrt(C)
        return {'patch_embs': jax.random.normal(ks[0], (N, C), jnp.float32), 'edge_index': jax.random.randint(ks[1], (2, E), 0, N, dtype=jnp.int32), 'edge_attr': jax.random.normal(ks[2], (E, 1), jnp.float32), 'Wl': jax.random.normal(ks[3], (L, C, H * C), jnp.float32) * s, 'bl': jnp.zeros((L, H * C), jnp.float32), 'Wr': jax.random.normal(ks[4], (L, C, H * C), jnp.float32) * s, 'br': jnp.zeros((L, H * C), jnp.float32), 'att': jax.random.normal(ks[5], (L, H, C), jnp.float32) * s, 'conv_bias': jnp.zeros((L, C), jnp.float32), 'bn_gamma': jnp.ones((L, C), jnp.float32), 'bn_beta': jnp.zeros((L, C), jnp.float32)}
    _L1_gnn_all = _L1_gnn_setup()
    _L1_gnn_in = {k: v for k, v in _L1_gnn_all.items() if k in ('Wl', 'bl', 'Wr', 'br', 'att', 'conv_bias', 'bn_gamma', 'bn_beta')}
    del _L1_gnn_all
    return {'x': x, 'src': src, 'dst': dst, 'edge_attr_32': edge_attr_32, 'edge_attr_4': edge_attr_4, 'edge_weight1': edge_weight1, 'L0_gnn_W1': _L0_gnn_in['W1'], 'L0_gnn_b1': _L0_gnn_in['b1'], 'L0_gnn_W2': _L0_gnn_in['W2'], 'L0_gnn_b2': _L0_gnn_in['b2'], 'L0_gnn_si_w0': _L0_gnn_in['si_w0'], 'L0_gnn_si_w1': _L0_gnn_in['si_w1'], 'L1_gnn_Wl': _L1_gnn_in['Wl'], 'L1_gnn_bl': _L1_gnn_in['bl'], 'L1_gnn_Wr': _L1_gnn_in['Wr'], 'L1_gnn_br': _L1_gnn_in['br'], 'L1_gnn_att': _L1_gnn_in['att'], 'L1_gnn_conv_bias': _L1_gnn_in['conv_bias'], 'L1_gnn_bn_gamma': _L1_gnn_in['bn_gamma'], 'L1_gnn_bn_beta': _L1_gnn_in['bn_beta']}

def reference(x, src, dst, edge_attr_32, edge_attr_4, edge_weight1, L0_gnn_W1, L0_gnn_b1, L0_gnn_W2, L0_gnn_b2, L0_gnn_si_w0, L0_gnn_si_w1, L1_gnn_Wl, L1_gnn_bl, L1_gnn_Wr, L1_gnn_br, L1_gnn_att, L1_gnn_conv_bias, L1_gnn_bn_gamma, L1_gnn_bn_beta):
    import jax
    import jax.numpy as jnp

    def _L0_gnn_ref(node_attr, edge_index, edge_sh, edge_feat, W1, b1, W2, b2, si_w0, si_w1):
        import jax, jax.numpy as jnp
        import numpy as np
        MUL = 8
        N_NODES = 3125
        N_EDGES = 25000
        EDGE_DIM = 32
        MLP_DIM = 64
        W_NUMEL = 4 * MUL * MUL
        ALPHA = 0.25
        C110 = 1.0 / np.sqrt(3.0)
        SI_SCALE = 1.0 / np.sqrt(MUL)
        n = node_attr.shape[0]
        e = edge_sh.shape[0]
        h = jax.nn.relu(edge_feat @ W1 + b1)
        w = (h @ W2 + b2).reshape(e, 4, MUL, MUL)
        w_000, w_011, w_101, w_110 = (w[:, 0], w[:, 1], w[:, 2], w[:, 3])
        s = node_attr[:, :MUL]
        v = node_attr[:, MUL:].reshape(n, MUL, 3)
        src, dst = (edge_index[0], edge_index[1])
        s_e = s[src]
        v_e = v[src]
        sh0 = edge_sh[:, 0]
        sh1 = edge_sh[:, 1:4]
        m0 = ALPHA * (jnp.einsum('ei,eio->eo', s_e * sh0[:, None], w_000) + C110 * jnp.einsum('eim,em,eio->eo', v_e, sh1, w_110))
        m1 = ALPHA * (jnp.einsum('ei,em,eio->eom', s_e, sh1, w_011) + jnp.einsum('eim,eio->eom', v_e * sh0[:, None, None], w_101))
        out0 = jax.ops.segment_sum(m0, dst, num_segments=n)
        out1 = jax.ops.segment_sum(m1.reshape(e, MUL * 3), dst, num_segments=n).reshape(n, MUL, 3)
        out0 = out0 + SI_SCALE * (s @ si_w0)
        out1 = out1 + SI_SCALE * jnp.einsum('nim,io->nom', v, si_w1)
        return jnp.concatenate([out0, out1.reshape(n, MUL * 3)], axis=-1)

    def _L1_gnn_ref(patch_embs, edge_index, edge_attr, Wl, bl, Wr, br, att, conv_bias, bn_gamma, bn_beta):
        import jax, jax.numpy as jnp
        import numpy as np
        N = 50000
        E = 25000
        H = 8
        C = 32
        L = 3
        NEG_SLOPE = 0.2
        BN_EPS = 1e-05

        def gatv2_layer(x, Wl, bl, Wr, br, att, bias, src, dst, n):
            xl = (x @ Wl + bl).reshape(n, H, C)
            xr = (x @ Wr + br).reshape(n, H, C)
            e = jax.nn.leaky_relu(xl[src] + xr[dst], NEG_SLOPE)
            logits = jnp.einsum('ehc,hc->eh', e, att)
            m = jax.ops.segment_max(logits, dst, num_segments=n)
            m = jnp.where(jnp.isfinite(m), m, 0.0)
            p = jnp.exp(logits - jax.lax.stop_gradient(m)[dst])
            denom = jax.ops.segment_sum(p, dst, num_segments=n)
            alpha = p / (denom[dst] + 1e-16)
            out = jax.ops.segment_sum(xl[src] * alpha[:, :, None], dst, num_segments=n)
            return out.mean(axis=1) + bias

        def batchnorm_train(x, gamma, beta):
            mu = x.mean(axis=0)
            var = x.var(axis=0)
            return (x - mu) * jax.lax.rsqrt(var + BN_EPS) * gamma + beta
        n = patch_embs.shape[0]
        loops = jnp.arange(n, dtype=edge_index.dtype)
        src = jnp.concatenate([edge_index[0], loops])
        dst = jnp.concatenate([edge_index[1], loops])
        x = patch_embs
        h1 = gatv2_layer(x, Wl[0], bl[0], Wr[0], br[0], att[0], conv_bias[0], src, dst, n)
        x = batchnorm_train(jax.nn.leaky_relu(h1, 0.01) + x, bn_gamma[0], bn_beta[0])
        h2 = gatv2_layer(x, Wl[1], bl[1], Wr[1], br[1], att[1], conv_bias[1], src, dst, n)
        x = batchnorm_train(jax.nn.leaky_relu(h2, 0.01) + x, bn_gamma[1], bn_beta[1])
        h3 = gatv2_layer(x, Wl[2], bl[2], Wr[2], br[2], att[2], conv_bias[2], src, dst, n)
        x = batchnorm_train(h3 + x, bn_gamma[2], bn_beta[2])
        return x
    edge_index = jnp.stack([src, dst])
    h = jnp.maximum(_layernorm(x, axis=-1), 0.0)
    x = x + _L0_gnn_ref(h, edge_index, edge_attr_4, edge_attr_32, L0_gnn_W1, L0_gnn_b1, L0_gnn_W2, L0_gnn_b2, L0_gnn_si_w0, L0_gnn_si_w1)
    h = jnp.maximum(_layernorm(x, axis=-1), 0.0)
    x = x + _L1_gnn_ref(h, edge_index, edge_weight1, L1_gnn_Wl, L1_gnn_bl, L1_gnn_Wr, L1_gnn_br, L1_gnn_att, L1_gnn_conv_bias, L1_gnn_bn_gamma, L1_gnn_bn_beta)
    return x

_drawn_inputs = setup_inputs


def setup_inputs(seed=0):
    import zlib

    import numpy as np

    out = dict(_drawn_inputs(seed))
    spreads = {'L0_gnn_b1': (0.0, 0.1),
     'L0_gnn_b2': (0.0, 0.1),
     'L1_gnn_bl': (0.0, 0.8),
     'L1_gnn_br': (0.0, 0.8),
     'L1_gnn_conv_bias': (0.0, 0.514),
     'L1_gnn_bn_gamma': (1.0, 0.2),
     'L1_gnn_bn_beta': (0.0, 0.1)}
    factors = {'L1_gnn_Wr': 3.753}
    for name, (base, spread) in spreads.items():
        noise = np.random.default_rng([zlib.crc32(name.encode()), seed]).standard_normal(out[name].shape)
        drawn = base * np.exp(spread * noise) if base else spread * noise
        out[name] = jnp.asarray(drawn.astype(out[name].dtype))
    for name, factor in factors.items():
        out[name] = (out[name] * factor).astype(out[name].dtype)
    return out
```

```python
import concourse.bass as bass
from concourse import mybir
from contextlib import ExitStack

F32 = mybir.dt.float32
BF16 = mybir.dt.bfloat16
I32 = mybir.dt.int32
ALU = mybir.AluOpType
ACT = mybir.ActivationFunctionType
AX = mybir.AxisListType

P = 128
N, E, C = 3125, 50000, 32
NB = 25
NP = NB * P
REAL = N - (NB - 1) * P
CH = 16
J = 25
T = CH * J
EP = T * P
CE = J * P
H, HC = 8, 256
ROW = C + H
VW = HC + 2 * H
MW = C + 1
ST = 4
NS = T // ST
ITEMS = NS + NB - 1
PAD_NODE = NP - 1
BIG = 1e30
EPS = 1e-5
L = 3
MUL, MLP = 8, 64
ALPHA = 0.25
C110 = 3.0 ** -0.5
SI = 8.0 ** -0.5
GATHER = 16


class Chain:

    def __init__(self, eng, sem):
        self.eng, self.sem, self.n, self.base = eng, sem, 0, None

    def value(self):
        return self.n if self.base is None else self.base + self.n

    def mark(self, ins):
        ins.then_inc(self.sem, 1)
        self.n += 1
        return self.value()

    def link(self, ins):
        self.mark(ins)
        self.eng.wait_ge(self.sem, self.value())

    def enter(self, i, start, per):
        self.out, self.per = self.n, per
        self.base, self.n = i * per + (self.out - start * per), 0

    def leave(self, rounds):
        assert self.n == self.per, (self.n, self.per)
        self.n, self.base = self.out + self.per * rounds, None


def build(nc, A, out):
    ctx = ExitStack()
    with ctx, nc.allow_non_contiguous_dma(reason="small vectors and list transposes"):
        def sb(name, shape, dt=F32):
            return ctx.enter_context(nc.sbuf_tensor(name, shape, dt))

        def dram(name, shape, dt=F32):
            return nc.dram_tensor(name, shape, dt, kind="Internal").ap()

        dst_pad = dram("dst_pad", (EP + 2,), I32)
        src_pad = dram("src_pad", (EP,), I32)
        ea32_pad = dram("ea32_pad", (EP, C))
        table_src = dram("table_src", (NP, ROW))
        table_dst = dram("table_dst", (NP, ROW))
        ends_d = dram("ends_d", (P, 2))
        pens_d = dram("pens_d", (P, 2))
        carry_d = dram("carry_d", (H, 2, CH))
        walk_d = dram("walk_d", (2, P))

        ident = sb("ident", [P, P])
        ones = sb("ones", [P, P])
        iota_f = sb("iota_f", [P, P])
        iota_i = sb("iota_i", [P, P], I32)
        part_f = sb("part_f", [P, 1])
        nodemask = sb("nodemask", [P, NB])
        src_all = sb("src_all", [P, T + 2])
        dst_all = sb("dst_all", [P, T + 2])
        srcf, dstf = src_all[:, 0:T], dst_all[:, 0:T]
        lastf = sb("lastf", [P, T])
        start_pen = sb("start_pen", [P, CE], BF16)
        end_pen = sb("end_pen", [P, CE], BF16)
        pens = sb("pens", [H, 2, CH])
        walk_t = sb("walk_t", [1, P], I32)
        walk_b = sb("walk_b", [1, P], I32)
        base128 = sb("base128", [P, P])
        xres = sb("xres", [P, NB, C])
        feat = sb("feat", [P, NB, C])
        tabs = sb("tabs", [P, NB, ROW])
        tabd = sb("tabd", [P, NB, ROW])
        lself = sb("lself", [P, NB, H])
        count = sb("count", [P, NB])
        xsr = sb("xsr", [P, T, MW])
        pm = sb("pm", [P, T, 2 * H])
        ring = sb("ring", [P, 2, CH, 2 * ROW])
        gate = sb("gate", [P, 2])
        stage = sb("stage", [P, 2, 2 * CH], I32)
        work = sb("work", [P, 8192 + CE])
        logit = work[:, 8192:8192 + CE]
        slotV = work[:, 0:2 * ST * VW].rearrange("p (s t w) -> p s t w", s=2, t=ST)
        slotO = work[:, 2 * ST * VW:2 * ST * (VW + P)].rearrange("p (s t w) -> p s t w", s=2, t=ST)
        acc = work[:, 3200:3200 + NB * VW].rearrange("p (b w) -> p b w", b=NB)
        conv = work[:, 10000:10000 + NB * C].rearrange("p (b c) -> p b c", c=C)
        featT = work[0:C + 1, 0:NP]
        drel = sb("drel", [P, 2, ST])
        small = sb("small", [P, 1024])
        wst = sb("wst", [P, HC])
        wl_aug = sb("wl_aug", [C + 1, HC])
        wr_aug = sb("wr_aug", [C + 1, HC])
        wz = sb("wz", [C + 1, HC + 2 * H])
        attb = sb("attb", [P, HC])
        attc = sb("attc", [P, 2])
        attp = sb("attp", [P, 2, P])
        bz = sb("bz", [P, 4])
        wlr = sb("wlr", [P, 2, C])
        vecs = sb("vecs", [P, 4, HC])
        w1_sb = sb("w1_sb", [C, MLP])
        b1_sb = sb("b1_sb", [MLP, 1])
        w2_sb = sb("w2_sb", [MLP + 1, HC])
        siw = sb("siw", [C, C])
        ea4 = sb("ea4", [P, T, 4])

        ps = ctx.enter_context(nc.psum_tensor("ps", [P, 8, 512], F32))
        psf = ps[:, :, :].rearrange("p a b -> p (a b)")

        XT = work[:, 0:2048].rearrange("p (s q e) -> p s q e", s=2, e=P)
        RE = work[:, 2048:4096].rearrange("p (s h e) -> p s h e", s=2, h=2)
        LIN = work[:, 4096:4352].rearrange("p (s e) -> p s e", s=2)
        XP = work[:, 4352:6400].rearrange("p (s q g r) -> p s q g r", s=2, q=4, g=4)
        EA = work[:, 0:1024].rearrange("p (s c k) -> p s c k", s=2, k=C)
        EAT = work[0:C, 1024:2048].rearrange("p (s e) -> p s e", s=2)
        H1T = work[0:MLP + 1, 2048:3072].rearrange("p (s e) -> p s e", s=2)
        COEF = work[:, 3072:3840].rearrange("p (c r i) -> p c r i", c=CH, r=6)
        PROD = work[:, 3840:5376].rearrange("p (s t r) -> p s t r", s=2, t=2)
        RED = work[:, 5376:6144].rearrange("p (c r o) -> p c r o", c=CH, r=6)
        TMP = work[:, 6144:6528].rearrange("p (c i m) -> p c i m", c=CH, m=3)
        SCAN_F = work[:, 0:CE]
        SCAN_B = work[:, CE:2 * CE]

        names = [0]

        class Phase:

            def __enter__(self):
                self.ctx, self.sems = ExitStack(), []
                names[0] += 1
                return self

            def sem(self, name):
                self.sems.append(nc.alloc_semaphore(name=f"{name}_{names[0]}"))
                return self.sems[-1]

            def block(self):
                return self.ctx.enter_context(nc.Block())

            def __exit__(self, *a):
                self.ctx.close()
                nc.clear_and_free_semaphores(self.sems)
                nc.all_engine_barrier()

        def row_bcast(ap, parts=P):
            return ap.partition_broadcast(parts)

        with Phase() as ph:
            s_x, s_pads, s_pool, s_dma, s_c = (ph.sem(n) for n in ("x_in", "pads_set", "pool_step", "pad_copies", "dve_step"))
            block = ph.block()
            padi = small[0:1, 0:1024].bitcast(I32)
            minus = stage[0:1, 0, 0:1]

            @block.gpsimd
            def _(e):
                ch = Chain(e, s_pool)
                ch.link(e.memset(ident[:, :], 0.0))
                ch.link(e.affine_select(out=ident[:, :], in_=ident[:, :], compare_op=ALU.not_equal, fill=1.0,
                                        base=0, pattern=[[-1, P]], channel_multiplier=1))
                ch.link(e.memset(nodemask[:, :], 1.0))
                ch.link(e.affine_select(out=nodemask[:, NB - 1:NB], in_=nodemask[:, NB - 1:NB], compare_op=ALU.is_gt,
                                        fill=0.0, base=REAL, pattern=[[0, 1]], channel_multiplier=-1))
                ch.link(e.iota(iota_i[:, :], pattern=[[1, P]], base=0, channel_multiplier=0))
                ch.link(e.tensor_copy(iota_f[:, :], iota_i[:, :]))
                ch.link(e.iota(iota_i[:, 0:1], pattern=[[0, 1]], base=0, channel_multiplier=1))
                ch.link(e.tensor_copy(part_f[:, :], iota_i[:, 0:1]))

            @block.vector
            def _(e):
                ch = Chain(e, s_c)
                v = nc.vector
                v.memset(padi, PAD_NODE).then_inc(s_pads, 1)
                v.memset(minus, -1).then_inc(s_pads, 1)
                v.memset(work[:, 0:C], 0.0).then_inc(s_pads, 1)
                v.memset(ones[:, :], 1.0)
                v.memset(src_all[:, T:], 0.0)
                v.memset(dst_all[:, T:], 0.0)
                v.memset(xsr[:, :, :], 0.0)
                v.memset(ring[:, :, :, :], 0.0)
                v.memset(ea4[:, :, :], 0.0).then_inc(s_pads, 1)
                ch.link(v.memset(xres[:, :, :], 0.0))
                v.memset(siw[:, :], 0.0).then_inc(s_pads, 1)

            @block.sync
            def _(e):
                e.wait_ge(s_pads, 5)
                e.wait_ge(s_c, 1)
                n = 0
                pads = EP + 1 - E
                e.dma_start(dst_pad[0:1].rearrange("(a n) -> a n", a=1), minus).then_inc(s_dma, 16)
                e.dma_start(dst_pad[1:E + 1], A["dst"]).then_inc(s_dma, 16)
                e.dma_start(src_pad[0:E], A["src"]).then_inc(s_dma, 16)
                n = 3
                for o in range(0, pads, 1024):
                    w = min(1024, pads - o)
                    e.dma_start(dst_pad[1 + E + o:1 + E + o + w].rearrange("(a n) -> a n", a=1), padi[:, 0:w]).then_inc(s_dma, 16)
                    w = min(1024, EP - E - o)
                    e.dma_start(src_pad[E + o:E + o + w].rearrange("(a n) -> a n", a=1), padi[:, 0:w]).then_inc(s_dma, 16)
                    n += 2
                e.dma_start(ea32_pad[0:E, :], A["edge_attr_32"]).then_inc(s_dma, 16)
                full = E // P
                e.dma_start(ea4[:, 0:full, :], A["edge_attr_4"][0:full * P, :].rearrange("(t p) k -> p t k", p=P)).then_inc(s_dma, 16)
                e.dma_start(ea4[0:E - full * P, full, :], A["edge_attr_4"][full * P:E, :]).then_inc(s_dma, 16)
                e.dma_start(xres[:, 0:NB - 1, :], A["x"][0:(NB - 1) * P, :].rearrange("(b p) c -> p b c", p=P)).then_inc(s_dma, 16)
                e.dma_start(xres[0:REAL, NB - 1, :], A["x"][(NB - 1) * P:N, :]).then_inc(s_dma, 16)
                e.dma_start(w1_sb[:, :], A["L0_gnn_W1"]).then_inc(s_dma, 16)
                e.dma_start(b1_sb[:, :], A["L0_gnn_b1"].rearrange("(p a) -> p a", a=1)).then_inc(s_dma, 16)
                e.dma_start(w2_sb[0:MLP, :], A["L0_gnn_W2"]).then_inc(s_dma, 16)
                e.dma_start(w2_sb[MLP:MLP + 1, :], A["L0_gnn_b2"].rearrange("(a n) -> a n", a=1)).then_inc(s_dma, 16)
                e.dma_start(siw[0:MUL, 0:MUL], A["L0_gnn_si_w0"]).then_inc(s_dma, 16)
                n += 10
                for m in range(3):
                    e.dma_start(siw[MUL + m:C:3, MUL + m:C:3], A["L0_gnn_si_w1"]).then_inc(s_dma, 16)
                    n += 1
                e.wait_ge(s_dma, 16 * n)

            @block.scalar
            def _(e):
                e.wait_ge(s_pads, 3)
                k = 0
                for o in range(E, EP, P):
                    w = min(P, EP - o)
                    e.dma_start(ea32_pad[o:o + w, :], work[0:w, 0:C]).then_inc(s_x, 16)
                    k += 1
                e.wait_ge(s_x, 16 * k)

        TR = T // 4
        with Phase() as ph:
            s_in, s_t, s_c, s_w, s_rep = (ph.sem(n) for n in ("lists_in", "lists_turned", "dve_step", "walk_out", "dst_in"))
            s_conv = ph.sem("lists_float")
            block = ph.block()
            rows = [logit[0:TR, k * 512:(k + 1) * 512] for k in range(3)]
            rowsf = [logit[0:TR, (3 + k) * 512:(4 + k) * 512] if k < 3 else None for k in range(3)]
            rep = work[:, 0:CE + 2].bitcast(I32)
            repf = work[:, CE + 2:2 * CE + 4]
            lastd = small[:, 0:NS].bitcast(I32)
            key = small[:, 128:128 + NS]
            cmpk = small[:, 256:256 + NS]
            tk = small[:, 384:388]

            @block.sync
            def _(e):
                for k, a in enumerate((src_pad[0:EP], dst_pad[1:EP + 1], dst_pad[2:EP + 2])):
                    e.dma_start(rows[k].bitcast(I32), a.rearrange("(p n) -> p n", n=512)).then_inc(s_in, 16)
                e.dma_start(lastd, row_bcast(dst_pad[1:EP + 1].rearrange("(s n) -> s n", n=ST * P)[:, ST * P - 1]),).then_inc(s_in, 16)
                for c in range(CH):
                    e.dma_start(rep[c * H:(c + 1) * H, :], row_bcast(dst_pad[c * CE:(c + 1) * CE + 2], H)).then_inc(s_rep, 16)
                e.wait_ge(s_w, 1)
                e.dma_start(walk_d.rearrange("a p -> p a"), tk[:, 0:2]).then_inc(s_w, 16)
                e.dma_start(pens_d, small[:, 400:402]).then_inc(s_w, 16)
                e.wait_ge(s_w, 33)
                e.dma_start(small[0:1, 512:512 + P], walk_d[0:1, :]).then_inc(s_w, 16)
                e.dma_start(small[0:1, 640:640 + P], walk_d[1:2, :]).then_inc(s_w, 16)
                e.dma_start(base128[:, :], row_bcast(walk_d[1, :])).then_inc(s_w, 16)
                for k in range(2):
                    e.dma_start(pens[:, k, :], pens_d[:, k].rearrange("(c h) -> h c", h=H)).then_inc(s_w, 16)
                e.wait_ge(s_w, 33 + 80)

            @block.vector
            def _(e):
                v = nc.vector
                ch = Chain(e, s_c)
                e.wait_ge(s_in, 64)
                for k in range(3):
                    ch.link(v.tensor_copy(rowsf[k], rows[k].bitcast(I32)))
                v.memset(small[:, 1000:1001], 0.0).then_inc(s_conv, 1)
                ch.link(v.tensor_scalar(lastd, lastd, 7, None, ALU.arith_shift_right))
                ch.link(v.tensor_copy(key, lastd))
                ch.link(v.tensor_tensor(key, key, iota_f[:, 0:NS], ALU.add))
                ch.link(v.tensor_scalar(cmpk, key, part_f[:, 0:1], None, ALU.is_lt))
                ch.link(v.tensor_reduce(tk[:, 2:3], cmpk, AX.X, ALU.add))
                ch.link(v.tensor_scalar(tk[:, 0:1], tk[:, 2:3], float(ST), None, ALU.mult))
                ch.link(v.tensor_tensor(tk[:, 1:2], part_f[:, 0:1], tk[:, 2:3], ALU.subtract))
                e.wait_ge(s_rep, 16 * CH)
                ch.link(v.tensor_copy(repf, rep))
                ch.link(v.tensor_tensor(work[:, 0:CE], repf[:, 1:CE + 1], repf[:, 0:CE], ALU.not_equal))
                ch.link(v.tensor_scalar(start_pen[:, :], work[:, 0:CE], -BIG, None, ALU.mult))
                ch.link(v.tensor_tensor(work[:, 0:CE], repf[:, 1:CE + 1], repf[:, 2:CE + 2], ALU.not_equal))
                ch.link(v.tensor_scalar(end_pen[:, :], work[:, 0:CE], -BIG, None, ALU.mult))
                ch.link(v.tensor_reduce(small[:, 400:401], start_pen[:, :], AX.X, ALU.min))
                ch.link(v.tensor_reduce(small[:, 401:402], end_pen[:, :], AX.X, ALU.min))
                v.memset(small[:, 1001:1002], 0.0).then_inc(s_w, 1)
                e.wait_ge(s_t, 3)
                for k, o in enumerate((srcf, dstf, lastf)):
                    ch.link(v.tensor_copy(o[:, :].rearrange("p (a b) -> p b a", b=4),
                                          psf[:, k * 512:k * 512 + 4 * TR].rearrange("p (b a) -> p b a", b=4)))
                ch.link(v.tensor_tensor(lastf[:, :], lastf[:, :], dstf[:, :], ALU.not_equal))
                ch.link(v.tensor_copy(xsr[:, :, C], lastf[:, :]))
                e.wait_ge(s_w, 33 + 80)
                ch.link(v.tensor_copy(walk_t[:, :], small[0:1, 512:512 + P]))
                ch.link(v.tensor_copy(walk_b[:, :], small[0:1, 640:640 + P]))
                ch.link(v.tensor_scalar(base128[:, :], base128[:, :], float(P), None, ALU.mult))

            @block.tensor
            def _(e):
                e.wait_ge(s_conv, 1)
                for k in range(3):
                    for b in range(4):
                        last = nc.tensor.transpose(psf[:, k * 512 + b * TR:k * 512 + (b + 1) * TR],
                                                   rowsf[k][:, b * P:(b + 1) * P], ident[0:TR, 0:TR])
                    last.then_inc(s_t, 1)

        def layer_norm_relu(src, dst):
            with Phase() as ph:
                s_c, s_q = ph.sem("dve_step"), ph.sem("root")
                block = ph.block()
                mu, var = small[:, 0:NB], small[:, 32:32 + NB]
                sq = work[:, 0:NB * C].rearrange("p (b c) -> p b c", c=C)

                @block.vector
                def _(e):
                    v = nc.vector
                    ch = Chain(e, s_c)
                    ch.link(v.tensor_reduce(mu, src[:, :, :], AX.X, ALU.add))
                    ch.link(v.tensor_scalar(mu, mu, 1.0 / C, None, ALU.mult))
                    ch.link(v.tensor_tensor(dst[:, :, :], src[:, :, :], mu[:, :, None].to_broadcast([P, NB, C]), ALU.subtract))
                    ch.link(v.tensor_tensor(sq, dst[:, :, :], dst[:, :, :], ALU.mult))
                    ch.link(v.tensor_reduce(var, sq, AX.X, ALU.add))
                    ch.link(v.tensor_scalar(var, var, 1.0 / C, EPS, ALU.mult, ALU.add))
                    n = ch.n
                    e.wait_ge(s_q, 1)
                    ch.link(v.reciprocal(mu, var))
                    ch.link(v.tensor_tensor(dst[:, :, :], dst[:, :, :], mu[:, :, None].to_broadcast([P, NB, C]), ALU.mult))
                    ch.link(v.tensor_scalar(dst[:, :, :], dst[:, :, :], 0.0, None, ALU.max))

                @block.scalar
                def _(e):
                    e.wait_ge(s_c, 6)
                    nc.scalar.activation(var, var, ACT.Sqrt).then_inc(s_q, 1)

        def turn_features():
            with Phase() as ph:
                s_t = ph.sem("turned")
                s_e = ph.sem("copied")
                block = ph.block()
                groups = [(g, min(4, NB - g)) for g in range(0, NB, 4)]

                @block.vector
                def _(e):
                    nc.vector.memset(featT[C:C + 1, :], 1.0)

                @block.tensor
                def _(e):
                    for g, w in groups:
                        for b in range(w):
                            last = nc.tensor.transpose(ps[0:C, g // 4, b * P:(b + 1) * P], feat[:, g + b, :], ident[:, :])
                        last.then_inc(s_t, 1)

                @block.scalar
                def _(e):
                    for g, w in groups:
                        e.wait_ge(s_t, g // 4 + 1)
                        nc.scalar.activation(featT[0:C, g * P:(g + w) * P], ps[0:C, g // 4, 0:w * P], ACT.Copy).then_inc(s_e, 1)

        def write_tables(both):
            with Phase() as ph:
                s_o = ph.sem("tables_out")
                block = ph.block()

                @block.sync
                def _(e):
                    e.dma_start(table_src.rearrange("(b p) c -> p b c", p=P), tabs[:, :, :]).then_inc(s_o, 16)
                    if both:
                        e.dma_start(table_dst.rearrange("(b p) c -> p b c", p=P), tabd[:, :, :]).then_inc(s_o, 16)
                    e.wait_ge(s_o, 32 if both else 16)

        def by_chunk(a):
            return a.rearrange("p (c j) -> p j c", j=J)

        src_jc, dst_jc = by_chunk(srcf[:, :]), by_chunk(dstf[:, :])
        src_next, dst_next = by_chunk(src_all[:, 2:T + 2]), by_chunk(dst_all[:, 2:T + 2])

        def gather_program(e, s_ready, s_gath, s_gate, both):
            def window(par, need):
                e.wait_ge(s_ready[par], need)
                e.tensor_tensor(gate[:, par:par + 1], ones[:, 0:1], ones[:, 0:1], ALU.add).then_inc(s_gate, 1)
                for c in range(CH):
                    for k, tab in ((0, table_src), (1, table_dst))[:2 if both else 1]:
                        e.indirect_dma_start(
                            out=ring[:, par, c, k * ROW:(k + 1) * ROW], out_offset=None, in_=tab[:, :],
                            in_offset=bass.IndirectOffsetOnAxis(ap=stage[:, par, k * CH + c:k * CH + c + 1], axis=0),
                        ).then_inc(s_gath[par], GATHER)
            window(0, 1)
            window(1, 1)
            with e.Fori(1, J // 2) as i:
                window(0, i + 1)
                window(1, i + 1)
            window(0, J // 2 + 1)

        def pairs(e, body, chains=()):
            body(0, 0, 0)
            body(1, 1, 0)
            with e.Fori(1, J // 2) as i:
                for ch, per in chains:
                    ch.enter(i, 1, per)
                body(2 * i, 0, i)
                body(2 * i + 1, 1, i)
                for ch, per in chains:
                    ch.leave(J // 2 - 1)
            body(J - 1, 0, J // 2)

        def first(x):
            return isinstance(x, int)

        def wait(e, sem, x):
            if not (isinstance(x, int) and x <= 0):
                e.wait_ge(sem, x)

        layer_norm_relu(xres, feat)
        with Phase() as ph:
            s_c = ph.sem("dve_step")
            block = ph.block()

            @block.vector
            def _(e):
                ch = Chain(e, s_c)
                ch.link(nc.vector.memset(tabs[:, :, :], 0.0))
                ch.link(nc.vector.tensor_copy(tabs[:, :, 0:C], feat[:, :, :]))
                ch.link(nc.vector.memset(work[:, 2048:3072], 1.0))
                for par in range(2):
                    nc.vector.tensor_copy(stage[:, par, 0:CH], src_jc[:, par, :])
        write_tables(False)

        GW = CH * GATHER
        with Phase() as ph:
            s_ready = [ph.sem("staged0"), ph.sem("staged1")]
            s_gath = [ph.sem("gathered0"), ph.sem("gathered1")]
            s_gate = ph.sem("gate_passed")
            s_ea = [ph.sem("attr0"), ph.sem("attr1")]
            s_t, s_tc, s_h, s_hr, s_w, s_pr, s_c, s_red = (
                ph.sem(n) for n in ("attr_turned", "attr_copied", "hidden", "hidden_relu", "weights", "products", "dve_step", "reduced"))
            block = ph.block()

            @block.gpsimd
            def _(e):
                gather_program(e, s_ready, s_gath, s_gate, False)

            @block.sync
            def _(e):
                ea_v = ea32_pad.rearrange("(c j p) k -> j p c k", c=CH, p=P)

                def window(j, par, i):
                    wait(e, s_t, 4 * j - 4 if not first(j) or j >= 2 else 0)
                    e.dma_start(EA[:, par, :, :], ea32_rows(j)).then_inc(s_ea[par], 16)

                def ea32_rows(j):
                    if first(j):
                        return ea_v[j]
                    return ea_v[bass.ds(j, 1)].rearrange("a p c k -> (a p) c k")
                pairs(e, window)

            @block.tensor
            def _(e):
                def turn(j, par, i, g):
                    if g == 0:
                        e.wait_ge(s_ea[par], 16 * i + 16)
                    wait(e, s_tc, 4 * j + g - 1)
                    for k in range(4):
                        last = nc.tensor.transpose(ps[0:C, g % 2, k * P:(k + 1) * P], EA[:, par, 4 * g + k, :], ident[:, :])
                    last.then_inc(s_t, 1)

                def hidden(j, g):
                    e.wait_ge(s_tc, 4 * j + g + 1)
                    wait(e, s_hr, 4 * j + g - 1)
                    nc.tensor.matmul(ps[0:MLP, 2 + g % 2, :], w1_sb[:, :], EAT[:, g % 2, :], start=True, stop=True).then_inc(s_h, 1)

                def weights(j, g):
                    e.wait_ge(s_hr, 4 * j + g + 1)
                    wait(e, s_pr, 8 * j + 2 * g - 2)
                    for k in range(4):
                        last = nc.tensor.matmul(ps[:, 4 + 2 * (g % 2) + k // 2, (k % 2) * HC:(k % 2 + 1) * HC],
                                                H1T[:, g % 2, k * P:(k + 1) * P], w2_sb[:, :], start=True, stop=True)
                        if k % 2:
                            last.then_inc(s_w, 1)

                def window(j, par, i):
                    turn(j, par, i, 0)
                    for g in range(4):
                        hidden(j, g)
                        if g < 3:
                            turn(j, par, i, g + 1)
                        weights(j, g)
                pairs(e, window)

            @block.scalar
            def _(e):
                def window(j, par, i):
                    for g in range(4):
                        e.wait_ge(s_t, 4 * j + g + 1)
                        wait(e, s_h, 4 * j + g - 1)
                        nc.scalar.activation(EAT[:, g % 2, :], ps[0:C, g % 2, :], ACT.Copy).then_inc(s_tc, 1)
                        e.wait_ge(s_h, 4 * j + g + 1)
                        wait(e, s_w, 8 * j + 2 * g - 2)
                        nc.scalar.activation(H1T[0:MLP, g % 2, :], ps[0:MLP, 2 + g % 2, :], ACT.Relu,
                                             bias=b1_sb[:, :]).then_inc(s_hr, 1)
                pairs(e, window)

            @block.vector
            def _(e):
                v = nc.vector
                ch = Chain(e, s_c)
                v.memset(small[:, 0:1], 0.0).then_inc(s_ready[0], 1)
                v.memset(small[:, 1:2], 0.0).then_inc(s_ready[1], 1)
                per = 2 * (14 + 8 * 3)

                def window(j, par, i):
                    at = bass.ds(j, 1) if not first(j) else slice(j, j + 1)
                    sh = ea4[:, :, :].rearrange("p (c j) k -> p j c k", j=J)[:, at, :, :].rearrange("p a c k -> p (a c) k")
                    e.wait_ge(s_gath[par], GW * i + GW)
                    x = ring[:, par, :, :]
                    xv = x[:, :, MUL:C].rearrange("p c (i m) -> p c i m", m=3)
                    sh0 = sh[:, :, 0:1]
                    ch.link(v.tensor_scalar(COEF[:, :, 1, :], x[:, :, 0:MUL], ALPHA, None, ALU.mult))
                    ch.mark(v.tensor_tensor(COEF[:, :, 0, :], COEF[:, :, 1, :], sh0.to_broadcast([P, CH, MUL]), ALU.mult))
                    for m in range(3):
                        ch.mark(v.tensor_tensor(TMP[:, :, :, m], xv[:, :, :, m], sh[:, :, 1 + m:2 + m].to_broadcast([P, CH, MUL]), ALU.mult))
                    for m in range(3):
                        ch.link(v.tensor_tensor(COEF[:, :, 2 + m, :], xv[:, :, :, m], sh0.to_broadcast([P, CH, MUL]), ALU.mult))
                    ch.link(v.tensor_reduce(COEF[:, :, 5, :], TMP[:, :, :, :], AX.X, ALU.add))
                    ch.mark(v.tensor_scalar(COEF[:, :, 2:5, :], COEF[:, :, 2:5, :], ALPHA, None, ALU.mult))
                    ch.link(v.tensor_scalar(COEF[:, :, 5, :], COEF[:, :, 5, :], ALPHA * C110, None, ALU.mult))
                    if not (first(j) and j + 2 >= J):
                        e.wait_ge(s_gate, j + 1)
                        v.tensor_copy(stage[:, par, 0:CH], src_next[:, at, :].rearrange("p a c -> p (a c)")).then_inc(s_ready[par], 1)
                    for u in range(8):
                        e.wait_ge(s_w, 8 * j + u + 1)
                        W = ps[:, 4 + u % 4, :].rearrange("p (t r) -> p t r", t=2)
                        pr = PROD[:, u % 2, :, :]
                        cf = COEF[:, 2 * u:2 * u + 2, :, :].rearrange("p t r i -> p t (r i)")
                        v.tensor_tensor(pr[:, :, 0:128].rearrange("p t (k o) -> p t k o", o=MUL),
                                        W[:, :, 0:128].rearrange("p t (k o) -> p t k o", o=MUL),
                                        cf[:, :, 0:16, None].to_broadcast([P, 2, 16, MUL]), ALU.mult)
                        for m in range(3):
                            v.tensor_tensor(pr[:, :, 128 + 64 * m:192 + 64 * m].rearrange("p t (k o) -> p t k o", o=MUL),
                                            W[:, :, 128:192].rearrange("p t (k o) -> p t k o", o=MUL),
                                            cf[:, :, 16 + 8 * m:24 + 8 * m, None].to_broadcast([P, 2, MUL, MUL]), ALU.mult)
                        last = v.tensor_tensor(pr[:, :, 320:384].rearrange("p t (k o) -> p t k o", o=MUL),
                                               W[:, :, 192:256].rearrange("p t (k o) -> p t k o", o=MUL),
                                               cf[:, :, 40:48, None].to_broadcast([P, 2, MUL, MUL]), ALU.mult)
                        last.then_inc(s_pr, 1)
                        e.wait_ge(s_pr, 8 * j + u + 1)
                        v.tensor_reduce(RED[:, 2 * u:2 * u + 2, :, :].rearrange("p t r o -> p (t r) o"),
                                        pr.rearrange("p t (r i o) -> p (t r) o i", i=MUL, o=MUL), AX.X, ALU.add).then_inc(s_red, 1)
                    e.wait_ge(s_red, 8 * j + 8)
                    msg = xsr[:, :, :].rearrange("p (c j) k -> p j c k", j=J)[:, at, :, :].rearrange("p a c k -> p (a c) k")
                    ch.mark(v.tensor_tensor(msg[:, :, 0:MUL], RED[:, :, 0, :], RED[:, :, 5, :], ALU.add))
                    mv = msg[:, :, MUL:C].rearrange("p c (o m) -> p c o m", m=3)
                    for m in range(3):
                        ch.link(v.tensor_tensor(TMP[:, :, :, m], RED[:, :, 1, :], sh[:, :, 1 + m:2 + m].to_broadcast([P, CH, MUL]), ALU.mult))
                    for m in range(3):
                        ch.link(v.tensor_tensor(mv[:, :, :, m], TMP[:, :, :, m], RED[:, :, 2 + m, :], ALU.add))

                pairs(e, window, [(ch, 2 * 18)])

        def segment_sums(width, edge_values):
            with Phase() as ph:
                s_v, s_mm, s_acc, s_c, s_d = (ph.sem(n) for n in ("values", "sums", "added", "zeroed", "relative"))
                block = ph.block()

                @block.vector
                def _(e):
                    v = nc.vector
                    v.memset(acc[:, :, :], 0.0).then_inc(s_acc, 1)

                    def make(k, slot):
                        at = first(k) and slice(k, k + 1) or bass.ds(k, 1)
                        t4 = e.value_load(walk_t[0:1, at], min_val=0, max_val=T - ST)
                        v.tensor_tensor(drel[:, slot, :], dstf[:, bass.ds(t4, ST)], base128[:, at].to_broadcast([P, ST]),
                                        ALU.subtract).then_inc(s_d, 1)
                        wait(e, s_mm, k - 1)
                        n = edge_values(v, slot, t4)
                        e.wait_ge(s_d, k + 1)
                        v.tensor_tensor(slotO[:, slot, :, :], iota_f[:, None, :].to_broadcast([P, ST, P]),
                                        drel[:, slot, :, None].to_broadcast([P, ST, P]), ALU.is_equal).then_inc(s_v, 1)

                    def add(k, slot):
                        at = first(k) and slice(k, k + 1) or bass.ds(k, 1)
                        b = e.value_load(walk_b[0:1, at], min_val=0, max_val=NB - 1)
                        e.wait_ge(s_mm, k + 1)
                        e.wait_ge(s_acc, k + 1)
                        row = acc[:, bass.ds(b, 1), 0:width].rearrange("p a w -> p (a w)")
                        v.tensor_tensor(row, row, ps[:, slot, 0:width], ALU.add).then_inc(s_acc, 1)
                    make(0, 0)
                    make(1, 1)
                    add(0, 0)
                    with e.Fori(1, ITEMS // 2) as i:
                        make(2 * i, 0)
                        add(2 * i - 1, 1)
                        make(2 * i + 1, 1)
                        add(2 * i, 0)
                    add(ITEMS - 1, 1)

                @block.tensor
                def _(e):
                    def item(k, slot):
                        e.wait_ge(s_v, k + 1)
                        wait(e, s_acc, k if not (first(k) and k < 2) else 0)
                        for t in range(ST):
                            last = nc.tensor.matmul(ps[:, slot, 0:width], slotO[:, slot, t, :], slotV[:, slot, t, 0:width],
                                                    start=(t == 0), stop=(t == ST - 1))
                        last.then_inc(s_mm, 1)
                    item(0, 0)
                    item(1, 1)
                    with e.Fori(1, ITEMS // 2) as i:
                        item(2 * i, 0)
                        item(2 * i + 1, 1)

        def message_values(v, slot, t4):
            v.tensor_copy(slotV[:, slot, :, 0:MW], xsr[:, bass.ds(t4, ST), :])

        segment_sums(MW, message_values)
        turn_features()

        with Phase() as ph:
            s_m, s_c = ph.sem("self"), ph.sem("dve_step")
            s_w = ph.sem("scaled")
            block = ph.block()

            @block.vector
            def _(e):
                v = nc.vector
                ch = Chain(e, s_c)
                v.tensor_scalar(siw[:, :], siw[:, :], SI, None, ALU.mult).then_inc(s_w, 1)
                ch.link(v.tensor_copy(count[:, :], acc[:, :, C]))
                ch.link(v.tensor_tensor(xres[:, :, :], xres[:, :, :], acc[:, :, 0:C], ALU.add))
                e.wait_ge(s_m, 1)
                ch.link(v.tensor_tensor(xres[:, 0:16, :], xres[:, 0:16, :], ps[:, 0, :].rearrange("p (b c) -> p b c", c=C), ALU.add))
                ch.link(v.tensor_tensor(xres[:, 16:NB, :], xres[:, 16:NB, :],
                                        ps[:, 1, 0:(NB - 16) * C].rearrange("p (b c) -> p b c", c=C), ALU.add))

            @block.tensor
            def _(e):
                e.wait_ge(s_w, 1)
                for b in range(NB):
                    last = nc.tensor.matmul(psf[:, b * C:(b + 1) * C], featT[0:C, b * P:(b + 1) * P], siw[:, :], start=True, stop=True)
                last.then_inc(s_m, 1)
        layer_norm_relu(xres, feat)

        for l in range(L):
            Wl, Wr = A["L1_gnn_Wl"][l], A["L1_gnn_Wr"][l]
            bl, br = A["L1_gnn_bl"][l], A["L1_gnn_br"][l]
            att = A["L1_gnn_att"][l].rearrange("h c -> (h c)")
            turn_features()
            with Phase() as ph:
                s_in, s_c = ph.sem("weights_in"), ph.sem("dve_step")
                block = ph.block()

                @block.sync
                def _(e):
                    n = 0
                    for k, w in enumerate((Wl, Wr, Wl, Wr)):
                        e.dma_start(wst[k * C:(k + 1) * C, :], w).then_inc(s_in, 16)
                    for dst_t, w, b in ((wl_aug, Wl, bl), (wr_aug, Wr, br)):
                        e.dma_start(dst_t[0:C, :], w).then_inc(s_in, 16)
                        e.dma_start(dst_t[C:C + 1, :], b.rearrange("(a n) -> a n", a=1)).then_inc(s_in, 16)
                    e.dma_start(attb[:, :], row_bcast(att)).then_inc(s_in, 16)
                    e.dma_start(attc[:, :], att.rearrange("(k p) -> p k", p=P)).then_inc(s_in, 16)
                    e.dma_start(bz[:, 0:2], bl.rearrange("(k p) -> p k", p=P)).then_inc(s_in, 16)
                    e.dma_start(bz[:, 2:4], br.rearrange("(k p) -> p k", p=P)).then_inc(s_in, 16)
                    for h in range(H):
                        e.dma_start(wlr[(h % 4) * C:(h % 4 + 1) * C, h // 4, :], Wl[:, h * C:(h + 1) * C]).then_inc(s_in, 16)
                    e.dma_start(vecs[:, 0, :], row_bcast(bl)).then_inc(s_in, 16)
                    for k, name in enumerate(("conv_bias", "bn_gamma", "bn_beta")):
                        e.dma_start(vecs[:, 1 + k, 0:C], row_bcast(A["L1_gnn_" + name][l])).then_inc(s_in, 16)
                    e.wait_ge(s_in, 16 * 24)

                @block.vector
                def _(e):
                    v = nc.vector
                    ch = Chain(e, s_c)
                    ch.link(v.memset(attp[:, :, :], 0.0))
                    e.wait_ge(s_in, 16 * 24)
                    ch.link(v.tensor_scalar(attb[:, :], attb[:, :], 0.8, None, ALU.mult))
                    ch.link(v.tensor_scalar(attc[:, :], attc[:, :], 0.8, None, ALU.mult))
                    for h in range(H):
                        a, half = h % 4, h // 4
                        v.tensor_copy(attp[a * C:(a + 1) * C, half, h:P:40], attc[a * C:(a + 1) * C, half:half + 1].to_broadcast([C, 4]))
                    ch.link(v.tensor_tensor(bz[:, 0:2], bz[:, 0:2], bz[:, 2:4], ALU.add))
                    ch.link(v.tensor_tensor(wz[:, 0:HC], wl_aug[:, :], wr_aug[:, :], ALU.add))
                    for k, w in enumerate((wl_aug, wr_aug)):
                        ch.link(v.tensor_tensor(w[:, :], w[:, :], attb[0:C + 1, :], ALU.mult))
                        ch.link(v.tensor_reduce(wz[:, HC + k * H:HC + (k + 1) * H], w[:, :].rearrange("p (h c) -> p h c", c=C), AX.X, ALU.add))
                    ch.link(v.tensor_scalar(wz[:, HC:], wz[:, HC:], 0.25, None, ALU.mult))
                    ch.link(v.tensor_scalar(wlr[:, :, :], wlr[:, :, :], 1.0 / H, None, ALU.mult))
                    ch.link(v.tensor_reduce(small[:, 0:C], vecs[:, 0, :].rearrange("p (h c) -> p c h", c=C), AX.X, ALU.add))
                    ch.link(v.scalar_tensor_tensor(vecs[:, 1, 0:C], small[:, 0:C], 1.0 / H, vecs[:, 1, 0:C], ALU.mult, ALU.add))

            with Phase() as ph:
                s_z, s_r, s_l, s_c, s_p = (ph.sem(n) for n in ("self_z", "self_relu", "self_logit", "dve_step", "self_prod"))
                block = ph.block()
                rz = work[:, 3200:3712].rearrange("p (s n) -> p s n", s=2)

                @block.tensor
                def _(e):
                    for b in range(NB):
                        wait(e, s_l, b - 1)
                        nc.tensor.matmul(ps[:, b % 2, 0:HC + 2 * H], featT[:, b * P:(b + 1) * P], wz[:, :], start=True, stop=True).then_inc(s_z, 1)

                @block.scalar
                def _(e):
                    for b in range(NB):
                        e.wait_ge(s_z, b + 1)
                        wait(e, s_l, b - 1)
                        nc.scalar.activation(rz[:, b % 2, :], ps[:, b % 2, 0:HC], ACT.Relu).then_inc(s_r, 1)

                @block.vector
                def _(e):
                    v = nc.vector
                    ch = Chain(e, s_c)
                    v.tensor_copy(tabs[:, :, 0:C], feat[:, :, :])
                    v.tensor_copy(tabd[:, :, 0:C], feat[:, :, :])
                    for par in range(2):
                        v.tensor_copy(stage[:, par, 0:CH], src_jc[:, par, :])
                        v.tensor_copy(stage[:, par, CH:], dst_jc[:, par, :])
                    for b in range(NB):
                        e.wait_ge(s_r, b + 1)
                        v.tensor_tensor(rz[:, b % 2, :], rz[:, b % 2, :], attb[:, :], ALU.mult).then_inc(s_p, 1)
                        v.tensor_copy(tabs[:, b, C:], ps[:, b % 2, HC:HC + H])
                        ch.mark(v.tensor_copy(tabd[:, b, C:], ps[:, b % 2, HC + H:HC + 2 * H]))
                        e.wait_ge(s_p, b + 1)
                        v.tensor_reduce(lself[:, b, :], rz[:, b % 2, :].rearrange("p (h c) -> p h c", c=C), AX.X, ALU.add).then_inc(s_l, 1)
                    e.wait_ge(s_l, NB)
                    e.wait_ge(s_c, ch.n)
                    ch.link(v.tensor_tensor(lself[:, :, :], lself[:, :, :], tabs[:, :, C:], ALU.add))
                    ch.link(v.tensor_tensor(lself[:, :, :], lself[:, :, :], tabd[:, :, C:], ALU.add))
            write_tables(True)

            GWB = 2 * CH * GATHER
            with Phase() as ph:
                s_ready = [ph.sem("staged0"), ph.sem("staged1")]
                s_gath = [ph.sem("gathered0"), ph.sem("gathered1")]
                s_gate = ph.sem("gate_passed")
                s_lin, s_xp, s_tr, s_xt, s_z, s_r, s_q, s_xs, s_lge = (
                    ph.sem(n) for n in ("linear", "packed", "turned", "turned_copied", "z", "relu", "logits", "src_kept", "logits_out"))
                block = ph.block()

                @block.gpsimd
                def _(e):
                    gather_program(e, s_ready, s_gath, s_gate, True)

                def quad_chunks(q):
                    return [q, q + 4, q + 8, q + 12]

                @block.tensor
                def _(e):
                    def z(j, par, q):
                        wait(e, s_r, 8 * j + 2 * q - 2)
                        for half in range(2):
                            for side in range(2):
                                last = nc.tensor.matmul(ps[:, 2 + 2 * (q % 2) + side, half * 256:(half + 1) * 256],
                                                        wst[64 * side:64 * side + 64, half * P:(half + 1) * P],
                                                        XT[64 * side:64 * side + 64, par, 2 * q:2 * q + 2, :],
                                                        start=True, stop=True)
                        last.then_inc(s_z, 1)

                    def logits(j, par, q):
                        e.wait_ge(s_r, 8 * j + 2 * q + 2)
                        for half in range(2):
                            for g in range(4):
                                last = nc.tensor.matmul(ps[32 * g:32 * g + 32, 6 + par, 0:P], attp[:, half, 32 * q:32 * q + 32],
                                                        RE[:, q % 2, half, (g % 2) * 256 + (g // 2) * P:(g % 2) * 256 + (g // 2) * P + P],
                                                        start=False, stop=(q == 3 and half == 1), skip_group_check=True)
                        last.then_inc(s_q, 1)

                    def window(j, par, i):
                        e.wait_ge(s_xp, 2 * j + 2)
                        wait(e, s_xt, j)
                        for q in range(4):
                            for pr in range(2):
                                rows = XP[:, par, q, 2 * pr:2 * pr + 2, :].rearrange("p g r -> p (g r)")
                                last = nc.tensor.transpose(psf[:, (2 * q + pr) * P:(2 * q + pr + 1) * P], rows, ident[:, :])
                        last.then_inc(s_tr, 1)
                        e.wait_ge(s_lin, j + 1)
                        wait(e, s_lge, j - 1)
                        nc.tensor.matmul(ps[:, 6 + par, 0:P], LIN[:, par, :], ident[:, :], start=True, stop=False, skip_group_check=True)
                        e.wait_ge(s_xt, j + 1)
                        z(j, par, 0)
                        for q in range(1, 4):
                            z(j, par, q)
                            logits(j, par, q - 1)
                        logits(j, par, 3)
                    pairs(e, window)

                @block.scalar
                def _(e):
                    def window(j, par, i):
                        at = bass.ds(j, 1) if not first(j) else slice(j, j + 1)
                        e.wait_ge(s_gath[par], GWB * i + GWB)
                        kept = xsr[:, :, :].rearrange("p (c j) k -> p j c k", j=J)[:, at, :, 0:C].rearrange("p a c k -> p (a c) k")
                        nc.scalar.activation(kept, ring[:, par, :, 0:C], ACT.Copy).then_inc(s_xs, 1)
                        for q in range(4):
                            e.wait_ge(s_z, 4 * j + q + 1)
                            wait(e, s_q, 4 * j + q - 1)
                            for half in range(2):
                                nc.scalar.activation(RE[:, q % 2, half, :].rearrange("p (s e) -> p s e", s=2),
                                                     ps[:, 2 + 2 * (q % 2):4 + 2 * (q % 2), half * 256:(half + 1) * 256],
                                                     ACT.Relu, bias=bz[:, half:half + 1]).then_inc(s_r, 1)
                        e.wait_ge(s_q, 4 * j + 4)
                        col = bass.ds(j * P, P) if not first(j) else slice(j * P, j * P + P)
                        nc.scalar.activation(logit[:, col], ps[:, 6 + par, 0:P], ACT.Copy).then_inc(s_lge, 1)
                    pairs(e, window)

                @block.vector
                def _(e):
                    v = nc.vector
                    v.memset(small[:, 0:1], 0.0).then_inc(s_ready[0], 1)
                    v.memset(small[:, 1:2], 0.0).then_inc(s_ready[1], 1)

                    def window(j, par, i):
                        e.wait_ge(s_gath[par], GWB * i + GWB)
                        wait(e, s_tr, j - 1)
                        for k in range(2):
                            v.tensor_copy(XP[:, par, :, :, k * C:(k + 1) * C],
                                          ring[:, par, :, k * ROW:k * ROW + C].rearrange("p (g q) r -> p q g r", q=4)).then_inc(s_xp, 1)
                        wait(e, s_q, 4 * j - 4)
                        v.tensor_tensor(LIN[:, par, :].rearrange("p (c h) -> p c h", h=H), ring[:, par, :, C:ROW],
                                        ring[:, par, :, ROW + C:], ALU.add).then_inc(s_lin, 1)
                        e.wait_ge(s_tr, j + 1)
                        v.tensor_copy(XT[:, par, :, :], psf[:, 0:1024].rearrange("p (q e) -> p q e", e=P)).then_inc(s_xt, 1)
                        if not (first(j) and j + 2 >= J):
                            e.wait_ge(s_gate, j + 1)
                            at = bass.ds(j, 1) if not first(j) else slice(j, j + 1)
                            e.wait_ge(s_xs, j + 1)
                            e.wait_ge(s_lin, j + 1)
                            e.wait_ge(s_xp, 2 * j + 2)
                            v.tensor_copy(stage[:, par, 0:CH], src_next[:, at, :].rearrange("p a c -> p (a c)"))
                            v.tensor_copy(stage[:, par, CH:], dst_next[:, at, :].rearrange("p a c -> p (a c)")).then_inc(s_ready[par], 1)
                    pairs(e, window)

            with Phase() as ph:
                s_c, s_d, s_e, s_t, s_o = (ph.sem(n) for n in ("dve_step", "carries", "exp", "turned", "copied"))
                block = ph.block()
                ends = small[:, 0:2]
                carry = small[:, 4:6]
                eh = small[0:H, 16:16 + 2 * CH].rearrange("p (k c) -> p k c", k=2)
                cc = small[0:H, 64:64 + 2 * (CH + 1)].rearrange("p (k c) -> p k c", k=2)
                probs = logit

                @block.vector
                def _(e):
                    v = nc.vector
                    ch = Chain(e, s_c)
                    ch.mark(v.tensor_tensor_scan(SCAN_F, start_pen[:, :], logit[:, :], -BIG, ALU.add, ALU.max))
                    ch.link(v.tensor_tensor_scan(SCAN_B[:, ::-1], end_pen[:, ::-1], logit[:, ::-1], -BIG, ALU.add, ALU.max))
                    ch.link(v.tensor_copy(ends[:, 0:1], SCAN_F[:, CE - 1:CE]))
                    ch.link(v.tensor_copy(ends[:, 1:2], SCAN_B[:, 0:1]))
                    ch.link(v.memset(small[0:H, 64:64 + 2 * (CH + 1)], -BIG))
                    e.wait_ge(s_d, 48)
                    ch.mark(v.tensor_tensor_scan(cc[:, 0, 1:CH + 1], pens[:, 0, :], eh[:, 0, :], -BIG, ALU.add, ALU.max))
                    ch.link(v.tensor_tensor_scan(cc[:, 1, 0:CH][:, ::-1], pens[:, 1, ::-1], eh[:, 1, ::-1], -BIG, ALU.add, ALU.max))
                    e.wait_ge(s_d, 112)
                    ch.mark(v.tensor_tensor_scan(SCAN_F, start_pen[:, :], logit[:, :], carry[:, 0:1], ALU.add, ALU.max))
                    ch.link(v.tensor_tensor_scan(SCAN_B[:, ::-1], end_pen[:, ::-1], logit[:, ::-1], carry[:, 1:2], ALU.add, ALU.max))
                    ch.link(v.tensor_tensor(SCAN_F, SCAN_F, SCAN_B, ALU.max))
                    ch.link(v.tensor_tensor(logit[:, :], logit[:, :], SCAN_F, ALU.subtract))
                    for j in range(J):
                        e.wait_ge(s_t, j + 1)
                        pmv = pm[:, :, :].rearrange("p (c j) k -> p j c k", j=J)[:, j, :, :]
                        lj = lastf[:, :].rearrange("p (c j) -> p j c", j=J)[:, j, :, None].to_broadcast([P, CH, H])
                        v.tensor_copy(pmv[:, :, 0:H], ps[:, j % 2, 0:P].rearrange("p (c h) -> p c h", h=H))
                        v.tensor_tensor(pmv[:, :, H:], ps[:, j % 2, P:2 * P].rearrange("p (c h) -> p c h", h=H), lj, ALU.mult).then_inc(s_o, 1)

                @block.sync
                def _(e):
                    e.wait_ge(s_c, 5)
                    e.dma_start(ends_d, ends).then_inc(s_d, 16)
                    e.wait_ge(s_d, 16)
                    for k in range(2):
                        e.dma_start(eh[:, k, :], ends_d[:, k].rearrange("(c h) -> h c", h=H)).then_inc(s_d, 16)
                    e.wait_ge(s_c, 7)
                    e.dma_start(carry_d[:, 0, :], cc[:, 0, 0:CH]).then_inc(s_d, 16)
                    e.dma_start(carry_d[:, 1, :], cc[:, 1, 1:CH + 1]).then_inc(s_d, 16)
                    e.wait_ge(s_d, 80)
                    for k in range(2):
                        e.dma_start(carry[:, k:k + 1], carry_d[:, k, :].rearrange("h c -> c h")).then_inc(s_d, 16)

                @block.scalar
                def _(e):
                    e.wait_ge(s_c, 11)
                    nc.scalar.activation(logit[:, :], logit[:, :], ACT.Exp).then_inc(s_e, 1)

                @block.tensor
                def _(e):
                    e.wait_ge(s_e, 1)
                    for j in range(J):
                        wait(e, s_o, j - 1)
                        nc.tensor.transpose(ps[:, j % 2, 0:P], logit[:, j * P:(j + 1) * P], ident[:, :])
                        nc.tensor.transpose(ps[:, j % 2, P:2 * P], SCAN_F[:, j * P:(j + 1) * P], ident[:, :]).then_inc(s_t, 1)

            def attention_values(v, slot, t4):
                v.tensor_copy(slotV[:, slot, :, HC:], pm[:, bass.ds(t4, ST), :])
                v.tensor_tensor(slotV[:, slot, :, 0:HC].rearrange("p t (h c) -> p t h c", c=C),
                                pm[:, bass.ds(t4, ST), 0:H, None].to_broadcast([P, ST, H, C]),
                                xsr[:, bass.ds(t4, ST), None, 0:C].to_broadcast([P, ST, H, C]), ALU.mult)

            segment_sums(VW, attention_values)

            with Phase() as ph:
                s_c, s_x = ph.sem("dve_step"), ph.sem("exps")
                block = ph.block()
                NH = NB * H
                m1 = small[:, 0:NH].rearrange("p (b h) -> p b h", h=H)
                m2 = small[:, NH:2 * NH].rearrange("p (b h) -> p b h", h=H)
                w12 = small[:, 0:2 * NH]
                mx = small[:, 2 * NH:3 * NH].rearrange("p (b h) -> p b h", h=H)
                cb = small[:, 3 * NH:3 * NH + NB]

                @block.vector
                def _(e):
                    v = nc.vector
                    ch = Chain(e, s_c)
                    ch.link(v.tensor_scalar(cb, count[:, :], -1.0, BIG, ALU.add, ALU.mult))
                    ch.link(v.tensor_tensor(m1, acc[:, :, HC + H:], cb[:, :, None].to_broadcast([P, NB, H]), ALU.add))
                    ch.link(v.tensor_tensor(mx, m1, lself[:, :, :], ALU.max))
                    ch.link(v.tensor_tensor(m1, m1, mx, ALU.subtract))
                    ch.link(v.tensor_tensor(m2, lself[:, :, :], mx, ALU.subtract))
                    e.wait_ge(s_x, 1)
                    ch.link(v.tensor_tensor(mx, acc[:, :, HC:HC + H], m1, ALU.mult))
                    ch.link(v.tensor_tensor(mx, mx, m2, ALU.add))
                    ch.link(v.tensor_scalar(mx, mx, 1e-16, None, ALU.add))
                    ch.link(v.reciprocal(mx, mx))
                    ch.link(v.tensor_tensor(m1, m1, mx, ALU.mult))
                    ch.link(v.tensor_tensor(m2, m2, mx, ALU.mult))
                    for g in range(0, NB, 5):
                        a = acc[:, g:g + 5, 0:HC].rearrange("p b (h c) -> p b h c", c=C)
                        t = work[:, 0:5 * HC].rearrange("p (b h c) -> p b h c", h=H, c=C)
                        ch.mark(v.tensor_tensor(a, a, m1[:, g:g + 5, :, None].to_broadcast([P, 5, H, C]), ALU.mult))
                        ch.link(v.tensor_tensor(t, feat[:, g:g + 5, None, :].to_broadcast([P, 5, H, C]),
                                                m2[:, g:g + 5, :, None].to_broadcast([P, 5, H, C]), ALU.mult))
                        ch.link(v.tensor_tensor(a, a, t, ALU.add))

                @block.scalar
                def _(e):
                    e.wait_ge(s_c, 5)
                    nc.scalar.activation(w12, w12, ACT.Exp).then_inc(s_x, 1)

            with Phase() as ph:
                s_t, s_a, s_m, s_o = (ph.sem(n) for n in ("turned", "turned_copied", "heads", "conv"))
                block = ph.block()
                G = 5
                AT = work[:, 0:2 * G * P].rearrange("p (b k n) -> p b k n", b=G, k=2)

                @block.tensor
                def _(e):
                    for g in range(NB // G):
                        wait(e, s_a, g)
                        for b in range(G):
                            for k in range(2):
                                last = nc.tensor.transpose(psf[:, (2 * b + k) * P:(2 * b + k + 1) * P], acc[:, g * G + b, k * P:(k + 1) * P], ident[:, :])
                        last.then_inc(s_t, 1)
                        e.wait_ge(s_a, g + 1)
                        wait(e, s_o, g - 1)
                        for b in range(G):
                            for k in range(2):
                                last = nc.tensor.matmul(ps[:, 4 + g % 2, b * C:(b + 1) * C], AT[:, b, k, :], wlr[:, k, :], start=(k == 0), stop=(k == 1))
                        last.then_inc(s_m, 1)

                @block.scalar
                def _(e):
                    for g in range(NB // G):
                        e.wait_ge(s_t, g + 1)
                        wait(e, s_m, g)
                        nc.scalar.activation(AT[:, :, :, :].rearrange("p b k n -> p (b k n)"), psf[:, 0:2 * G * P], ACT.Copy).then_inc(s_a, 1)

                @block.vector
                def _(e):
                    for g in range(NB // G):
                        e.wait_ge(s_m, g + 1)
                        nc.vector.tensor_tensor(conv[:, g * G:(g + 1) * G, :], ps[:, 4 + g % 2, 0:G * C].rearrange("p (b c) -> p b c", c=C),
                                                vecs[:, 1, None, 0:C].to_broadcast([P, G, C]), ALU.add).then_inc(s_o, 1)

            with Phase() as ph:
                s_c, s_m, s_q = (ph.sem(n) for n in ("dve_step", "node_sums", "root"))
                block = ph.block()
                flat = work[:, 0:NB * C].rearrange("p (b c) -> p b c", c=C)
                part = small[:, 0:C]
                mean, var, rstd, shift = (small[:, 32 * k:32 * k + C] for k in range(1, 5))

                @block.vector
                def _(e):
                    v = nc.vector
                    ch = Chain(e, s_c)
                    mask = nodemask[:, :, None].to_broadcast([P, NB, C])
                    if l < L - 1:
                        ch.link(v.scalar_tensor_tensor(conv[:, :, :], conv[:, :, :], 0.01, conv[:, :, :], ALU.mult, ALU.max))
                    ch.link(v.tensor_tensor(feat[:, :, :], feat[:, :, :], conv[:, :, :], ALU.add))
                    ch.link(v.tensor_tensor(feat[:, :, :], feat[:, :, :], mask, ALU.mult))
                    ch.link(v.tensor_reduce(part, feat[:, :, :].rearrange("p b c -> p c b"), AX.X, ALU.add))
                    n1 = ch.n
                    e.wait_ge(s_m, 1)
                    ch.link(v.tensor_scalar(mean, ps[:, 0, 0:C], 1.0 / N, None, ALU.mult))
                    ch.link(v.tensor_tensor(feat[:, :, :], feat[:, :, :], mean[:, None, :].to_broadcast([P, NB, C]), ALU.subtract))
                    ch.link(v.tensor_tensor(flat, feat[:, :, :], mask, ALU.mult))
                    ch.link(v.tensor_tensor(flat, flat, flat, ALU.mult))
                    ch.link(v.tensor_reduce(part, flat.rearrange("p b c -> p c b"), AX.X, ALU.add))
                    e.wait_ge(s_m, 2)
                    ch.link(v.tensor_scalar(var, ps[:, 1, 0:C], 1.0 / N, EPS, ALU.mult, ALU.add))
                    e.wait_ge(s_q, 1)
                    ch.link(v.reciprocal(rstd, rstd))
                    ch.link(v.tensor_tensor(rstd, rstd, vecs[:, 2, 0:C], ALU.mult))
                    ch.link(v.tensor_tensor(feat[:, :, :], feat[:, :, :], rstd[:, None, :].to_broadcast([P, NB, C]), ALU.mult))
                    ch.link(v.tensor_tensor(feat[:, :, :], feat[:, :, :], vecs[:, 3, None, 0:C].to_broadcast([P, NB, C]), ALU.add))
                    if l == L - 1:
                        ch.link(v.tensor_tensor(xres[:, :, :], xres[:, :, :], feat[:, :, :], ALU.add))
                base = 4 if l < L - 1 else 3

                @block.tensor
                def _(e):
                    e.wait_ge(s_c, base)
                    nc.tensor.matmul(ps[:, 0, 0:C], ones[:, :], part, start=True, stop=True).then_inc(s_m, 1)
                    e.wait_ge(s_c, base + 5)
                    nc.tensor.matmul(ps[:, 1, 0:C], ones[:, :], part, start=True, stop=True).then_inc(s_m, 1)

                @block.scalar
                def _(e):
                    e.wait_ge(s_c, base + 6)
                    nc.scalar.activation(rstd, var, ACT.Sqrt).then_inc(s_q, 1)

        with Phase() as ph:
            s_o = ph.sem("out_written")
            block = ph.block()

            @block.sync
            def _(e):
                e.dma_start(out[0:(NB - 1) * P, :].rearrange("(b p) c -> p b c", p=P), xres[:, 0:NB - 1, :]).then_inc(s_o, 16)
                e.dma_start(out[(NB - 1) * P:N, :], xres[0:REAL, NB - 1, :]).then_inc(s_o, 16)
                e.wait_ge(s_o, 32)


NAMES = ("x", "src", "dst", "edge_attr_32", "edge_attr_4", "L0_gnn_W1", "L0_gnn_b1", "L0_gnn_W2", "L0_gnn_b2",
         "L0_gnn_si_w0", "L0_gnn_si_w1", "L1_gnn_Wl", "L1_gnn_bl", "L1_gnn_Wr", "L1_gnn_br", "L1_gnn_att",
         "L1_gnn_conv_bias", "L1_gnn_bn_gamma", "L1_gnn_bn_beta")


def kernel(**inputs):
    import numpy as np
    import concourse.bacc as bacc
    from concourse.bass_utils import run_bass_kernel_spmd as run

    nc = bacc.Bacc("TRN2", target_bir_lowering=False, num_devices=1)
    arrays, aps = {}, {}
    for name in NAMES:
        a = np.ascontiguousarray(inputs[name])
        arrays[name + "_in"] = a
        aps[name] = nc.dram_tensor(name + "_in", a.shape, mybir.dt.from_np(a.dtype), kind="ExternalInput").ap()
    out = nc.dram_tensor("out", (N, C), F32, kind="ExternalOutput").ap()
    build(nc, aps, out)
    return run(nc, [arrays], core_ids=[0]).results[0]["out"]
```

```python
import concourse.bass as bass
from concourse import mybir
from contextlib import ExitStack

F32 = mybir.dt.float32
BF16 = mybir.dt.bfloat16
I32 = mybir.dt.int32
ALU = mybir.AluOpType
ACT = mybir.ActivationFunctionType
AX = mybir.AxisListType

P = 128
N, E, C = 3125, 50000, 32
NB = 25
NP = NB * P
REAL = N - (NB - 1) * P
CH = 16
J = 25
T = CH * J
EP = T * P
CE = J * P
H, HC = 8, 256
VW = HC + 2 * H
MW = C + 2
ST = 4
NS = T // ST
ITEMS = NS + NB - 1
PAD_NODE = NP - 1
BIG = 1e30
EPS = 1e-5
EROW = 40
L = 3
MUL, MLP = 8, 64
ALPHA = 0.25
C110 = 3.0 ** -0.5
SI = 8.0 ** -0.5
GATHER = 16


class Chain:

    def __init__(self, eng, sem):
        self.eng, self.sem, self.n, self.base = eng, sem, 0, None

    def value(self):
        return self.n if self.base is None else self.base + self.n

    def mark(self, ins):
        ins.then_inc(self.sem, 1)
        self.n += 1
        return self.value()

    def link(self, ins):
        self.mark(ins)
        self.eng.wait_ge(self.sem, self.value())

    def enter(self, i, start, per):
        self.out, self.per = self.n, per
        self.base, self.n = i * per + (self.out - start * per), 0

    def leave(self, rounds):
        assert self.n == self.per, (self.n, self.per)
        self.n, self.base = self.out + self.per * rounds, None


def build(nc, A, out):
    ctx = ExitStack()
    with ctx, nc.allow_non_contiguous_dma(reason="small vectors and list transposes"):
        def sb(name, shape, dt=F32):
            return ctx.enter_context(nc.sbuf_tensor(name, shape, dt))

        def dram(name, shape, dt=F32):
            return nc.dram_tensor(name, shape, dt, kind="Internal").ap()

        dst_pad = dram("dst_pad", (EP + 2,), I32)
        src_pad = dram("src_pad", (EP,), I32)
        ea32_pad = dram("ea32_pad", (EP, C))
        ea4_pad = dram("ea4_pad", (EP, 4))
        edge_rows = dram("edge_rows", (EP, EROW))
        table = dram("table", (NP, C))
        first_rows = dram("first_rows", (EP + NP, C))
        same_d = dram("same_d", (CH, CE), BF16)
        ends_d = dram("ends_d", (P, 2))
        pens_d = dram("pens_d", (P, 2))
        carry_d = dram("carry_d", (H, 2, CH))
        walk_d = dram("walk_d", (2, P))

        ident = sb("ident", [P, P])
        ones = sb("ones", [P, P])
        iota_f = sb("iota_f", [P, P])
        iota_i = sb("iota_i", [P, P], I32)
        part_f = sb("part_f", [P, 1])
        nodemask = sb("nodemask", [P, NB])
        src_all = sb("src_all", [P, T + 2])
        dst_all = sb("dst_all", [P, T + 2])
        srcf, dstf = src_all[:, 0:T], dst_all[:, 0:T]
        lastf = sb("lastf", [P, T])
        start_pen = sb("start_pen", [P, CE], BF16)
        end_pen = sb("end_pen", [P, CE], BF16)
        pens = sb("pens", [H, 2, CH])
        walk_t = sb("walk_t", [1, P], I32)
        walk_b = sb("walk_b", [1, P], I32)
        base128 = sb("base128", [P, P])
        xres = sb("xres", [P, NB, C])
        feat = sb("feat", [P, NB, C])
        first_at = sb("first_at", [P, NB], I32)
        lself = sb("lself", [P, NB, H])
        count = sb("count", [P, NB])
        xsr = sb("xsr", [P, T, MW])
        pm = sb("pm", [P, T, 2 * H])
        ring = sb("ring", [P, 2, CH, 2 * C])
        gate = sb("gate", [P, 2])
        stage = sb("stage", [P, 2, 2 * CH], I32)
        work = sb("work", [P, 14000])
        logit = work[:, 8192:8192 + CE]
        SLOTS = 4
        slotV = work[:, 0:SLOTS * ST * VW].rearrange("p (s t w) -> p s t w", s=SLOTS, t=ST)
        slotO = work[:, SLOTS * ST * VW:SLOTS * ST * (VW + P)].rearrange("p (s t w) -> p s t w", s=SLOTS, t=ST)
        acc = work[:, 6400:6400 + NB * VW].rearrange("p (b w) -> p b w", b=NB)
        conv = work[:, 13200:13200 + NB * C].rearrange("p (b c) -> p b c", c=C)
        featT = work[0:C + 1, 0:NP]
        apart = sb("apart", [P, ITEMS, ST])
        small = sb("small", [P, 1024])
        wst = sb("wst", [P, HC])
        wl_aug = sb("wl_aug", [C + 1, HC])
        wr_aug = sb("wr_aug", [C + 1, HC])
        wz = sb("wz", [C + 1, HC])
        attb = sb("attb", [P, HC])
        attc = sb("attc", [P, 2])
        attp = sb("attp", [P, 2, P])
        bz = sb("bz", [P, 4])
        wlr = sb("wlr", [P, 2, C])
        vecs = sb("vecs", [P, 4, HC])
        w1_sb = sb("w1_sb", [P, 4, MLP])
        b1_sb = sb("b1_sb", [MLP, 1])
        w2_sb = sb("w2_sb", [MLP + 1, HC])
        siw = sb("siw", [C, C])
        ea4 = sb("ea4", [P, T, 4])
        unsorted = sb("unsorted", [1, 1], I32)

        ps = ctx.enter_context(nc.psum_tensor("ps", [P, 8, 512], F32))
        psf = ps[:, :, :].rearrange("p a b -> p (a b)")

        XT = work[:, 0:2048].rearrange("p (s q e) -> p s q e", s=2, e=P)
        RE = work[:, 2048:6144].rearrange("p (s h e) -> p s h e", s=4, h=2)
        SAME = work[:, 6144:7168].bitcast(BF16).rearrange("p (s q e) -> p s q e", s=2, e=P)
        EA = work[:, 0:1024].rearrange("p (s c k) -> p s c k", s=2, k=C)
        EAT = work[:, 1024:1024 + 2 * P].rearrange("p (s e) -> p s e", s=2)
        H1T = work[0:MLP + 1, 2048:3072].rearrange("p (s e) -> p s e", s=2)
        COEF = work[:, 3072:4608].rearrange("p (s c r i) -> p s c r i", s=2, c=CH, r=6)
        RED = work[:, 4608:5376].rearrange("p (c r o) -> p c r o", c=CH, r=6)
        TMP = work[:, 5376:5760].rearrange("p (c i m) -> p c i m", c=CH, m=3)
        XC = work[:, 5760:6784].rearrange("p (s c r) -> p s c r", s=2, r=C)
        PROD = work[:, 6784:9856].rearrange("p (s t r) -> p s t r", s=2, t=4)
        SCAN_F = work[:, 0:CE]
        SCAN_B = work[:, CE:2 * CE]

        names = [0]

        class Phase:

            def __enter__(self):
                self.ctx, self.sems = ExitStack(), []
                names[0] += 1
                return self

            def sem(self, name):
                self.sems.append(nc.alloc_semaphore(name=f"{name}_{names[0]}"))
                return self.sems[-1]

            def block(self):
                return self.ctx.enter_context(nc.Block())

            def __exit__(self, *a):
                self.ctx.close()
                nc.clear_and_free_semaphores(self.sems)
                nc.all_engine_barrier()

        def row_bcast(ap, parts=P):
            return ap.partition_broadcast(parts)

        s_attr = nc.alloc_semaphore(name="attributes_copied")
        with Phase() as ph:
            s_x, s_pads, s_pool, s_dma, s_c = (ph.sem(n) for n in ("x_in", "pads_set", "pool_step", "pad_copies", "dve_step"))
            block = ph.block()
            padi = small[0:1, 0:1024].bitcast(I32)
            minus, beyond = stage[0:1, 0, 0:1], stage[0:1, 0, 1:2]

            @block.gpsimd
            def _(e):
                ch = Chain(e, s_pool)
                ch.link(e.memset(ident[:, :], 0.0))
                ch.link(e.affine_select(out=ident[:, :], in_=ident[:, :], compare_op=ALU.not_equal, fill=1.0,
                                        base=0, pattern=[[-1, P]], channel_multiplier=1))
                ch.link(e.memset(nodemask[:, :], 1.0))
                ch.link(e.affine_select(out=nodemask[:, NB - 1:NB], in_=nodemask[:, NB - 1:NB], compare_op=ALU.is_gt,
                                        fill=0.0, base=REAL, pattern=[[0, 1]], channel_multiplier=-1))
                ch.link(e.iota(iota_i[:, :], pattern=[[1, P]], base=0, channel_multiplier=0))
                ch.link(e.tensor_copy(iota_f[:, :], iota_i[:, :]))
                ch.link(e.iota(iota_i[:, 0:1], pattern=[[0, 1]], base=0, channel_multiplier=1))
                ch.link(e.tensor_copy(part_f[:, :], iota_i[:, 0:1]))

            @block.vector
            def _(e):
                ch = Chain(e, s_c)
                v = nc.vector
                v.memset(padi, PAD_NODE).then_inc(s_pads, 1)
                v.memset(beyond, NP)
                v.memset(minus, -1).then_inc(s_pads, 1)
                v.memset(work[:, 0:C], 0.0).then_inc(s_pads, 1)
                v.memset(ones[:, :], 1.0)
                v.memset(src_all[:, T:], 0.0)
                v.memset(dst_all[:, T:], 0.0)
                v.memset(xsr[:, :, :], 0.0)
                v.memset(ring[:, :, :, :], 0.0)
                v.memset(gate[:, :], 0.0).then_inc(s_pads, 1)
                v.memset(SAME[:, :, :, :], 0.0)
                v.memset(w1_sb[:, :, :], 0.0)
                ch.link(v.memset(xres[:, :, :], 0.0))
                v.memset(siw[:, :], 0.0).then_inc(s_pads, 1)

            @block.sync
            def _(e):
                e.wait_ge(s_pads, 5)
                e.wait_ge(s_c, 1)
                n = 0
                pads = EP - E
                e.dma_start(dst_pad[EP + 1:EP + 2].rearrange("(a n) -> a n", a=1), beyond).then_inc(s_dma, 16)
                e.dma_start(dst_pad[0:1].rearrange("(a n) -> a n", a=1), minus).then_inc(s_dma, 16)
                e.dma_start(dst_pad[1:E + 1], A["dst"]).then_inc(s_dma, 16)
                e.dma_start(src_pad[0:E], A["src"]).then_inc(s_dma, 16)
                n = 4
                for o in range(0, pads, 1024):
                    w = min(1024, pads - o)
                    e.dma_start(dst_pad[1 + E + o:1 + E + o + w].rearrange("(a n) -> a n", a=1), padi[:, 0:w]).then_inc(s_dma, 16)
                    w = min(1024, EP - E - o)
                    e.dma_start(src_pad[E + o:E + o + w].rearrange("(a n) -> a n", a=1), padi[:, 0:w]).then_inc(s_dma, 16)
                    n += 2
                e.dma_start(xres[:, 0:NB - 1, :], A["x"][0:(NB - 1) * P, :].rearrange("(b p) c -> p b c", p=P)).then_inc(s_dma, 16)
                e.dma_start(xres[0:REAL, NB - 1, :], A["x"][(NB - 1) * P:N, :]).then_inc(s_dma, 16)
                for k in range(4):
                    e.dma_start(w1_sb[k * C:(k + 1) * C, k, :], A["L0_gnn_W1"]).then_inc(s_dma, 16)
                e.dma_start(b1_sb[:, :], A["L0_gnn_b1"].rearrange("(p a) -> p a", a=1)).then_inc(s_dma, 16)
                W2, b2 = A["L0_gnn_W2"], A["L0_gnn_b2"].rearrange("(a n) -> a n", a=1)
                for at, lo, hi in ((0, 0, 64), (64, 192, 256), (128, 64, 192)):
                    e.dma_start(w2_sb[0:MLP, at:at + hi - lo], W2[:, lo:hi]).then_inc(s_dma, 16)
                    e.dma_start(w2_sb[MLP:MLP + 1, at:at + hi - lo], b2[:, lo:hi]).then_inc(s_dma, 16)
                e.dma_start(siw[0:MUL, 0:MUL], A["L0_gnn_si_w0"]).then_inc(s_dma, 16)
                n += 2 + 4 + 1 + 6 + 1
                for m in range(3):
                    e.dma_start(siw[MUL + m:C:3, MUL + m:C:3], A["L0_gnn_si_w1"]).then_inc(s_dma, 16)
                    n += 1
                e.wait_ge(s_dma, 16 * n)

            @block.scalar
            def _(e):
                e.dma_start(ea32_pad[0:E, :], A["edge_attr_32"]).then_inc(s_attr, 16)
                e.dma_start(ea4_pad[0:E, :], A["edge_attr_4"]).then_inc(s_attr, 16)
                e.wait_ge(s_pads, 3)
                for o in range(E, EP, P):
                    w = min(P, EP - o)
                    e.dma_start(ea32_pad[o:o + w, :], work[0:w, 0:C]).then_inc(s_x, 16)
                    e.dma_start(ea4_pad[o:o + w, :], work[0:w, 0:4]).then_inc(s_x, 16)
                e.wait_ge(s_pads, 4)
                e.dma_start(first_rows[0:EP, :].rearrange("(p t) c -> p (t c)", p=P),
                            xsr[:, :, :].rearrange("p t k -> p (t k)")[:, 0:T * C]).then_inc(s_x, 16)
                e.wait_ge(s_x, 16 * 2 * -(-(EP - E) // P) + 16)

        with Phase() as ph:
            s_in, s_c, s_m = ph.sem("lists_in"), ph.sem("dve_step"), ph.sem("counted")
            block = ph.block()
            here, after = (work[:, k * T:(k + 1) * T].bitcast(I32) for k in range(2))

            @block.sync
            def _(e):
                for k, a in enumerate((here, after)):
                    e.dma_start(a, dst_pad[1 + k:1 + k + EP].rearrange("(p n) -> p n", n=T)).then_inc(s_in, 16)

            @block.vector
            def _(e):
                v = nc.vector
                ch = Chain(e, s_c)
                e.wait_ge(s_in, 32)
                ch.link(v.tensor_tensor(work[:, 2 * T:3 * T], here, after, ALU.is_gt))
                ch.link(v.tensor_reduce(small[:, 0:1], work[:, 2 * T:3 * T], AX.X, ALU.add))
                e.wait_ge(s_m, 1)
                ch.link(v.tensor_scalar(unsorted[:, :], ps[0:1, 0, 0:1], 0.0, None, ALU.is_gt))

            @block.tensor
            def _(e):
                e.wait_ge(s_c, 2)
                nc.tensor.matmul(ps[:, 0, 0:1], ones[:, :], small[:, 0:1], start=True, stop=True).then_inc(s_m, 1)

        with Phase() as ph:
            s_k, s_st, s_th, s_cc, s_cmp, s_row, s_idx, s_gate, s_put, s_back, s_set, s_i = (ph.sem(n) for n in (
                "chunk_in", "tile_dst_in", "threshold_step", "chunk_step", "compared", "row_in", "rank_staged", "gate_passed",
                "row_put", "list_back", "sort_set", "iotas"))
            s_kc = ph.sem("keys")
            block = ph.block()
            key_i = work[:, 0:CE].bitcast(I32)
            key, less, place = (work[:, k * CE:(k + 1) * CE] for k in (0, 1, 2))
            pmf = pm[:, :, :].rearrange("p t k -> p (t k)")
            d4, inner, chunk_of, thr, t1, cnt, rank, dcol = (pmf[:, k * T:(k + 1) * T] for k in range(8))
            row = small[:, 0:EROW]
            rank_i = small[:, 64:65].bitcast(I32)
            chunk_at = small[:, 66:67]
            KEY = 4096.0

            @block.gpsimd
            def _(e):
                flag = e.value_load(unsorted[0:1, 0:1], min_val=0, max_val=1)
                with e.If(flag > 0):
                    e.iota(work[:, CE:CE + T].bitcast(I32), pattern=[[0, CH], [P, J]], base=0, channel_multiplier=1).then_inc(s_i, 1)
                    e.iota(work[:, CE + T:CE + 2 * T].bitcast(I32), pattern=[[1, CH], [0, J]], base=0, channel_multiplier=0).then_inc(s_i, 1)
                    e.iota(place.bitcast(I32), pattern=[[1, CE]], base=0, channel_multiplier=0).then_inc(s_i, 1)
                    with e.Fori(0, T) as t:
                        e.wait_ge(s_idx, t + 1)
                        e.tensor_tensor(gate[:, 0:1], ones[:, 0:1], ones[:, 0:1], ALU.add).then_inc(s_gate, 1)
                        e.indirect_dma_start(out=edge_rows[:, :], out_offset=bass.IndirectOffsetOnAxis(ap=rank_i, axis=0),
                                             in_=row, in_offset=None).then_inc(s_put, 16)

            @block.vector
            def _(e):
                v = nc.vector
                flag = e.value_load(unsorted[0:1, 0:1], min_val=0, max_val=1)
                with e.If(flag > 0):
                    ch = Chain(e, s_th)
                    e.wait_ge(s_i, 3)
                    ch.link(v.tensor_copy(inner, work[:, CE:CE + T].bitcast(I32)))
                    ch.link(v.tensor_copy(chunk_of, work[:, CE + T:CE + 2 * T].bitcast(I32)))
                    ch.link(v.tensor_copy(place, place.bitcast(I32)))
                    ch.link(v.memset(rank, 0.0))
                    ch.link(v.memset(row, 0.0))
                    ch.link(v.memset(chunk_at, 0.0))
                    e.wait_ge(s_st, 16)
                    ch.link(v.tensor_scalar(d4, dcol.bitcast(I32), KEY, None, ALU.mult))
                    with e.Fori(0, CH) as c:
                        ch.enter(c, 0, 9)
                        e.wait_ge(s_k, 16 * c + 16)
                        ch.link(v.tensor_scalar(key, key_i, KEY, None, ALU.mult))
                        ch.link(v.tensor_tensor(key, key, place, ALU.add))
                        ch.link(v.tensor_scalar(t1, chunk_of, chunk_at, KEY - 1, ALU.is_gt, ALU.mult))
                        ch.link(v.tensor_tensor(thr, d4, t1, ALU.add))
                        ch.link(v.scalar_tensor_tensor(t1, chunk_of, chunk_at, inner, ALU.is_equal, ALU.mult))
                        ch.link(v.tensor_tensor(thr, thr, t1, ALU.add))
                        ch.mark(v.memset(small[:, 67:68], 0.0))
                        with e.Fori(0, T) as t:
                            v.tensor_scalar(less, key, thr[:, bass.ds(t, 1)], None, ALU.is_lt).then_inc(s_cmp, 1)
                            e.wait_ge(s_cmp, c * (2 * T) + 2 * t + 1)
                            v.tensor_reduce(cnt[:, bass.ds(t, 1)], less, AX.X, ALU.add).then_inc(s_cmp, 1)
                            e.wait_ge(s_cmp, c * (2 * T) + 2 * t + 2)
                        ch.link(v.tensor_tensor(rank, rank, cnt, ALU.add))
                        ch.link(v.tensor_scalar(chunk_at, chunk_at, 1.0, None, ALU.add))
                        ch.leave(CH)
                    e.wait_ge(s_row, 64)
                    v.tensor_copy(rank_i, rank[:, 0:1]).then_inc(s_idx, 1)
                    with e.Fori(1, T) as t:
                        e.wait_ge(s_gate, t)
                        e.wait_ge(s_row, 64 * t + 64)
                        v.tensor_copy(rank_i, rank[:, bass.ds(t, 1)]).then_inc(s_idx, 1)

            @block.sync
            def _(e):
                flag = e.value_load(unsorted[0:1, 0:1], min_val=0, max_val=1)
                with e.If(flag > 0):
                    e.wait_ge(s_attr, 32)
                    e.dma_start(dcol.bitcast(I32), dst_pad[1:EP + 1].rearrange("(t p) -> p t", p=P)).then_inc(s_st, 16)
                    e.wait_ge(s_st, 16)
                    chunks = dst_pad[1:EP + 1].rearrange("(c n) -> c n", n=CE)
                    with e.Fori(0, CH) as c:
                        e.wait_ge(s_th, c * 9 + 7)
                        e.dma_start(key_i, chunks[bass.ds(c, 1), :].rearrange("a n -> (a n)").partition_broadcast(P)).then_inc(s_k, 16)
                    tiles = dst_pad[1:EP + 1].rearrange("(t p a) -> t p a", p=P, a=1)
                    srcs = src_pad.rearrange("(t p a) -> t p a", p=P, a=1)
                    e.wait_ge(s_th, 7 + 9 * CH)
                    attr4, attr32 = ea4_pad.rearrange("(t p) k -> t p k", p=P), ea32_pad.rearrange("(t p) k -> t p k", p=P)

                    def load_row(t):
                        for lo, hi, a in ((0, 1, tiles), (1, 2, srcs), (2, 6, attr4), (6, 6 + C, attr32)):
                            to = row[:, lo:hi].bitcast(I32) if hi <= 2 else row[:, lo:hi]
                            at = bass.ds(t, 1) if not isinstance(t, int) else slice(t, t + 1)
                            e.dma_start(to, a[at].rearrange("t p a -> (t p) a")).then_inc(s_row, 16)
                    load_row(0)
                    with e.Fori(1, T) as t:
                        e.wait_ge(s_put, 16 * t)
                        load_row(t)
                    e.wait_ge(s_put, 16 * T)
                    rows_i = edge_rows.bitcast(I32)
                    n = 0
                    for o in range(0, EP, CE):
                        e.dma_start(dst_pad[1 + o:1 + o + CE].rearrange("(n a) -> n a", a=1), rows_i[o:o + CE, 0:1]).then_inc(s_back, 16)
                        e.dma_start(src_pad[o:o + CE].rearrange("(n a) -> n a", a=1), rows_i[o:o + CE, 1:2]).then_inc(s_back, 16)
                        e.dma_start(ea4_pad[o:o + CE, :], edge_rows[o:o + CE, 2:6]).then_inc(s_back, 16)
                        e.dma_start(ea32_pad[o:o + CE, :], edge_rows[o:o + CE, 6:6 + C]).then_inc(s_back, 16)
                        n += 4
                    e.wait_ge(s_back, 16 * n)

        TR = T // 4
        slotless = work[:, 7624:8024]
        with Phase() as ph:
            s_in, s_t, s_c, s_w, s_rep = (ph.sem(n) for n in ("lists_in", "lists_turned", "dve_step", "walk_out", "dst_in"))
            s_conv, s_same, s_same_out, s_e, s_ea4 = (ph.sem(n) for n in ("lists_float", "same_set", "same_out", "places", "attr4_in"))
            same = xsr[:, 0:CE // MW + 1, :].rearrange("p a b -> p (a b)")[:, 0:CE // 2].bitcast(BF16)
            block = ph.block()
            rows = [logit[0:TR, k * 512:(k + 1) * 512] for k in range(3)] + [work[0:TR, 6600:7112]]
            rowsf = [logit[0:TR, (3 + k) * 512:(4 + k) * 512] for k in range(3)] + [work[0:TR, 7112:7624]]
            before = small[:, 404:404 + T]
            rep = work[:, 0:CE + 2].bitcast(I32)
            repf = work[:, CE + 2:2 * CE + 4]
            lastd = slotless[:, 0:NS].bitcast(I32)
            key = slotless[:, 128:128 + NS]
            cmpk = slotless[:, 256:256 + NS]
            tk = slotless[:, 384:388]

            @block.sync
            def _(e):
                for k, a in enumerate((src_pad[0:EP], dst_pad[1:EP + 1], dst_pad[2:EP + 2], dst_pad[0:EP])):
                    e.dma_start(rows[k].bitcast(I32), a.rearrange("(p n) -> p n", n=512)).then_inc(s_in, 16)
                e.dma_start(lastd, row_bcast(dst_pad[1:EP + 1].rearrange("(s n) -> s n", n=ST * P)[:, ST * P - 1]),).then_inc(s_in, 16)
                for c in range(CH):
                    e.dma_start(rep[c * H:(c + 1) * H, :], row_bcast(dst_pad[c * CE:(c + 1) * CE + 2], H)).then_inc(s_rep, 16)
                e.wait_ge(s_attr, 32)
                e.dma_start(ea4[:, :, :], ea4_pad.rearrange("(t p) k -> p t k", p=P)).then_inc(s_ea4, 16)
                e.wait_ge(s_w, 1)
                e.dma_start(walk_d.rearrange("a p -> p a"), tk[:, 0:2]).then_inc(s_w, 16)
                e.dma_start(pens_d, small[:, 400:402]).then_inc(s_w, 16)
                e.wait_ge(s_w, 33)
                e.dma_start(pm[0:1, 0:8, :].rearrange("p a b -> p (a b)"), walk_d[0:1, :]).then_inc(s_w, 16)
                e.dma_start(pm[0:1, 8:16, :].rearrange("p a b -> p (a b)"), walk_d[1:2, :]).then_inc(s_w, 16)
                e.dma_start(base128[:, :], row_bcast(walk_d[1, :])).then_inc(s_w, 16)
                for k in range(2):
                    e.dma_start(pens[:, k, :], pens_d[:, k].rearrange("(c h) -> h c", h=H)).then_inc(s_w, 16)
                e.wait_ge(s_w, 33 + 80)
                e.wait_ge(s_ea4, 16)

            place_i = pm[:, 100:100 + T // (2 * H), :].rearrange("p a b -> p (a b)").bitcast(I32)
            place = pm[:, 200:200 + T // (2 * H), :].rearrange("p a b -> p (a b)")

            @block.gpsimd
            def _(e):
                e.iota(place_i, pattern=[[P, T]], base=0, channel_multiplier=1).then_inc(s_e, 1)

            @block.scalar
            def _(e):
                e.wait_ge(s_same, 1)
                e.dma_start(same_d, same[0:P:H, :]).then_inc(s_same_out, 16)

            @block.vector
            def _(e):
                v = nc.vector
                ch = Chain(e, s_c)
                e.wait_ge(s_in, 80)
                for k in range(4):
                    ch.link(v.tensor_copy(rowsf[k], rows[k].bitcast(I32)))
                v.memset(small[:, 1000:1001], 0.0).then_inc(s_conv, 1)
                ch.link(v.tensor_scalar(lastd, lastd, 7, None, ALU.arith_shift_right))
                ch.link(v.tensor_copy(key, lastd))
                ch.link(v.tensor_tensor(key, key, iota_f[:, 0:NS], ALU.add))
                ch.link(v.tensor_scalar(cmpk, key, part_f[:, 0:1], None, ALU.is_lt))
                ch.link(v.tensor_reduce(tk[:, 2:3], cmpk, AX.X, ALU.add))
                ch.link(v.tensor_scalar(tk[:, 0:1], tk[:, 2:3], float(ST), None, ALU.mult))
                ch.link(v.tensor_tensor(tk[:, 1:2], part_f[:, 0:1], tk[:, 2:3], ALU.subtract))
                e.wait_ge(s_rep, 16 * CH)
                ch.link(v.tensor_copy(repf, rep))
                ch.link(v.tensor_tensor(same[:, :], repf[:, 1:CE + 1], repf[:, 0:CE], ALU.is_equal))
                v.memset(small[:, 1003:1004], 0.0).then_inc(s_same, 1)
                ch.link(v.tensor_tensor(work[:, 0:CE], repf[:, 1:CE + 1], repf[:, 0:CE], ALU.not_equal))
                ch.link(v.tensor_scalar(start_pen[:, :], work[:, 0:CE], -BIG, None, ALU.mult))
                ch.link(v.tensor_tensor(work[:, 0:CE], repf[:, 1:CE + 1], repf[:, 2:CE + 2], ALU.not_equal))
                ch.link(v.tensor_scalar(end_pen[:, :], work[:, 0:CE], -BIG, None, ALU.mult))
                ch.link(v.tensor_reduce(small[:, 400:401], start_pen[:, :], AX.X, ALU.min))
                ch.link(v.tensor_reduce(small[:, 401:402], end_pen[:, :], AX.X, ALU.min))
                v.memset(small[:, 1001:1002], 0.0).then_inc(s_w, 1)
                e.wait_ge(s_t, 4)
                for k, o in enumerate((srcf, dstf, lastf, before)):
                    ch.link(v.tensor_copy(o[:, :].rearrange("p (a b) -> p b a", b=4),
                                          psf[:, k * 512:k * 512 + 4 * TR].rearrange("p (b a) -> p b a", b=4)))
                ch.link(v.tensor_tensor(lastf[:, :], lastf[:, :], dstf[:, :], ALU.not_equal))
                e.wait_ge(s_same_out, 16)
                e.wait_ge(s_e, 1)
                ch.link(v.tensor_copy(xsr[:, :, C], lastf[:, :]))
                ch.link(v.tensor_tensor(before, before, dstf[:, :], ALU.not_equal))
                ch.link(v.tensor_copy(place, place_i))
                ch.link(v.tensor_tensor(xsr[:, :, C + 1], before, place, ALU.mult))
                e.wait_ge(s_w, 33 + 80)
                ch.link(v.tensor_copy(walk_t[:, :], pm[0:1, 0:8, :].rearrange("p a b -> p (a b)")))
                ch.link(v.tensor_copy(walk_b[:, :], pm[0:1, 8:16, :].rearrange("p a b -> p (a b)")))
                ch.link(v.tensor_scalar(base128[:, :], base128[:, :], float(P), None, ALU.mult))

            @block.tensor
            def _(e):
                e.wait_ge(s_conv, 1)
                for k in range(4):
                    for b in range(4):
                        last = nc.tensor.transpose(psf[:, k * 512 + b * TR:k * 512 + (b + 1) * TR],
                                                   rowsf[k][:, b * P:(b + 1) * P], ident[0:TR, 0:TR])
                    last.then_inc(s_t, 1)

        def layer_norm_relu(src, dst):
            with Phase() as ph:
                s_c, s_q = ph.sem("dve_step"), ph.sem("root")
                block = ph.block()
                mu, var = small[:, 0:NB], small[:, 32:32 + NB]
                sq = work[:, 0:NB * C].rearrange("p (b c) -> p b c", c=C)

                @block.vector
                def _(e):
                    v = nc.vector
                    ch = Chain(e, s_c)
                    ch.link(v.tensor_reduce(mu, src[:, :, :], AX.X, ALU.add))
                    ch.link(v.tensor_scalar(mu, mu, 1.0 / C, None, ALU.mult))
                    ch.link(v.tensor_tensor(dst[:, :, :], src[:, :, :], mu[:, :, None].to_broadcast([P, NB, C]), ALU.subtract))
                    ch.link(v.tensor_tensor(sq, dst[:, :, :], dst[:, :, :], ALU.mult))
                    ch.link(v.tensor_reduce(var, sq, AX.X, ALU.add))
                    ch.link(v.tensor_scalar(var, var, 1.0 / C, EPS, ALU.mult, ALU.add))
                    n = ch.n
                    e.wait_ge(s_q, 1)
                    ch.link(v.reciprocal(mu, var))
                    ch.link(v.tensor_tensor(dst[:, :, :], dst[:, :, :], mu[:, :, None].to_broadcast([P, NB, C]), ALU.mult))
                    ch.link(v.tensor_scalar(dst[:, :, :], dst[:, :, :], 0.0, None, ALU.max))

                @block.scalar
                def _(e):
                    e.wait_ge(s_c, 6)
                    nc.scalar.activation(var, var, ACT.Sqrt).then_inc(s_q, 1)

        def turn_features():
            with Phase() as ph:
                s_t = ph.sem("turned")
                s_e = ph.sem("copied")
                block = ph.block()
                groups = [(g, min(4, NB - g)) for g in range(0, NB, 4)]

                @block.vector
                def _(e):
                    nc.vector.memset(featT[C:C + 1, :], 1.0)

                @block.tensor
                def _(e):
                    for g, w in groups:
                        for b in range(w):
                            last = nc.tensor.transpose(ps[0:C, g // 4, b * P:(b + 1) * P], feat[:, g + b, :], ident[:, :])
                        last.then_inc(s_t, 1)

                @block.scalar
                def _(e):
                    for g, w in groups:
                        e.wait_ge(s_t, g // 4 + 1)
                        nc.scalar.activation(featT[0:C, g * P:(g + w) * P], ps[0:C, g // 4, 0:w * P], ACT.Copy).then_inc(s_e, 1)

        def write_table():
            with Phase() as ph:
                s_o = ph.sem("table_out")
                block = ph.block()

                @block.sync
                def _(e):
                    e.dma_start(table.rearrange("(b p) c -> p b c", p=P), feat[:, :, :]).then_inc(s_o, 16)
                    e.wait_ge(s_o, 16)

        def by_chunk(a):
            return a.rearrange("p (c j) -> p j c", j=J)

        src_jc, dst_jc = by_chunk(srcf[:, :]), by_chunk(dstf[:, :])
        src_next, dst_next = by_chunk(src_all[:, 2:T + 2]), by_chunk(dst_all[:, 2:T + 2])

        def ring_place(c):
            return 4 * (c % 4) + c // 4

        def gather_program(e, s_ready, s_gath, s_gate, s_dst=None):

            def rows(par, at, part, sem):
                for c in range(CH):
                    e.indirect_dma_start(
                        out=ring[:, par, ring_place(c), part * C:(part + 1) * C], out_offset=None, in_=table[:, :],
                        in_offset=bass.IndirectOffsetOnAxis(ap=at[:, c:c + 1], axis=0)).then_inc(sem, GATHER)

            def window(par, need):
                e.wait_ge(s_ready[par], need)
                e.tensor_tensor(gate[:, par:par + 1], ones[:, 0:1], ones[:, 0:1], ALU.add).then_inc(s_gate, 1)
                rows(par, stage[:, par, 0:CH], 0, s_gath[par])
            window(0, 1)
            if s_dst is not None:
                rows(0, stage[:, 0, CH:], 1, s_dst)
            window(1, 1)
            with e.Fori(1, J // 2) as i:
                window(0, i + 1)
                window(1, i + 1)
            window(0, J // 2 + 1)

        def pairs(e, body, chains=()):
            body(0, 0, 0)
            body(1, 1, 0)
            with e.Fori(1, J // 2) as i:
                for ch, per in chains:
                    ch.enter(i, 1, per)
                body(2 * i, 0, i)
                body(2 * i + 1, 1, i)
                for ch, per in chains:
                    ch.leave(J // 2 - 1)
            body(J - 1, 0, J // 2)

        def first(x):
            return isinstance(x, int)

        def wait(e, sem, x):
            if not (isinstance(x, int) and x <= 0):
                e.wait_ge(sem, x)

        layer_norm_relu(xres, feat)
        with Phase() as ph:
            s_c = ph.sem("dve_step")
            block = ph.block()

            @block.vector
            def _(e):
                ch = Chain(e, s_c)
                ch.mark(nc.vector.memset(H1T[:, :, :], 1.0))
                ch.link(nc.vector.tensor_scalar(w2_sb[:, :], w2_sb[:, :], ALPHA, None, ALU.mult))
                ch.link(nc.vector.tensor_scalar(w2_sb[:, 64:128], w2_sb[:, 64:128], C110, None, ALU.mult))
                for par in range(2):
                    nc.vector.tensor_copy(stage[:, par, 0:CH], src_jc[:, par, :])
        write_table()

        GW = CH * GATHER
        with Phase() as ph:
            s_ready = [ph.sem("staged0"), ph.sem("staged1")]
            s_gath = [ph.sem("gathered0"), ph.sem("gathered1")]
            s_gate = ph.sem("gate_passed")
            s_ea = [ph.sem("attr0"), ph.sem("attr1")]
            s_t, s_tc, s_h, s_hr, s_w, s_pr, s_c, s_red, s_xc, s_cf = (ph.sem(n) for n in (
                "attr_turned", "attr_copied", "hidden", "hidden_relu", "weights", "products", "dve_step", "reduced",
                "rows_copied", "coefficients"))
            block = ph.block()

            @block.gpsimd
            def _(e):
                gather_program(e, s_ready, s_gath, s_gate)

            @block.sync
            def _(e):
                ea_v = ea32_pad.rearrange("(c j p) k -> j p c k", c=CH, p=P)

                def window(j, par, i):
                    wait(e, s_t, 4 * j - 4 if not first(j) or j >= 2 else 0)
                    e.dma_start(EA[:, par, :, :], ea32_rows(j)).then_inc(s_ea[par], 16)

                def ea32_rows(j):
                    if first(j):
                        return ea_v[j]
                    return ea_v[bass.ds(j, 1)].rearrange("a p c k -> (a p) c k")
                pairs(e, window)

            @block.tensor
            def _(e):
                def turn(j, par, i, g):
                    if g == 0:
                        e.wait_ge(s_ea[par], 16 * i + 16)
                    wait(e, s_tc, 4 * j + g - 1)
                    nc.tensor.transpose(ps[:, g % 2, 0:P], EA[:, par, 4 * g:4 * g + 4, :].rearrange("p c k -> p (c k)"),
                                        ident[:, :]).then_inc(s_t, 1)

                def hidden(j, g):
                    e.wait_ge(s_tc, 4 * j + g + 1)
                    wait(e, s_hr, 4 * j + g - 1)
                    for k in range(4):
                        last = nc.tensor.matmul(ps[0:MLP, 2 + g % 2, k * P:(k + 1) * P], w1_sb[:, k, :],
                                                EAT[:, g % 2, :], start=True, stop=True)
                    last.then_inc(s_h, 1)

                def weights(j, g):
                    e.wait_ge(s_hr, 4 * j + g + 1)
                    wait(e, s_pr, 4 * j + g - 1)
                    for k in range(4):
                        last = nc.tensor.matmul(ps[:, 4 + 2 * (g % 2) + k // 2, (k % 2) * HC:(k % 2 + 1) * HC],
                                                H1T[:, g % 2, k * P:(k + 1) * P], w2_sb[:, :], start=True, stop=True)
                    last.then_inc(s_w, 1)

                def window(j, par, i):
                    for g in range(4):
                        last = first(j) and j == J - 1
                        if g < 2:
                            turn(j, par, i, g + 2)
                        elif not last:
                            turn(j + 1, 1 - par, i + par, g - 2)
                        if g < 3:
                            hidden(j, g + 1)
                        elif not last:
                            hidden(j + 1, 0)
                        weights(j, g)
                turn(0, 0, 0, 0)
                turn(0, 0, 0, 1)
                hidden(0, 0)
                pairs(e, window)

            @block.scalar
            def _(e):
                def window(j, par, i):
                    for g in range(4):
                        e.wait_ge(s_t, 4 * j + g + 1)
                        wait(e, s_h, 4 * j + g - 1)
                        nc.scalar.activation(EAT[:, g % 2, :], ps[:, g % 2, 0:P], ACT.Copy).then_inc(s_tc, 1)
                        e.wait_ge(s_h, 4 * j + g + 1)
                        wait(e, s_w, 4 * j + g - 1)
                        nc.scalar.activation(H1T[0:MLP, g % 2, :], ps[0:MLP, 2 + g % 2, :], ACT.Relu,
                                             bias=b1_sb[:, :]).then_inc(s_hr, 1)
                        if g == 1:
                            e.wait_ge(s_gath[par], GW * i + GW)
                            wait(e, s_cf, j - 1)
                            wait(e, s_pr, 4 * j - 4)
                            for q in range(4):
                                nc.scalar.activation(XC[:, par, 4 * q:4 * q + 4, :], ring[:, par, q:CH:4, 0:C], ACT.Copy).then_inc(s_xc, 1)
                            e.wait_ge(s_xc, 5 * j + 4)
                            nc.scalar.activation(COEF[:, par, :, 2, :], XC[:, par, :, 0:MUL], ACT.Copy).then_inc(s_xc, 1)
                pairs(e, window)

            @block.vector
            def _(e):
                v = nc.vector
                ch = Chain(e, s_c)
                v.memset(small[:, 0:1], 0.0).then_inc(s_ready[0], 1)
                v.memset(small[:, 1:2], 0.0).then_inc(s_ready[1], 1)

                def window(j, par, i):
                    at = bass.ds(j, 1) if not first(j) else slice(j, j + 1)
                    sh = ea4[:, :, :].rearrange("p (c j) k -> p j c k", j=J)[:, at, :, :].rearrange("p a c k -> p (a c) k")
                    sh1 = sh[:, :, None, 1:4].to_broadcast([P, CH, MUL, 3])
                    cf = COEF[:, par, :, :, :]
                    e.wait_ge(s_xc, 5 * j + 5)
                    xv = XC[:, par, :, MUL:C].rearrange("p c (i m) -> p c i m", m=3)
                    ch.mark(v.tensor_tensor(cf[:, :, 0, :], XC[:, par, :, 0:MUL], sh[:, :, 0:1].to_broadcast([P, CH, MUL]), ALU.mult))
                    ch.link(v.tensor_tensor(cf[:, :, 3:6, :], xv.rearrange("p c i m -> p c m i"),
                                            sh[:, :, 0:1, None].to_broadcast([P, CH, 3, MUL]), ALU.mult))
                    ch.link(v.tensor_tensor(TMP[:, :, :, :], xv, sh1, ALU.mult))
                    ch.link(v.tensor_reduce(cf[:, :, 1, :], TMP[:, :, :, :], AX.X, ALU.add))
                    if not (first(j) and j + 2 >= J):
                        e.wait_ge(s_gate, j + 1)
                        v.tensor_copy(stage[:, par, 0:CH], src_next[:, at, :].rearrange("p a c -> p (a c)")).then_inc(s_ready[par], 1)
                    for g in range(4):
                        e.wait_ge(s_w, 4 * j + g + 1)
                        W = ps[:, 4 + 2 * (g % 2):6 + 2 * (g % 2), :].rearrange("p a (t r) -> p (a t) r", t=2)
                        pr = PROD[:, g % 2, :, :]
                        c4 = cf[:, 4 * g:4 * g + 4, :, :].rearrange("p t r i -> p t (r i)")
                        first_three = v.tensor_tensor(pr[:, :, 0:192].rearrange("p t (k o) -> p t k o", o=MUL),
                                                      W[:, :, 0:192].rearrange("p t (k o) -> p t k o", o=MUL),
                                                      c4[:, :, 0:24, None].to_broadcast([P, 4, 24, MUL]), ALU.mult)
                        if g == 0:
                            first_three.then_inc(s_cf, 1)
                        for m in range(3):
                            last = v.tensor_tensor(pr[:, :, 192 + 64 * m:256 + 64 * m].rearrange("p t (k o) -> p t k o", o=MUL),
                                                   W[:, :, 192:256].rearrange("p t (k o) -> p t k o", o=MUL),
                                                   c4[:, :, 24 + 8 * m:32 + 8 * m, None].to_broadcast([P, 4, MUL, MUL]), ALU.mult)
                        last.then_inc(s_pr, 1)
                        e.wait_ge(s_pr, 4 * j + g + 1)
                        v.tensor_reduce(RED[:, 4 * g:4 * g + 4, :, :].rearrange("p t r o -> p (t r) o"),
                                        pr.rearrange("p t (r i o) -> p (t r) o i", i=MUL, o=MUL), AX.X, ALU.add).then_inc(s_red, 1)
                    e.wait_ge(s_red, 4 * j + 4)
                    msg = xsr[:, :, :].rearrange("p (c j) k -> p j c k", j=J)[:, at, :, :].rearrange("p a c k -> p (a c) k")
                    ch.mark(v.tensor_tensor(msg[:, :, 0:MUL], RED[:, :, 0, :], RED[:, :, 1, :], ALU.add))
                    ch.link(v.tensor_tensor(TMP[:, :, :, :], RED[:, :, 2, :, None].to_broadcast([P, CH, MUL, 3]), sh1, ALU.mult))
                    ch.mark(v.tensor_tensor(msg[:, :, MUL:C].rearrange("p c (o m) -> p c o m", m=3), TMP[:, :, :, :],
                                            RED[:, :, 3:6, :].rearrange("p c m o -> p c o m"), ALU.add))

                pairs(e, window, [(ch, 2 * 7)])

        def walk(table, k, n, most):
            at = slice(k, k + n) if first(k) else bass.ds(k, n)
            return list(nc.values_load_multi_w_load_instructions(
                table[0:1, at], engines=(mybir.EngineType.DVE,), min_val=0, max_val=most,
                skip_runtime_bounds_check_because="the walk is made on the chip and ends at the last tile and block")[1])

        def segment_sums(width, edge_values, on_dve=0):
            with Phase() as ph:
                s_v, s_o, s_mm, s_acc, s_ap = (ph.sem(n) for n in ("values", "selected", "sums", "added", "apart"))
                block = ph.block()
                on_act = ST - on_dve

                @block.vector
                def _(e):
                    v = nc.vector
                    v.memset(acc[:, :, :], 0.0).then_inc(s_acc, 1)

                    def make(k, slot, t4):
                        if on_dve:
                            item = slice(k, k + 1) if first(k) else bass.ds(k, 1)
                            v.tensor_tensor(apart[:, item, :].rearrange("p a t -> p (a t)"), base128[:, item].to_broadcast([P, ST]),
                                            dstf[:, bass.ds(t4, ST)], ALU.subtract).then_inc(s_ap, 1)
                        wait(e, s_mm, k - SLOTS + 1)
                        if on_dve:
                            e.wait_ge(s_ap, k + 1)
                            for t in range(on_act, ST):
                                v.tensor_scalar(slotO[:, slot, t, :], iota_f[:, :], apart[:, item, t:t + 1].rearrange("p a t -> p (a t)"),
                                                0.0, ALU.add, ALU.is_equal)
                        edge_values(v, slot, t4).then_inc(s_v, 1)

                    def add(k, slot, b):
                        e.wait_ge(s_mm, k + 1)
                        e.wait_ge(s_acc, k + 1)
                        row = acc[:, bass.ds(b, 1), 0:width].rearrange("p a w -> p (a w)")
                        v.tensor_tensor(row, row, ps[:, slot, 0:width], ALU.add).then_inc(s_acc, 1)

                    def round_of(k, before):
                        t4 = walk(walk_t, k, 4, T - ST)
                        b = walk(walk_b, k - 2, 4, NB - 1) if before else [None, None] + walk(walk_b, k, 2, NB - 1)
                        for u in range(4):
                            make(k + u, u, t4[u])
                            if b[u] is not None:
                                add(k + u - 2, (u - 2) % 4, b[u])
                    round_of(0, False)
                    with e.Fori(1, ITEMS // 4) as i:
                        round_of(4 * i, True)
                    for u, b in enumerate(walk(walk_b, ITEMS - 2, 2, NB - 1)):
                        add(ITEMS - 2 + u, 2 + u, b)

                @block.scalar
                def _(e):
                    def select(k, slot):
                        wait(e, s_mm, k - SLOTS + 1)
                        item = slice(k, k + 1) if first(k) else bass.ds(k, 1)
                        if on_dve:
                            e.wait_ge(s_ap, k + 1)
                        for t in range(on_act):
                            nc.scalar.activation(slotO[:, slot, t, :], iota_f[:, :], ACT.Abs,
                                                 bias=apart[:, item, t:t + 1].rearrange("p a t -> p (a t)")).then_inc(s_o, 1)
                        e.wait_ge(s_o, k * (on_act + 1) + on_act)
                        nc.scalar.activation(slotO[:, slot, 0:on_act, :], slotO[:, slot, 0:on_act, :], ACT.Relu, scale=-1.0, bias=1.0).then_inc(s_o, 1)
                    for k in range(4):
                        select(k, k)
                    with e.Fori(1, ITEMS // 4) as i:
                        for u in range(4):
                            select(4 * i + u, u)

                @block.tensor
                def _(e):
                    def item(k, slot):
                        e.wait_ge(s_v, k + 1)
                        e.wait_ge(s_o, (k + 1) * (on_act + 1))
                        wait(e, s_acc, k - SLOTS + 2 if not (first(k) and k < SLOTS) else 0)
                        for t in range(ST):
                            last = nc.tensor.matmul(ps[:, slot, 0:width], slotO[:, slot, t, :], slotV[:, slot, t, 0:width],
                                                    start=(t == 0), stop=(t == ST - 1))
                        last.then_inc(s_mm, 1)
                    for k in range(4):
                        item(k, k)
                    with e.Fori(1, ITEMS // 4) as i:
                        for u in range(4):
                            item(4 * i + u, u)

        def message_values(v, slot, t4):
            return v.tensor_copy(slotV[:, slot, :, 0:MW], xsr[:, bass.ds(t4, ST), :])

        segment_sums(MW, message_values, on_dve=2)
        turn_features()

        with Phase() as ph:
            s_m, s_c = ph.sem("self"), ph.sem("dve_step")
            s_w = ph.sem("scaled")
            s_i = ph.sem("own_rows")
            block = ph.block()

            @block.gpsimd
            def _(e):
                e.iota(small[:, 64:64 + NB].bitcast(I32), pattern=[[P, NB]], base=EP, channel_multiplier=1).then_inc(s_i, 1)

            @block.vector
            def _(e):
                v = nc.vector
                ch = Chain(e, s_c)
                e.wait_ge(s_i, 1)
                v.tensor_scalar(siw[:, :], siw[:, :], SI, None, ALU.mult).then_inc(s_w, 1)
                ch.link(v.tensor_copy(count[:, :], acc[:, :, C]))
                ch.link(v.tensor_scalar(small[:, 0:NB], count[:, :], -1.0, -1.0, ALU.add, ALU.mult))
                ch.link(v.tensor_copy(small[:, 32:32 + NB], small[:, 64:64 + NB].bitcast(I32)))
                ch.link(v.tensor_tensor(small[:, 0:NB], small[:, 0:NB], small[:, 32:32 + NB], ALU.mult))
                ch.link(v.tensor_tensor(small[:, 0:NB], small[:, 0:NB], acc[:, :, C + 1], ALU.add))
                ch.link(v.tensor_copy(first_at[:, :], small[:, 0:NB]))
                ch.link(v.tensor_tensor(xres[:, :, :], xres[:, :, :], acc[:, :, 0:C], ALU.add))
                e.wait_ge(s_m, 1)
                ch.link(v.tensor_tensor(xres[:, 0:16, :], xres[:, 0:16, :], ps[:, 0, :].rearrange("p (b c) -> p b c", c=C), ALU.add))
                ch.link(v.tensor_tensor(xres[:, 16:NB, :], xres[:, 16:NB, :],
                                        ps[:, 1, 0:(NB - 16) * C].rearrange("p (b c) -> p b c", c=C), ALU.add))

            @block.tensor
            def _(e):
                e.wait_ge(s_w, 1)
                for b in range(NB):
                    last = nc.tensor.matmul(psf[:, b * C:(b + 1) * C], featT[0:C, b * P:(b + 1) * P], siw[:, :], start=True, stop=True)
                last.then_inc(s_m, 1)
        layer_norm_relu(xres, feat)

        for l in range(L):
            Wl, Wr = A["L1_gnn_Wl"][l], A["L1_gnn_Wr"][l]
            bl, br = A["L1_gnn_bl"][l], A["L1_gnn_br"][l]
            att = A["L1_gnn_att"][l].rearrange("h c -> (h c)")
            turn_features()
            with Phase() as ph:
                s_in, s_c = ph.sem("weights_in"), ph.sem("dve_step")
                block = ph.block()

                @block.sync
                def _(e):
                    n = 0
                    for k, w in enumerate((Wl, Wr, Wl, Wr)):
                        e.dma_start(wst[k * C:(k + 1) * C, :], w).then_inc(s_in, 16)
                    for dst_t, w, b in ((wl_aug, Wl, bl), (wr_aug, Wr, br)):
                        e.dma_start(dst_t[0:C, :], w).then_inc(s_in, 16)
                        e.dma_start(dst_t[C:C + 1, :], b.rearrange("(a n) -> a n", a=1)).then_inc(s_in, 16)
                    e.dma_start(attb[:, :], row_bcast(att)).then_inc(s_in, 16)
                    e.dma_start(attc[:, :], att.rearrange("(k p) -> p k", p=P)).then_inc(s_in, 16)
                    e.dma_start(bz[:, 0:2], bl.rearrange("(k p) -> p k", p=P)).then_inc(s_in, 16)
                    e.dma_start(bz[:, 2:4], br.rearrange("(k p) -> p k", p=P)).then_inc(s_in, 16)
                    for h in range(H):
                        e.dma_start(wlr[(h % 4) * C:(h % 4 + 1) * C, h // 4, :], Wl[:, h * C:(h + 1) * C]).then_inc(s_in, 16)
                    e.dma_start(vecs[:, 0, :], row_bcast(bl)).then_inc(s_in, 16)
                    for k, name in enumerate(("conv_bias", "bn_gamma", "bn_beta")):
                        e.dma_start(vecs[:, 1 + k, 0:C], row_bcast(A["L1_gnn_" + name][l])).then_inc(s_in, 16)
                    e.wait_ge(s_in, 16 * 24)

                @block.vector
                def _(e):
                    v = nc.vector
                    ch = Chain(e, s_c)
                    ch.link(v.memset(attp[:, :, :], 0.0))
                    e.wait_ge(s_in, 16 * 24)
                    for h in range(H):
                        a, half = h % 4, h // 4
                        v.tensor_copy(attp[a * C:(a + 1) * C, half, h:P:40], attc[a * C:(a + 1) * C, half:half + 1].to_broadcast([C, 4]))
                    ch.link(v.tensor_tensor(bz[:, 0:2], bz[:, 0:2], bz[:, 2:4], ALU.add))
                    ch.link(v.tensor_tensor(wz[:, 0:HC], wl_aug[:, :], wr_aug[:, :], ALU.add))
                    ch.link(v.tensor_scalar(wlr[:, :, :], wlr[:, :, :], 1.0 / H, None, ALU.mult))
                    ch.link(v.tensor_reduce(small[:, 0:C], vecs[:, 0, :].rearrange("p (h c) -> p c h", c=C), AX.X, ALU.add))
                    ch.link(v.scalar_tensor_tensor(vecs[:, 1, 0:C], small[:, 0:C], 1.0 / H, vecs[:, 1, 0:C], ALU.mult, ALU.add))

            with Phase() as ph:
                s_z, s_r, s_l, s_p, s_f, s_e = (ph.sem(n) for n in (
                    "self_z", "self_copied", "self_logit", "self_prod", "features_out", "self_leaky"))
                s_sc = ph.sem("first_rows_put")
                block = ph.block()
                rz = work[:, 3200:3712].rearrange("p (s n) -> p s n", s=2)

                @block.sync
                def _(e):
                    e.dma_start(table.rearrange("(b p) c -> p b c", p=P), feat[:, :, :]).then_inc(s_f, 16)
                    e.wait_ge(s_f, 16)

                @block.gpsimd
                def _(e):
                    for b in range(NB):
                        e.indirect_dma_start(out=first_rows[:, :], out_offset=bass.IndirectOffsetOnAxis(ap=first_at[:, b:b + 1], axis=0),
                                             in_=feat[:, b, :], in_offset=None).then_inc(s_sc, 16)
                    e.wait_ge(s_sc, 16 * NB)

                @block.tensor
                def _(e):
                    for b in range(NB):
                        wait(e, s_r, b - 1)
                        nc.tensor.matmul(ps[:, b % 2, 0:HC], featT[:, b * P:(b + 1) * P], wz[:, :], start=True, stop=True).then_inc(s_z, 1)

                @block.scalar
                def _(e):
                    for b in range(NB):
                        e.wait_ge(s_z, b + 1)
                        wait(e, s_l, b - 1)
                        nc.scalar.activation(rz[:, b % 2, :], ps[:, b % 2, 0:HC], ACT.Copy).then_inc(s_r, 1)

                @block.vector
                def _(e):
                    v = nc.vector
                    for par in range(2):
                        v.tensor_copy(stage[:, par, 0:CH], src_jc[:, par, :])
                    v.tensor_copy(stage[:, 0, CH:], dst_jc[:, 0, :])
                    v.memset(SAME[:, 0, :, :], 0.0)
                    v.memset(SAME[0:C, 1, :, :], 0.0)
                    v.memset(SAME[2 * C:3 * C, 1, :, :], 0.0)
                    for b in range(NB):
                        z = rz[:, b % 2, :]
                        e.wait_ge(s_r, b + 1)
                        v.scalar_tensor_tensor(z, z, 0.2, z, ALU.mult, ALU.max).then_inc(s_e, 1)
                        e.wait_ge(s_e, b + 1)
                        v.tensor_tensor(z, z, attb[:, :], ALU.mult).then_inc(s_p, 1)
                        e.wait_ge(s_p, b + 1)
                        v.tensor_reduce(lself[:, b, :], z.rearrange("p (h c) -> p h c", c=C), AX.X, ALU.add).then_inc(s_l, 1)

            with Phase() as ph:
                s_ready = [ph.sem("staged0"), ph.sem("staged1")]
                s_gath = [ph.sem("gathered0"), ph.sem("gathered1")]
                s_v = [ph.sem("first0"), ph.sem("first1")]
                s_gate = ph.sem("gate_passed")
                s_tr, s_xt, s_z, s_r, s_e, s_q, s_xs, s_lge, s_dst = (ph.sem(n) for n in (
                    "turned", "filled", "z", "z_copied", "leaky", "logits", "src_kept", "logits_out", "dst_rows"))
                block = ph.block()

                @block.gpsimd
                def _(e):
                    gather_program(e, s_ready, s_gath, s_gate, s_dst)

                @block.sync
                def _(e):
                    fr = first_rows[0:EP, :].rearrange("(c j p) r -> j p c r", c=CH, p=P)
                    sd = same_d.rearrange("(r s q) (j e) -> j s q r e", r=2, s=2, e=P)

                    def window(j, par, i):
                        if first(j) and j == 0:
                            return
                        wait(e, s_tr, j - 1)
                        wait(e, s_xt, 8 * j - 8)
                        for q in range(4):
                            src = fr[j] if first(j) else fr[bass.ds(j, 1)].rearrange("a p c r -> (a p) c r")
                            e.dma_start(ring[:, par, 4 * q:4 * q + 4, C:], src[:, q:CH:4, :]).then_inc(s_v[par], 16)
                            for s in range(2):
                                m = sd[j] if first(j) else sd[bass.ds(j, 1)].rearrange("a s q r e -> (a s) q r e")
                                e.dma_start(SAME[(2 * s + 1) * C:(2 * s + 2) * C, par, 2 * q:2 * q + 2, :],
                                            m[s, q].partition_broadcast(C)).then_inc(s_v[par], 16)
                    pairs(e, window)
                VW1 = 12 * 16

                def loaded(e, j, par, i):
                    if first(j) and j == 0:
                        e.wait_ge(s_dst, CH * GATHER)
                    else:
                        e.wait_ge(s_v[par], VW1 * i + (VW1 if par else 0))

                @block.tensor
                def _(e):
                    def z(j, par, q):
                        wait(e, s_r, 8 * j + 2 * q - 2)
                        e.wait_ge(s_xt, 8 * j + 2 * q + 2)
                        for half in range(2):
                            for side in range(2):
                                last = nc.tensor.matmul(ps[:, 2 + 2 * (q % 2) + side, half * 256:(half + 1) * 256],
                                                        wst[64 * side:64 * side + 64, half * P:(half + 1) * P],
                                                        XT[64 * side:64 * side + 64, par, 2 * q:2 * q + 2, :],
                                                        start=True, stop=True)
                        last.then_inc(s_z, 1)

                    def logits(j, par, q):
                        e.wait_ge(s_e, 4 * j + q + 1)
                        for half in range(2):
                            for g in range(4):
                                last = nc.tensor.matmul(ps[32 * g:32 * g + 32, 6 + par, 0:P], attp[:, half, 32 * q:32 * q + 32],
                                                        RE[:, q, half, (g % 2) * 256 + (g // 2) * P:(g % 2) * 256 + (g // 2) * P + P],
                                                        start=(q == 0 and half == 0), stop=(q == 3 and half == 1), skip_group_check=True)
                        last.then_inc(s_q, 1)

                    def turn(j, par, i):
                        e.wait_ge(s_gath[par], GW * i + GW)
                        loaded(e, j, par, i)
                        wait(e, s_xt, 8 * j)
                        for k in range(8):
                            last = nc.tensor.transpose(psf[:, k * P:(k + 1) * P],
                                                       ring[:, par, 2 * k:2 * k + 2, :].rearrange("p g r -> p (g r)"), ident[:, :])
                        last.then_inc(s_tr, 1)

                    def window(j, par, i):
                        z(j, par, 0)
                        z(j, par, 1)
                        z(j, par, 2)
                        wait(e, s_lge, j - 1)
                        logits(j, par, 0)
                        z(j, par, 3)
                        logits(j, par, 1)
                        if not (first(j) and j == J - 1):
                            turn(j + 1, 1 - par, i + par)
                        logits(j, par, 2)
                        logits(j, par, 3)
                    turn(0, 0, 0)
                    pairs(e, window)

                @block.scalar
                def _(e):
                    def window(j, par, i):
                        at = bass.ds(j, 1) if not first(j) else slice(j, j + 1)
                        e.wait_ge(s_gath[par], GW * i + GW)
                        for g in range(4):
                            kept = xsr[:, 4 * g * J:4 * (g + 1) * J, :].rearrange("p (c j) k -> p j c k", j=J)[:, at, :, 0:C].rearrange("p a c k -> p (a c) k")
                            nc.scalar.activation(kept, ring[:, par, g:CH:4, 0:C], ACT.Copy).then_inc(s_xs, 1)
                        for q in range(4):
                            e.wait_ge(s_z, 4 * j + q + 1)
                            wait(e, s_q, 4 * j + q - 3)
                            for half in range(2):
                                nc.scalar.activation(RE[:, q, half, :].rearrange("p (s e) -> p s e", s=2),
                                                     ps[:, 2 + 2 * (q % 2):4 + 2 * (q % 2), half * 256:(half + 1) * 256],
                                                     ACT.Identity, bias=bz[:, half:half + 1]).then_inc(s_r, 1)
                        e.wait_ge(s_q, 4 * j + 4)
                        col = bass.ds(j * P, P) if not first(j) else slice(j * P, j * P + P)
                        nc.scalar.activation(logit[:, col], ps[:, 6 + par, 0:P], ACT.Copy).then_inc(s_lge, 1)
                    pairs(e, window)

                @block.vector
                def _(e):
                    v = nc.vector
                    v.memset(small[:, 0:1], 0.0).then_inc(s_ready[0], 1)
                    v.memset(small[:, 1:2], 0.0).then_inc(s_ready[1], 1)

                    def window(j, par, i):
                        e.wait_ge(s_tr, j + 1)
                        loaded(e, j, par, i)
                        wait(e, s_q, 4 * j - 4)
                        wait(e, s_xt, 8 * j)
                        for k in range(8):
                            v.tensor_tensor_scan(XT[:, par, k, :], SAME[:, par, k, :], psf[:, k * P:(k + 1) * P],
                                                 0.0 if first(j) and j == 0 else XT[:, 1 - par, k, P - 1:P],
                                                 ALU.mult, ALU.add).then_inc(s_xt, 1)
                        if not (first(j) and j + 2 >= J):
                            e.wait_ge(s_gate, j + 1)
                            e.wait_ge(s_xs, 4 * j + 4)
                            at = bass.ds(j, 1) if not first(j) else slice(j, j + 1)
                            v.tensor_copy(stage[:, par, 0:CH], src_next[:, at, :].rearrange("p a c -> p (a c)")).then_inc(s_ready[par], 1)
                        for q in range(4):
                            e.wait_ge(s_r, 8 * j + 2 * q + 2)
                            zc = RE[:, q, :, :].rearrange("p h e -> p (h e)")
                            v.scalar_tensor_tensor(zc, zc, 0.2, zc, ALU.mult, ALU.max).then_inc(s_e, 1)
                    pairs(e, window)

            with Phase() as ph:
                s_c, s_d, s_e, s_t, s_o = (ph.sem(n) for n in ("dve_step", "carries", "exp", "turned", "copied"))
                block = ph.block()
                ends = small[:, 0:2]
                carry = small[:, 4:6]
                eh = small[0:H, 16:16 + 2 * CH].rearrange("p (k c) -> p k c", k=2)
                cc = small[0:H, 64:64 + 2 * (CH + 1)].rearrange("p (k c) -> p k c", k=2)
                probs = logit

                @block.vector
                def _(e):
                    v = nc.vector
                    ch = Chain(e, s_c)
                    ch.mark(v.tensor_tensor_scan(SCAN_F, start_pen[:, :], logit[:, :], -BIG, ALU.add, ALU.max))
                    ch.link(v.tensor_tensor_scan(SCAN_B[:, ::-1], end_pen[:, ::-1], logit[:, ::-1], -BIG, ALU.add, ALU.max))
                    ch.link(v.tensor_copy(ends[:, 0:1], SCAN_F[:, CE - 1:CE]))
                    ch.link(v.tensor_copy(ends[:, 1:2], SCAN_B[:, 0:1]))
                    ch.link(v.memset(small[0:H, 64:64 + 2 * (CH + 1)], -BIG))
                    e.wait_ge(s_d, 48)
                    ch.mark(v.tensor_tensor_scan(cc[:, 0, 1:CH + 1], pens[:, 0, :], eh[:, 0, :], -BIG, ALU.add, ALU.max))
                    ch.link(v.tensor_tensor_scan(cc[:, 1, 0:CH][:, ::-1], pens[:, 1, ::-1], eh[:, 1, ::-1], -BIG, ALU.add, ALU.max))
                    e.wait_ge(s_d, 112)
                    ch.mark(v.tensor_tensor_scan(SCAN_F, start_pen[:, :], logit[:, :], carry[:, 0:1], ALU.add, ALU.max))
                    ch.link(v.tensor_tensor_scan(SCAN_B[:, ::-1], end_pen[:, ::-1], logit[:, ::-1], carry[:, 1:2], ALU.add, ALU.max))
                    ch.link(v.tensor_tensor(SCAN_F, SCAN_F, SCAN_B, ALU.max))
                    ch.link(v.tensor_tensor(logit[:, :], logit[:, :], SCAN_F, ALU.subtract))
                    for j in range(J):
                        e.wait_ge(s_t, j + 1)
                        pmv = pm[:, :, :].rearrange("p (c j) k -> p j c k", j=J)[:, j, :, :]
                        lj = lastf[:, :].rearrange("p (c j) -> p j c", j=J)[:, j, :, None].to_broadcast([P, CH, H])
                        v.tensor_copy(pmv[:, :, 0:H], ps[:, j % 2, 0:P].rearrange("p (c h) -> p c h", h=H))
                        v.tensor_tensor(pmv[:, :, H:], ps[:, j % 2, P:2 * P].rearrange("p (c h) -> p c h", h=H), lj, ALU.mult).then_inc(s_o, 1)

                @block.sync
                def _(e):
                    e.wait_ge(s_c, 5)
                    e.dma_start(ends_d, ends).then_inc(s_d, 16)
                    e.wait_ge(s_d, 16)
                    for k in range(2):
                        e.dma_start(eh[:, k, :], ends_d[:, k].rearrange("(c h) -> h c", h=H)).then_inc(s_d, 16)
                    e.wait_ge(s_c, 7)
                    e.dma_start(carry_d[:, 0, :], cc[:, 0, 0:CH]).then_inc(s_d, 16)
                    e.dma_start(carry_d[:, 1, :], cc[:, 1, 1:CH + 1]).then_inc(s_d, 16)
                    e.wait_ge(s_d, 80)
                    for k in range(2):
                        e.dma_start(carry[:, k:k + 1], carry_d[:, k, :].rearrange("h c -> c h")).then_inc(s_d, 16)

                @block.scalar
                def _(e):
                    e.wait_ge(s_c, 11)
                    nc.scalar.activation(logit[:, :], logit[:, :], ACT.Exp).then_inc(s_e, 1)

                @block.tensor
                def _(e):
                    e.wait_ge(s_e, 1)
                    for j in range(J):
                        wait(e, s_o, j - 1)
                        nc.tensor.transpose(ps[:, j % 2, 0:P], logit[:, j * P:(j + 1) * P], ident[:, :])
                        nc.tensor.transpose(ps[:, j % 2, P:2 * P], SCAN_F[:, j * P:(j + 1) * P], ident[:, :]).then_inc(s_t, 1)

            def attention_values(v, slot, t4):
                v.tensor_copy(slotV[:, slot, :, HC:], pm[:, bass.ds(t4, ST), :])
                return v.tensor_tensor(slotV[:, slot, :, 0:HC].rearrange("p t (h c) -> p t h c", c=C),
                                pm[:, bass.ds(t4, ST), 0:H, None].to_broadcast([P, ST, H, C]),
                                xsr[:, bass.ds(t4, ST), None, 0:C].to_broadcast([P, ST, H, C]), ALU.mult)

            segment_sums(VW, attention_values)

            with Phase() as ph:
                s_c, s_x = ph.sem("dve_step"), ph.sem("exps")
                s_g, s_t, s_a, s_m, s_o = (ph.sem(n) for n in ("means", "turned", "turned_copied", "heads", "conv"))
                block = ph.block()
                G = 5
                NH = NB * H
                m1 = small[:, 0:NH].rearrange("p (b h) -> p b h", h=H)
                m2 = small[:, NH:2 * NH].rearrange("p (b h) -> p b h", h=H)
                w12 = small[:, 0:2 * NH]
                mx = small[:, 2 * NH:3 * NH].rearrange("p (b h) -> p b h", h=H)
                cb = small[:, 3 * NH:3 * NH + NB]
                own = work[:, 0:G * HC].rearrange("p (b h c) -> p b h c", h=H, c=C)
                AT = work[:, G * HC:3 * G * HC].rearrange("p (s b k n) -> p s b k n", s=2, b=G, k=2)

                @block.vector
                def _(e):
                    v = nc.vector
                    ch = Chain(e, s_c)
                    ch.link(v.tensor_scalar(cb, count[:, :], -1.0, BIG, ALU.add, ALU.mult))
                    ch.link(v.tensor_tensor(m1, acc[:, :, HC + H:], cb[:, :, None].to_broadcast([P, NB, H]), ALU.add))
                    ch.link(v.tensor_tensor(mx, m1, lself[:, :, :], ALU.max))
                    ch.link(v.tensor_tensor(m1, m1, mx, ALU.subtract))
                    ch.link(v.tensor_tensor(m2, lself[:, :, :], mx, ALU.subtract))
                    e.wait_ge(s_x, 1)
                    ch.link(v.tensor_tensor(mx, acc[:, :, HC:HC + H], m1, ALU.mult))
                    ch.link(v.tensor_tensor(mx, mx, m2, ALU.add))
                    ch.link(v.tensor_scalar(mx, mx, 1e-16, None, ALU.add))
                    ch.link(v.reciprocal(mx, mx))
                    ch.mark(v.tensor_tensor(m1, m1, mx, ALU.mult))
                    ch.link(v.tensor_tensor(m2, m2, mx, ALU.mult))

                    def conv_out(g):
                        e.wait_ge(s_m, g + 1)
                        v.tensor_tensor(conv[:, g * G:(g + 1) * G, :], ps[:, 6 + g % 2, 0:G * C].rearrange("p (b c) -> p b c", c=C),
                                        vecs[:, 1, None, 0:C].to_broadcast([P, G, C]), ALU.add).then_inc(s_o, 1)
                    for g in range(NB // G):
                        lo, hi = g * G, (g + 1) * G
                        a = acc[:, lo:hi, 0:HC].rearrange("p b (h c) -> p b h c", c=C)
                        ch.mark(v.tensor_tensor(a, a, m1[:, lo:hi, :, None].to_broadcast([P, G, H, C]), ALU.mult))
                        ch.link(v.tensor_tensor(own, feat[:, lo:hi, None, :].to_broadcast([P, G, H, C]),
                                                m2[:, lo:hi, :, None].to_broadcast([P, G, H, C]), ALU.mult))
                        v.tensor_tensor(a, a, own, ALU.add).then_inc(s_g, 1)
                        e.wait_ge(s_g, g + 1)
                        if g >= 2:
                            conv_out(g - 2)
                    conv_out(NB // G - 2)
                    conv_out(NB // G - 1)

                @block.tensor
                def _(e):
                    def heads(g):
                        e.wait_ge(s_a, g + 1)
                        wait(e, s_o, g - 1)
                        for b in range(G):
                            for k in range(2):
                                last = nc.tensor.matmul(ps[:, 6 + g % 2, b * C:(b + 1) * C], AT[:, g % 2, b, k, :], wlr[:, k, :],
                                                        start=(k == 0), stop=(k == 1))
                        last.then_inc(s_m, 1)
                    for g in range(NB // G):
                        e.wait_ge(s_g, g + 1)
                        wait(e, s_a, g - 1)
                        for b in range(G):
                            for k in range(2):
                                n = (g % 2) * 3 * 512 + (2 * b + k) * P
                                last = nc.tensor.transpose(psf[:, n:n + P], acc[:, g * G + b, k * P:(k + 1) * P], ident[:, :])
                        last.then_inc(s_t, 1)
                        if g:
                            heads(g - 1)
                    heads(NB // G - 1)

                @block.scalar
                def _(e):
                    e.wait_ge(s_c, 5)
                    nc.scalar.activation(w12, w12, ACT.Exp).then_inc(s_x, 1)
                    for g in range(NB // G):
                        e.wait_ge(s_t, g + 1)
                        wait(e, s_m, g - 1)
                        nc.scalar.activation(AT[:, g % 2, :, :, :].rearrange("p b k n -> p (b k n)"),
                                             psf[:, (g % 2) * 3 * 512:(g % 2) * 3 * 512 + 2 * G * P], ACT.Copy).then_inc(s_a, 1)

            with Phase() as ph:
                s_c, s_m, s_q = (ph.sem(n) for n in ("dve_step", "node_sums", "root"))
                block = ph.block()
                flat = work[:, 0:NB * C].rearrange("p (b c) -> p b c", c=C)
                part = small[:, 0:C]
                mean, var, rstd, shift = (small[:, 32 * k:32 * k + C] for k in range(1, 5))

                @block.vector
                def _(e):
                    v = nc.vector
                    ch = Chain(e, s_c)
                    mask = nodemask[:, :, None].to_broadcast([P, NB, C])
                    if l < L - 1:
                        ch.link(v.scalar_tensor_tensor(conv[:, :, :], conv[:, :, :], 0.01, conv[:, :, :], ALU.mult, ALU.max))
                    ch.link(v.tensor_tensor(feat[:, :, :], feat[:, :, :], conv[:, :, :], ALU.add))
                    ch.link(v.tensor_tensor(feat[:, :, :], feat[:, :, :], mask, ALU.mult))
                    ch.link(v.tensor_reduce(part, feat[:, :, :].rearrange("p b c -> p c b"), AX.X, ALU.add))
                    n1 = ch.n
                    e.wait_ge(s_m, 1)
                    ch.link(v.tensor_scalar(mean, ps[:, 0, 0:C], 1.0 / N, None, ALU.mult))
                    ch.link(v.tensor_tensor(feat[:, :, :], feat[:, :, :], mean[:, None, :].to_broadcast([P, NB, C]), ALU.subtract))
                    ch.link(v.tensor_tensor(flat, feat[:, :, :], mask, ALU.mult))
                    ch.link(v.tensor_tensor(flat, flat, flat, ALU.mult))
                    ch.link(v.tensor_reduce(part, flat.rearrange("p b c -> p c b"), AX.X, ALU.add))
                    e.wait_ge(s_m, 2)
                    ch.link(v.tensor_scalar(var, ps[:, 1, 0:C], 1.0 / N, EPS, ALU.mult, ALU.add))
                    e.wait_ge(s_q, 1)
                    ch.link(v.reciprocal(rstd, rstd))
                    ch.link(v.tensor_tensor(rstd, rstd, vecs[:, 2, 0:C], ALU.mult))
                    ch.link(v.tensor_tensor(feat[:, :, :], feat[:, :, :], rstd[:, None, :].to_broadcast([P, NB, C]), ALU.mult))
                    ch.link(v.tensor_tensor(feat[:, :, :], feat[:, :, :], vecs[:, 3, None, 0:C].to_broadcast([P, NB, C]), ALU.add))
                    if l == L - 1:
                        ch.link(v.tensor_tensor(xres[:, :, :], xres[:, :, :], feat[:, :, :], ALU.add))
                base = 4 if l < L - 1 else 3

                @block.tensor
                def _(e):
                    e.wait_ge(s_c, base)
                    nc.tensor.matmul(ps[:, 0, 0:C], ones[:, :], part, start=True, stop=True).then_inc(s_m, 1)
                    e.wait_ge(s_c, base + 5)
                    nc.tensor.matmul(ps[:, 1, 0:C], ones[:, :], part, start=True, stop=True).then_inc(s_m, 1)

                @block.scalar
                def _(e):
                    e.wait_ge(s_c, base + 6)
                    nc.scalar.activation(rstd, var, ACT.Sqrt).then_inc(s_q, 1)

        with Phase() as ph:
            s_o = ph.sem("out_written")
            block = ph.block()

            @block.sync
            def _(e):
                e.dma_start(out[0:(NB - 1) * P, :].rearrange("(b p) c -> p b c", p=P), xres[:, 0:NB - 1, :]).then_inc(s_o, 16)
                e.dma_start(out[(NB - 1) * P:N, :], xres[0:REAL, NB - 1, :]).then_inc(s_o, 16)
                e.wait_ge(s_o, 32)


NAMES = ("x", "src", "dst", "edge_attr_32", "edge_attr_4", "L0_gnn_W1", "L0_gnn_b1", "L0_gnn_W2", "L0_gnn_b2",
         "L0_gnn_si_w0", "L0_gnn_si_w1", "L1_gnn_Wl", "L1_gnn_bl", "L1_gnn_Wr", "L1_gnn_br", "L1_gnn_att",
         "L1_gnn_conv_bias", "L1_gnn_bn_gamma", "L1_gnn_bn_beta")


def kernel(**inputs):
    import numpy as np
    import concourse.bacc as bacc
    from concourse.bass_utils import run_bass_kernel_spmd as run

    nc = bacc.Bacc("TRN2", target_bir_lowering=False, num_devices=1)
    arrays, aps = {}, {}
    for name in NAMES:
        a = np.ascontiguousarray(inputs[name])
        arrays[name + "_in"] = a
        aps[name] = nc.dram_tensor(name + "_in", a.shape, mybir.dt.from_np(a.dtype), kind="ExternalInput").ap()
    out = nc.dram_tensor("out", (N, C), F32, kind="ExternalOutput").ap()
    build(nc, aps, out)
    return run(nc, [arrays], core_ids=[0]).results[0]["out"]
```

```python
import concourse.bass as bass
from concourse import mybir
from contextlib import ExitStack

F32 = mybir.dt.float32
BF16 = mybir.dt.bfloat16
I32 = mybir.dt.int32
ALU = mybir.AluOpType
ACT = mybir.ActivationFunctionType
AX = mybir.AxisListType

P = 128
N, E, C = 3125, 50000, 32
NB = 25
NP = NB * P
REAL = N - (NB - 1) * P
CH = 16
J = 25
T = CH * J
EP = T * P
CE = J * P
H, HC = 8, 256
VW = HC + 2 * H
MW = C + 2
ST = 4
NS = T // ST
FULL = -(-E // (ST * P))
ITEMS = FULL + NB - 1
PAD_WINDOW = -(-E // P) - (CH - 1) * J
PAD_NODE = NP - 1
BIG = 1e30
EPS = 1e-5
EROW = 40
L = 3
assert PAD_WINDOW % 2 == 0
MUL, MLP = 8, 64
ALPHA = 0.25
C110 = 3.0 ** -0.5
SI = 8.0 ** -0.5
GATHER = 16


class Chain:

    def __init__(self, eng, sem):
        self.eng, self.sem, self.n, self.base = eng, sem, 0, None

    def value(self):
        return self.n if self.base is None else self.base + self.n

    def mark(self, ins):
        ins.then_inc(self.sem, 1)
        self.n += 1
        return self.value()

    def link(self, ins):
        self.mark(ins)
        self.eng.wait_ge(self.sem, self.value())

    def enter(self, i, start, per):
        self.out, self.per = self.n, per
        self.base, self.n = i * per + (self.out - start * per), 0

    def leave(self, rounds):
        assert self.n == self.per, (self.n, self.per)
        self.n, self.base = self.out + self.per * rounds, None


def build(nc, A, out):
    ctx = ExitStack()
    with ctx, nc.allow_non_contiguous_dma(reason="small vectors and list transposes"):
        def sb(name, shape, dt=F32):
            return ctx.enter_context(nc.sbuf_tensor(name, shape, dt))

        def dram(name, shape, dt=F32):
            return nc.dram_tensor(name, shape, dt, kind="Internal").ap()

        dst_pad = dram("dst_pad", (EP + 2,), I32)
        src_pad = dram("src_pad", (EP,), I32)
        ea32_pad = dram("ea32_pad", (EP, C))
        ea4_pad = dram("ea4_pad", (EP, 4))
        edge_rows = dram("edge_rows", (EP, EROW))
        table = dram("table", (NP, C))
        first_rows = dram("first_rows", (EP + NP, C))
        same_d = dram("same_d", (CH, CE), BF16)
        pens_d = dram("pens_d", (P, 2))
        walk_d = dram("walk_d", (2, P))

        ident = sb("ident", [P, P])
        ones = sb("ones", [P, P])
        iota_f = sb("iota_f", [P, P])
        iota_i = sb("iota_i", [P, P], I32)
        part_f = sb("part_f", [P, 1])
        nodemask = sb("nodemask", [P, 1])
        of_chunk = sb("of_chunk", [P, CH])
        of_head = sb("of_head", [P, H])
        of_headT = sb("of_headT", [H, P])
        src_all = sb("src_all", [P, T + 2])
        srcf = src_all[:, 0:T]
        dstf = sb("dstf", [P, T])
        lastf = sb("lastf", [P, T])
        pen = sb("pen", [P, CE + 1], BF16)
        start_pen, end_pen = pen[:, 0:CE], pen[:, 1:CE + 1]
        pens = sb("pens", [H, 2, CH])
        walk_t = sb("walk_t", [1, P], I32)
        walk_b = sb("walk_b", [1, P], I32)
        base128 = sb("base128", [P, P])
        xres = sb("xres", [P, NB, C])
        feat = sb("feat", [P, NB, C])
        first_at = sb("first_at", [P, NB], I32)
        lself = sb("lself", [P, NB, H])
        count = sb("count", [P, NB])
        xsr = sb("xsr", [P, T, MW])
        pm = sb("pm", [P, T, 2 * H])
        ring = sb("ring", [P, 2, CH, 2 * C])
        gate = sb("gate", [P, 2])
        stage = sb("stage", [P, 2, CH], I32)
        start_dst = sb("start_dst", [CH, 1], I32)
        start_row = sb("start_row", [CH, C])
        work = sb("work", [P, 14000])
        logit = work[:, 8192:8192 + CE]
        SLOTS = 4
        slotV = work[:, 0:SLOTS * ST * VW].rearrange("p (s t w) -> p s t w", s=SLOTS, t=ST)
        slotO = work[:, SLOTS * ST * VW:SLOTS * ST * (VW + P)].rearrange("p (s t w) -> p s t w", s=SLOTS, t=ST)
        acc = work[:, 6400:6400 + NB * VW].rearrange("p (b w) -> p b w", b=NB)
        conv = work[:, 13200:13200 + NB * C].rearrange("p (b c) -> p b c", c=C)
        accT = work[0:MW, 6400:6400 + NP].rearrange("w (b n) -> w b n", b=NB)
        featT = work[0:C + 1, 0:NP]
        apart = sb("apart", [P, ITEMS, ST])
        ROUNDS = ITEMS // 4
        small = sb("small", [P, 1024])
        wst = sb("wst", [P, HC])
        wl_aug = sb("wl_aug", [C + 1, HC])
        wr_aug = sb("wr_aug", [C + 1, HC])
        wz = sb("wz", [C + 1, HC])
        attb = sb("attb", [P, HC])
        attc = sb("attc", [P, 2])
        attp = sb("attp", [P, 2, P])
        bz = sb("bz", [P, 4])
        wlr = sb("wlr", [P, 2, C])
        vecs = sb("vecs", [P, 4, HC])
        w1_sb = sb("w1_sb", [P, 4, MLP])
        b1_sb = sb("b1_sb", [MLP, 1])
        w2_sb = sb("w2_sb", [MLP + 1, HC])
        siw = sb("siw", [C, C])
        ea4 = sb("ea4", [P, T, 4])
        unsorted = sb("unsorted", [1, 1], I32)

        ps = ctx.enter_context(nc.psum_tensor("ps", [P, 8, 512], F32))
        psf = ps[:, :, :].rearrange("p a b -> p (a b)")

        XT = work[:, 0:2048].rearrange("p (s q e) -> p s q e", s=2, e=P)
        RE = work[:, 2048:6144].rearrange("p (s h e) -> p s h e", s=4, h=2)
        SAME = work[:, 6144:7168].bitcast(BF16).rearrange("p (s q e) -> p s q e", s=2, e=P)
        EA = work[:, 0:1024].rearrange("p (s c k) -> p s c k", s=2, k=C)
        EAT = work[:, 1024:1024 + 2 * P].rearrange("p (s e) -> p s e", s=2)
        H1T = work[0:MLP + 1, 2048:3072].rearrange("p (s e) -> p s e", s=2)
        COEF = work[:, 3072:4608].rearrange("p (s c r i) -> p s c r i", s=2, c=CH, r=6)
        RED = work[:, 4608:5376].rearrange("p (c r o) -> p c r o", c=CH, r=6)
        TMP = work[:, 5376:5760].rearrange("p (c i m) -> p c i m", c=CH, m=3)
        XC = work[:, 5760:6784].rearrange("p (s c r) -> p s c r", s=2, r=C)
        PROD = work[:, 6784:11392].rearrange("p (s t r) -> p s t r", s=3, t=4)
        SCAN_F = work[:, 0:CE]
        SCAN_B = work[:, CE:2 * CE]

        names = [0]

        class Phase:

            def __enter__(self):
                self.ctx, self.sems = ExitStack(), []
                names[0] += 1
                return self

            def sem(self, name):
                self.sems.append(nc.alloc_semaphore(name=f"{name}_{names[0]}"))
                return self.sems[-1]

            def block(self):
                return self.ctx.enter_context(nc.Block())

            def __exit__(self, *a):
                self.ctx.close()
                nc.clear_and_free_semaphores(self.sems)
                nc.all_engine_barrier()

        def row_bcast(ap, parts=P):
            return ap.partition_broadcast(parts)

        mean_at, var_at = small[:, 0:NB], small[:, 32:32 + NB]
        VARIANCE_STEP = 6

        def layer_norm_steps(e, ch, s_q, src, dst):
            v = nc.vector
            sq = work[:, 2048:2048 + NB * C].rearrange("p (b c) -> p b c", c=C)
            ch.link(v.tensor_reduce(mean_at, src[:, :, :], AX.X, ALU.add))
            ch.link(v.tensor_scalar(mean_at, mean_at, 1.0 / C, None, ALU.mult))
            ch.link(v.tensor_tensor(dst[:, :, :], src[:, :, :], mean_at[:, :, None].to_broadcast([P, NB, C]), ALU.subtract))
            ch.link(v.tensor_tensor(sq, dst[:, :, :], dst[:, :, :], ALU.mult))
            ch.link(v.tensor_reduce(var_at, sq, AX.X, ALU.add))
            ch.link(v.tensor_scalar(var_at, var_at, 1.0 / C, EPS, ALU.mult, ALU.add))
            e.wait_ge(s_q, 1)
            ch.link(v.reciprocal(mean_at, var_at))
            ch.link(v.tensor_tensor(dst[:, :, :], dst[:, :, :], mean_at[:, :, None].to_broadcast([P, NB, C]), ALU.mult))
            ch.link(v.tensor_scalar(dst[:, :, :], dst[:, :, :], 0.0, None, ALU.max))

        s_attr4, s_attr32 = nc.alloc_semaphore(name="attr4_copied"), nc.alloc_semaphore(name="attr32_copied")
        with Phase() as ph:
            s_x, s_pads, s_pool, s_dma = (ph.sem(n) for n in ("attr_pads", "set", "pool_step", "copies"))
            block = ph.block()
            padi = small[0:1, 0:1024].bitcast(I32)
            minus, beyond = stage[0:1, 0, 0:1], stage[0:1, 0, 1:2]

            @block.gpsimd
            def _(e):
                ch = Chain(e, s_pool)
                ch.link(e.memset(ident[:, :], 0.0))
                ch.link(e.affine_select(out=ident[:, :], in_=ident[:, :], compare_op=ALU.not_equal, fill=1.0,
                                        base=0, pattern=[[-1, P]], channel_multiplier=1))
                ch.link(e.memset(nodemask[:, :], 1.0))
                ch.link(e.affine_select(out=nodemask[:, :], in_=nodemask[:, :], compare_op=ALU.is_gt,
                                        fill=0.0, base=REAL, pattern=[[0, 1]], channel_multiplier=-1))
                ch.link(e.iota(iota_i[:, :], pattern=[[1, P]], base=0, channel_multiplier=0))
                ch.link(e.tensor_copy(iota_f[:, :], iota_i[:, :]))
                ch.link(e.iota(iota_i[:, 0:1], pattern=[[0, 1]], base=0, channel_multiplier=1))
                ch.link(e.tensor_copy(part_f[:, :], iota_i[:, 0:1]))

            @block.vector
            def _(e):
                v = nc.vector
                v.memset(padi, PAD_NODE)
                v.memset(beyond, NP)
                v.memset(minus, -1).then_inc(s_pads, 1)
                v.memset(siw[:, :], 0.0)
                v.memset(w1_sb[:, :, :], 0.0)
                v.memset(xres[:, NB - 1, :], 0.0).then_inc(s_pads, 1)
                v.memset(ring[:, :, :, :], 0.0).then_inc(s_pads, 1)
                v.memset(ones[:, :], 1.0)
                v.memset(src_all[:, T:], 0.0)
                v.memset(gate[:, :], 0.0)
                v.memset(SAME[:, :, :, :], 0.0)

            @block.sync
            def _(e):
                e.dma_start(dst_pad[1:E + 1], A["dst"]).then_inc(s_dma, 16)
                e.dma_start(src_pad[0:E], A["src"]).then_inc(s_dma, 16)
                pads = EP - E
                e.wait_ge(s_pads, 1)
                e.dma_start(dst_pad[EP + 1:EP + 2].rearrange("(a n) -> a n", a=1), beyond).then_inc(s_dma, 16)
                e.dma_start(dst_pad[0:1].rearrange("(a n) -> a n", a=1), minus).then_inc(s_dma, 16)
                n = 4
                for o in range(0, pads, 1024):
                    w = min(1024, pads - o)
                    e.dma_start(dst_pad[1 + E + o:1 + E + o + w].rearrange("(a n) -> a n", a=1), padi[:, 0:w]).then_inc(s_dma, 16)
                    w = min(1024, EP - E - o)
                    e.dma_start(src_pad[E + o:E + o + w].rearrange("(a n) -> a n", a=1), padi[:, 0:w]).then_inc(s_dma, 16)
                    n += 2
                e.wait_ge(s_pads, 2)
                e.dma_start(xres[:, 0:NB - 1, :], A["x"][0:(NB - 1) * P, :].rearrange("(b p) c -> p b c", p=P)).then_inc(s_dma, 16)
                e.dma_start(xres[0:REAL, NB - 1, :], A["x"][(NB - 1) * P:N, :]).then_inc(s_dma, 16)
                for k in range(4):
                    e.dma_start(w1_sb[k * C:(k + 1) * C, k, :], A["L0_gnn_W1"]).then_inc(s_dma, 16)
                e.dma_start(b1_sb[:, :], A["L0_gnn_b1"].rearrange("(p a) -> p a", a=1)).then_inc(s_dma, 16)
                W2, b2 = A["L0_gnn_W2"], A["L0_gnn_b2"].rearrange("(a n) -> a n", a=1)
                for at, lo, hi in ((0, 0, 64), (64, 192, 256), (128, 64, 192)):
                    e.dma_start(w2_sb[0:MLP, at:at + hi - lo], W2[:, lo:hi]).then_inc(s_dma, 16)
                    e.dma_start(w2_sb[MLP:MLP + 1, at:at + hi - lo], b2[:, lo:hi]).then_inc(s_dma, 16)
                e.dma_start(siw[0:MUL, 0:MUL], A["L0_gnn_si_w0"]).then_inc(s_dma, 16)
                n += 2 + 4 + 1 + 6 + 1
                for m in range(3):
                    e.dma_start(siw[MUL + m:C:3, MUL + m:C:3], A["L0_gnn_si_w1"]).then_inc(s_dma, 16)
                    n += 1
                e.wait_ge(s_dma, 16 * n)

            @block.scalar
            def _(e):
                e.wait_ge(s_pads, 3)
                zeros = ring[:, :, :, :].rearrange("p a b c -> p (a b c)")
                for o in range(E, EP, P):
                    w = min(P, EP - o)
                    e.dma_start(ea32_pad[o:o + w, :], zeros[0:w, 0:C]).then_inc(s_x, 16)
                    e.dma_start(ea4_pad[o:o + w, :], zeros[0:w, 0:4]).then_inc(s_x, 16)
                e.dma_start(ea4_pad[0:E, :], A["edge_attr_4"]).then_inc(s_attr4, 16)
                e.dma_start(ea32_pad[0:E, :], A["edge_attr_32"]).then_inc(s_attr32, 16)
                e.wait_ge(s_x, 16 * 2 * -(-(EP - E) // P))

        with Phase() as ph:
            s_in, s_c, s_m, s_k, s_n, s_q, s_o = (ph.sem(n) for n in (
                "lists_in", "dve_step", "counted", "masks", "norm_step", "root", "table_out"))
            block = ph.block()
            here, after = (work[:, k * T:(k + 1) * T].bitcast(I32) for k in range(2))

            @block.sync
            def _(e):
                for k, a in enumerate((here, after)):
                    e.dma_start(a, dst_pad[1 + k:1 + k + EP].rearrange("(p n) -> p n", n=T)).then_inc(s_in, 16)

            @block.vector
            def _(e):
                v = nc.vector
                ch = Chain(e, s_n)
                layer_norm_steps(e, ch, s_q, xres, feat)
                ch.link(v.tensor_scalar(w2_sb[:, :], w2_sb[:, :], ALPHA, None, ALU.mult))
                ch.link(v.tensor_scalar(w2_sb[:, 64:128], w2_sb[:, 64:128], C110, None, ALU.mult))
                ch = Chain(e, s_k)
                for lanes, number, masks in ((P, part_f[:, 0:1], ((of_chunk, CH, True), (of_head, H, False))),
                                             (H, iota_f[0:H, :], ((of_headT, P, False),))):
                    n = number.shape[-1]
                    whole, chunk, head = (small[0:lanes, 256 + k * P:256 + k * P + n] for k in range(3))
                    ch.link(v.tensor_copy(whole.bitcast(I32), number))
                    ch.link(v.tensor_scalar(whole.bitcast(I32), whole.bitcast(I32), 3, None, ALU.arith_shift_right))
                    ch.link(v.tensor_copy(chunk, whole.bitcast(I32)))
                    ch.link(v.tensor_scalar(head, chunk, -float(H), None, ALU.mult))
                    ch.link(v.tensor_tensor(head, head, number, ALU.add))
                    for mask, width, by_c in masks:
                        if n == 1:
                            ch.link(v.tensor_scalar(mask[:, :], iota_f[:, 0:width], chunk if by_c else head, None, ALU.is_equal))
                        else:
                            ch.link(v.tensor_scalar(mask[:, :], head, part_f[0:H, 0:1], None, ALU.is_equal))
                ch = Chain(e, s_c)
                e.wait_ge(s_in, 32)
                ch.link(v.tensor_tensor(work[:, 2 * T:3 * T], here, after, ALU.is_gt))
                ch.link(v.tensor_reduce(small[:, 128:129], work[:, 2 * T:3 * T], AX.X, ALU.add))
                e.wait_ge(s_m, 1)
                ch.link(v.tensor_scalar(unsorted[:, :], ps[0:1, 0, 0:1], 0.0, None, ALU.is_gt))

            @block.tensor
            def _(e):
                e.wait_ge(s_c, 2)
                nc.tensor.matmul(ps[:, 0, 0:1], ones[:, :], small[:, 128:129], start=True, stop=True).then_inc(s_m, 1)

            @block.scalar
            def _(e):
                e.wait_ge(s_n, VARIANCE_STEP)
                nc.scalar.activation(var_at, var_at, ACT.Sqrt).then_inc(s_q, 1)
                e.wait_ge(s_n, VARIANCE_STEP + 3)
                e.dma_start(table.rearrange("(b p) c -> p b c", p=P), feat[:, :, :]).then_inc(s_o, 16)
                e.wait_ge(s_o, 16)

        with Phase() as ph:
            s_k, s_st, s_th, s_cmp, s_row, s_idx, s_gate, s_put, s_back, s_i = (ph.sem(n) for n in (
                "chunk_in", "tile_dst_in", "threshold_step", "compared", "row_in", "rank_staged", "gate_passed",
                "row_put", "list_back", "iotas"))
            block = ph.block()
            key_i = work[:, 0:CE].bitcast(I32)
            key, less, place = (work[:, k * CE:(k + 1) * CE] for k in (0, 1, 2))
            pmf = pm[:, :, :].rearrange("p t k -> p (t k)")
            d4, inner, chunk_of, thr, t1, cnt, rank, dcol = (pmf[:, k * T:(k + 1) * T] for k in range(8))
            row = small[:, 0:EROW]
            rank_i = small[:, 64:65].bitcast(I32)
            chunk_at = small[:, 66:67]
            KEY = 4096.0

            @block.gpsimd
            def _(e):
                flag = e.value_load(unsorted[0:1, 0:1], min_val=0, max_val=1)
                with e.If(flag > 0):
                    e.iota(work[:, CE:CE + T].bitcast(I32), pattern=[[0, CH], [P, J]], base=0, channel_multiplier=1).then_inc(s_i, 1)
                    e.iota(work[:, CE + T:CE + 2 * T].bitcast(I32), pattern=[[1, CH], [0, J]], base=0, channel_multiplier=0).then_inc(s_i, 1)
                    e.iota(place.bitcast(I32), pattern=[[1, CE]], base=0, channel_multiplier=0).then_inc(s_i, 1)
                    with e.Fori(0, T) as t:
                        e.wait_ge(s_idx, t + 1)
                        e.tensor_tensor(gate[:, 0:1], ones[:, 0:1], ones[:, 0:1], ALU.add).then_inc(s_gate, 1)
                        e.indirect_dma_start(out=edge_rows[:, :], out_offset=bass.IndirectOffsetOnAxis(ap=rank_i, axis=0),
                                             in_=row, in_offset=None).then_inc(s_put, 16)

            @block.vector
            def _(e):
                v = nc.vector
                flag = e.value_load(unsorted[0:1, 0:1], min_val=0, max_val=1)
                with e.If(flag > 0):
                    ch = Chain(e, s_th)
                    e.wait_ge(s_i, 3)
                    ch.link(v.tensor_copy(inner, work[:, CE:CE + T].bitcast(I32)))
                    ch.link(v.tensor_copy(chunk_of, work[:, CE + T:CE + 2 * T].bitcast(I32)))
                    ch.link(v.tensor_copy(place, place.bitcast(I32)))
                    ch.link(v.memset(rank, 0.0))
                    ch.link(v.memset(row, 0.0))
                    ch.link(v.memset(chunk_at, 0.0))
                    e.wait_ge(s_st, 16)
                    ch.link(v.tensor_scalar(d4, dcol.bitcast(I32), KEY, None, ALU.mult))
                    with e.Fori(0, CH) as c:
                        ch.enter(c, 0, 9)
                        e.wait_ge(s_k, 16 * c + 16)
                        ch.link(v.tensor_scalar(key, key_i, KEY, None, ALU.mult))
                        ch.link(v.tensor_tensor(key, key, place, ALU.add))
                        ch.link(v.tensor_scalar(t1, chunk_of, chunk_at, KEY - 1, ALU.is_gt, ALU.mult))
                        ch.link(v.tensor_tensor(thr, d4, t1, ALU.add))
                        ch.link(v.scalar_tensor_tensor(t1, chunk_of, chunk_at, inner, ALU.is_equal, ALU.mult))
                        ch.link(v.tensor_tensor(thr, thr, t1, ALU.add))
                        ch.mark(v.memset(small[:, 67:68], 0.0))
                        with e.Fori(0, T) as t:
                            v.tensor_scalar(less, key, thr[:, bass.ds(t, 1)], None, ALU.is_lt).then_inc(s_cmp, 1)
                            e.wait_ge(s_cmp, c * (2 * T) + 2 * t + 1)
                            v.tensor_reduce(cnt[:, bass.ds(t, 1)], less, AX.X, ALU.add).then_inc(s_cmp, 1)
                            e.wait_ge(s_cmp, c * (2 * T) + 2 * t + 2)
                        ch.link(v.tensor_tensor(rank, rank, cnt, ALU.add))
                        ch.link(v.tensor_scalar(chunk_at, chunk_at, 1.0, None, ALU.add))
                        ch.leave(CH)
                    e.wait_ge(s_row, 64)
                    v.tensor_copy(rank_i, rank[:, 0:1]).then_inc(s_idx, 1)
                    with e.Fori(1, T) as t:
                        e.wait_ge(s_gate, t)
                        e.wait_ge(s_row, 64 * t + 64)
                        v.tensor_copy(rank_i, rank[:, bass.ds(t, 1)]).then_inc(s_idx, 1)

            @block.sync
            def _(e):
                flag = e.value_load(unsorted[0:1, 0:1], min_val=0, max_val=1)
                with e.If(flag > 0):
                    e.wait_ge(s_attr4, 16)
                    e.wait_ge(s_attr32, 16)
                    e.dma_start(dcol.bitcast(I32), dst_pad[1:EP + 1].rearrange("(t p) -> p t", p=P)).then_inc(s_st, 16)
                    e.wait_ge(s_st, 16)
                    chunks = dst_pad[1:EP + 1].rearrange("(c n) -> c n", n=CE)
                    with e.Fori(0, CH) as c:
                        e.wait_ge(s_th, c * 9 + 7)
                        e.dma_start(key_i, chunks[bass.ds(c, 1), :].rearrange("a n -> (a n)").partition_broadcast(P)).then_inc(s_k, 16)
                    tiles = dst_pad[1:EP + 1].rearrange("(t p a) -> t p a", p=P, a=1)
                    srcs = src_pad.rearrange("(t p a) -> t p a", p=P, a=1)
                    e.wait_ge(s_th, 7 + 9 * CH)
                    attr4, attr32 = ea4_pad.rearrange("(t p) k -> t p k", p=P), ea32_pad.rearrange("(t p) k -> t p k", p=P)

                    def load_row(t):
                        for lo, hi, a in ((0, 1, tiles), (1, 2, srcs), (2, 6, attr4), (6, 6 + C, attr32)):
                            to = row[:, lo:hi].bitcast(I32) if hi <= 2 else row[:, lo:hi]
                            at = bass.ds(t, 1) if not isinstance(t, int) else slice(t, t + 1)
                            e.dma_start(to, a[at].rearrange("t p a -> (t p) a")).then_inc(s_row, 16)
                    load_row(0)
                    with e.Fori(1, T) as t:
                        e.wait_ge(s_put, 16 * t)
                        load_row(t)
                    e.wait_ge(s_put, 16 * T)
                    rows_i = edge_rows.bitcast(I32)
                    n = 0
                    for o in range(0, EP, CE):
                        e.dma_start(dst_pad[1 + o:1 + o + CE].rearrange("(n a) -> n a", a=1), rows_i[o:o + CE, 0:1]).then_inc(s_back, 16)
                        e.dma_start(src_pad[o:o + CE].rearrange("(n a) -> n a", a=1), rows_i[o:o + CE, 1:2]).then_inc(s_back, 16)
                        e.dma_start(ea4_pad[o:o + CE, :], edge_rows[o:o + CE, 2:6]).then_inc(s_back, 16)
                        e.dma_start(ea32_pad[o:o + CE, :], edge_rows[o:o + CE, 6:6 + C]).then_inc(s_back, 16)
                        n += 4
                    e.wait_ge(s_back, 16 * n)

        TR = T // 4
        aside = work[:, 7624:8024]
        with Phase() as ph:
            s_in, s_t, s_c, s_w, s_rep = (ph.sem(n) for n in ("lists_in", "lists_turned", "dve_step", "walk_out", "dst_in"))
            s_conv, s_same, s_same_out, s_e, s_ea4, s_t4 = (ph.sem(n) for n in (
                "lists_float", "same_set", "same_out", "places", "attr4_in", "attr4_turned"))
            same = xsr[:, 0:CE // MW + 1, :].rearrange("p a b -> p (a b)")[:, 0:CE // 2 + 1].bitcast(BF16)[:, 0:CE + 1]
            block = ph.block()
            rows = [logit[0:TR, k * 512:(k + 1) * 512] for k in range(3)] + [work[0:TR, 6600:7112]]
            rowsf = [logit[0:TR, (3 + k) * 512:(4 + k) * 512] for k in range(3)] + [work[0:TR, 7112:7624]]
            before = small[:, 404:404 + T]
            rows4 = work[0:TR, 11400:11400 + 2048]
            rep = work[:, 0:CE + 2].bitcast(I32)
            repf = work[:, CE + 2:2 * CE + 4]
            lastd = aside[:, 0:NS].bitcast(I32)
            key = aside[:, 128:128 + NS]
            cmpk = aside[:, 256:256 + NS]
            tk = aside[:, 384:388]

            @block.sync
            def _(e):
                for k, a in enumerate((src_pad[0:EP], dst_pad[1:EP + 1], dst_pad[2:EP + 2], dst_pad[0:EP])):
                    e.dma_start(rows[k].bitcast(I32), a.rearrange("(p n) -> p n", n=512)).then_inc(s_in, 16)
                e.dma_start(lastd, row_bcast(dst_pad[1:EP + 1].rearrange("(s n) -> s n", n=ST * P)[:, ST * P - 1]),).then_inc(s_in, 16)
                for c in range(CH):
                    e.dma_start(rep[c * H:(c + 1) * H, :], row_bcast(dst_pad[c * CE:(c + 1) * CE + 2], H)).then_inc(s_rep, 16)
                e.dma_start(start_dst[:, :], dst_pad[1:EP + 1].rearrange("(c n) -> c n", c=CH)[:, 0:1]).then_inc(s_ea4, 16)
                e.wait_ge(s_attr4, 16)
                e.dma_start(rows4, ea4_pad.rearrange("(r q) k -> r (q k)", q=512)).then_inc(s_ea4, 16)
                e.wait_ge(s_w, 1)
                e.dma_start(walk_d.rearrange("a p -> p a"), tk[:, 0:2]).then_inc(s_w, 16)
                e.dma_start(pens_d, small[:, 400:402]).then_inc(s_w, 16)
                e.wait_ge(s_w, 33)
                e.dma_start(pm[0:1, 0:8, :].rearrange("p a b -> p (a b)"), walk_d[0:1, :]).then_inc(s_w, 16)
                e.dma_start(pm[0:1, 8:16, :].rearrange("p a b -> p (a b)"), walk_d[1:2, :]).then_inc(s_w, 16)
                e.dma_start(base128[:, :], row_bcast(walk_d[1, :])).then_inc(s_w, 16)
                for k in range(2):
                    e.dma_start(pens[:, k, :], pens_d[:, k].rearrange("(c h) -> h c", h=H)).then_inc(s_w, 16)
                e.wait_ge(s_w, 33 + 80)

            place_i = pm[:, 100:100 + T // (2 * H), :].rearrange("p a b -> p (a b)").bitcast(I32)
            place = pm[:, 200:200 + T // (2 * H), :].rearrange("p a b -> p (a b)")

            @block.gpsimd
            def _(e):
                e.iota(place_i, pattern=[[P, T]], base=0, channel_multiplier=1).then_inc(s_e, 1)

            @block.scalar
            def _(e):
                e.wait_ge(s_same, 1)
                e.dma_start(same_d, same[0:P:H, 0:CE]).then_inc(s_same_out, 16)
                for b in range(4):
                    e.wait_ge(s_t4, b + 1)
                    nc.scalar.activation(ea4[:, :, :].rearrange("p (r b) k -> p b k r", b=4)[:, b, :, :],
                                         ps[:, 4 + b, 0:4 * TR].rearrange("p (k r) -> p k r", k=4), ACT.Copy)

            @block.vector
            def _(e):
                v = nc.vector
                ch = Chain(e, s_c)
                e.wait_ge(s_in, 80)
                for k in range(4):
                    ch.link(v.tensor_copy(rowsf[k], rows[k].bitcast(I32)))
                v.memset(small[:, 1000:1001], 0.0).then_inc(s_conv, 1)
                ch.link(v.tensor_scalar(lastd, lastd, 7, None, ALU.arith_shift_right))
                ch.link(v.tensor_copy(key, lastd))
                ch.link(v.tensor_tensor(key, key, iota_f[:, 0:NS], ALU.add))
                ch.link(v.tensor_scalar(cmpk, key, part_f[:, 0:1], None, ALU.is_lt))
                ch.link(v.tensor_reduce(tk[:, 2:3], cmpk, AX.X, ALU.add))
                ch.link(v.tensor_scalar(tk[:, 0:1], tk[:, 2:3], float(ST), None, ALU.mult))
                ch.link(v.tensor_tensor(tk[:, 1:2], part_f[:, 0:1], tk[:, 2:3], ALU.subtract))
                e.wait_ge(s_rep, 16 * CH)
                ch.link(v.tensor_copy(repf, rep))
                ch.mark(v.tensor_tensor(small[:, 400:401], repf[:, 0:1], repf[:, CE:CE + 1], ALU.not_equal))
                ch.mark(v.tensor_tensor(small[:, 401:402], repf[:, 1:2], repf[:, CE + 1:CE + 2], ALU.not_equal))
                ch.link(v.tensor_tensor(same, repf[:, 1:CE + 2], repf[:, 0:CE + 1], ALU.is_equal))
                ch.mark(v.tensor_scalar(small[:, 400:402], small[:, 400:402], -BIG, None, ALU.mult))
                ch.link(v.tensor_scalar(pen[:, :], same, BIG, -BIG, ALU.mult, ALU.add))
                v.memset(same[:, 0:1], 0.0).then_inc(s_same, 1)
                v.memset(small[:, 1001:1002], 0.0).then_inc(s_w, 1)
                e.wait_ge(s_t, 4)
                for k, o in enumerate((srcf, dstf, lastf, before)):
                    ch.link(v.tensor_copy(o[:, :].rearrange("p (a b) -> p b a", b=4),
                                          psf[:, k * 512:k * 512 + 4 * TR].rearrange("p (b a) -> p b a", b=4)))
                ch.link(v.tensor_tensor(lastf[:, :], lastf[:, :], dstf[:, :], ALU.not_equal))
                e.wait_ge(s_same_out, 16)
                e.wait_ge(s_e, 1)
                ch.link(v.tensor_copy(xsr[:, :, C], lastf[:, :]))
                ch.link(v.tensor_tensor(before, before, dstf[:, :], ALU.not_equal))
                ch.link(v.tensor_copy(place, place_i))
                ch.link(v.tensor_tensor(xsr[:, :, C + 1], before, place, ALU.mult))
                e.wait_ge(s_w, 33 + 80)
                ch.link(v.tensor_copy(walk_t[:, :], pm[0:1, 0:8, :].rearrange("p a b -> p (a b)")))
                ch.link(v.tensor_copy(walk_b[:, :], pm[0:1, 8:16, :].rearrange("p a b -> p (a b)")))
                ch.link(v.tensor_scalar(base128[:, :], base128[:, :], float(P), None, ALU.mult))

            @block.tensor
            def _(e):
                e.wait_ge(s_conv, 1)
                for k in range(4):
                    for b in range(4):
                        last = nc.tensor.transpose(psf[:, k * 512 + b * TR:k * 512 + (b + 1) * TR],
                                                   rowsf[k][:, b * P:(b + 1) * P], ident[0:TR, 0:TR])
                    last.then_inc(s_t, 1)
                e.wait_ge(s_ea4, 32)
                for b in range(4):
                    for k in range(4):
                        last = nc.tensor.transpose(ps[:, 4 + b, k * TR:(k + 1) * TR],
                                                   rows4[:, 4 * b * P + k:4 * (b + 1) * P:4], ident[0:TR, 0:TR])
                    last.then_inc(s_t4, 1)

        def layer_norm_relu(src, dst):
            with Phase() as ph:
                s_c, s_q = ph.sem("dve_step"), ph.sem("root")
                block = ph.block()

                @block.vector
                def _(e):
                    layer_norm_steps(e, Chain(e, s_c), s_q, src, dst)

                @block.scalar
                def _(e):
                    e.wait_ge(s_c, VARIANCE_STEP)
                    nc.scalar.activation(var_at, var_at, ACT.Sqrt).then_inc(s_q, 1)

        def turn_features():
            with Phase() as ph:
                s_t = ph.sem("turned")
                s_e = ph.sem("copied")
                block = ph.block()
                groups = [(g, min(4, NB - g)) for g in range(0, NB, 4)]

                @block.vector
                def _(e):
                    nc.vector.memset(featT[C:C + 1, :], 1.0)

                @block.tensor
                def _(e):
                    for g, w in groups:
                        for b in range(w):
                            last = nc.tensor.transpose(ps[0:C, g // 4, b * P:(b + 1) * P], feat[:, g + b, :], ident[:, :])
                        last.then_inc(s_t, 1)

                @block.scalar
                def _(e):
                    for g, w in groups:
                        e.wait_ge(s_t, g // 4 + 1)
                        nc.scalar.activation(featT[0:C, g * P:(g + w) * P], ps[0:C, g // 4, 0:w * P], ACT.Copy).then_inc(s_e, 1)

        def by_chunk(a):
            return a.rearrange("p (c j) -> p j c", j=J)

        src_jc = by_chunk(srcf[:, :])
        src_next = by_chunk(src_all[:, 2:T + 2])

        def ring_place(c):
            return 4 * (c % 4) + c // 4

        def gather_program(e, s_ready, s_gath, s_gate, s_last=None):

            def window(par, need, padding=False):
                e.wait_ge(s_ready[par], need)
                e.tensor_tensor(gate[:, par:par + 1], ones[:, 0:1], ones[:, 0:1], ALU.add).then_inc(s_gate, 1)
                chunks = list(range(CH)) if s_last is None else [CH - 1] * (not padding) + list(range(CH - 1))
                for c in chunks:
                    sem = s_last if s_last is not None and c == CH - 1 else s_gath
                    e.indirect_dma_start(
                        out=ring[:, par, ring_place(c), 0:C], out_offset=None, in_=table[:, :],
                        in_offset=bass.IndirectOffsetOnAxis(ap=stage[:, par, c:c + 1], axis=0)).then_inc(sem[par], GATHER)
            window(0, 1)
            window(1, 1)
            real = J // 2 if s_last is None else PAD_WINDOW // 2
            with e.Fori(1, real) as i:
                window(0, i + 1)
                window(1, i + 1)
            if s_last is not None:
                with e.Fori(real, J // 2) as i:
                    window(0, i + 1, padding=True)
                    window(1, i + 1, padding=True)
            window(0, J // 2 + 1, padding=True)

        def pairs(e, body, chains=(), late=None):
            body(0, 0, 0)
            body(1, 1, 0)
            with e.Fori(1, PAD_WINDOW // 2 if late else J // 2) as i:
                for ch, per in chains:
                    ch.enter(i, 1, per)
                body(2 * i, 0, i)
                body(2 * i + 1, 1, i)
                for ch, per in chains:
                    ch.leave(J // 2 - 1)
            if late:
                with e.Fori(PAD_WINDOW // 2, J // 2) as i:
                    late(2 * i, 0, i)
                    late(2 * i + 1, 1, i)
            (late or body)(J - 1, 0, J // 2)

        def first(x):
            return isinstance(x, int)

        def wait(e, sem, x):
            if not (isinstance(x, int) and x <= 0):
                e.wait_ge(sem, x)

        with Phase() as ph:
            GW = CH * GATHER
            s_ready = [ph.sem("staged0"), ph.sem("staged1")]
            s_gath = [ph.sem("gathered0"), ph.sem("gathered1")]
            s_gate = ph.sem("gate_passed")
            s_ea = [ph.sem("attr0"), ph.sem("attr1")]
            s_t, s_tc, s_h, s_hr, s_w, s_pr, s_c, s_red, s_xc, s_cf, s_ones = (ph.sem(n) for n in (
                "attr_turned", "attr_copied", "hidden", "hidden_relu", "weights", "products", "dve_step", "reduced",
                "rows_copied", "coefficients", "ones_set"))
            block = ph.block()

            @block.gpsimd
            def _(e):
                gather_program(e, s_ready, s_gath, s_gate)

            @block.sync
            def _(e):
                ea_v = ea32_pad.rearrange("(c j p) k -> j p c k", c=CH, p=P)
                e.wait_ge(s_attr32, 16)

                def window(j, par, i):
                    wait(e, s_t, 4 * j - 4 if not first(j) or j >= 2 else 0)
                    e.dma_start(EA[:, par, :, :], ea32_rows(j)).then_inc(s_ea[par], 16)

                def ea32_rows(j):
                    if first(j):
                        return ea_v[j]
                    return ea_v[bass.ds(j, 1)].rearrange("a p c k -> (a p) c k")
                pairs(e, window)

            @block.tensor
            def _(e):
                def turn(j, par, i, g):
                    if g == 0:
                        e.wait_ge(s_ea[par], 16 * i + 16)
                    wait(e, s_tc, 4 * j + g - 1)
                    nc.tensor.transpose(ps[:, g % 2, 0:P], EA[:, par, 4 * g:4 * g + 4, :].rearrange("p c k -> p (c k)"),
                                        ident[:, :]).then_inc(s_t, 1)

                def hidden(j, g):
                    e.wait_ge(s_tc, 4 * j + g + 1)
                    wait(e, s_hr, 4 * j + g - 1)
                    for k in range(4):
                        last = nc.tensor.matmul(ps[0:MLP, 2 + g % 2, k * P:(k + 1) * P], w1_sb[:, k, :],
                                                EAT[:, g % 2, :], start=True, stop=True)
                    last.then_inc(s_h, 1)

                def weights(j, g):
                    e.wait_ge(s_hr, 4 * j + g + 1)
                    wait(e, s_pr, 4 * j + g - 1)
                    for k in range(4):
                        last = nc.tensor.matmul(ps[:, 4 + 2 * (g % 2) + k // 2, (k % 2) * HC:(k % 2 + 1) * HC],
                                                H1T[:, g % 2, k * P:(k + 1) * P], w2_sb[:, :], start=True, stop=True)
                    last.then_inc(s_w, 1)

                def window(j, par, i):
                    for g in range(4):
                        last = first(j) and j == J - 1
                        if g < 2:
                            turn(j, par, i, g + 2)
                        elif not last:
                            turn(j + 1, 1 - par, i + par, g - 2)
                        if g < 3:
                            hidden(j, g + 1)
                        elif not last:
                            hidden(j + 1, 0)
                        weights(j, g)
                e.wait_ge(s_ones, 1)
                turn(0, 0, 0, 0)
                turn(0, 0, 0, 1)
                hidden(0, 0)
                pairs(e, window)

            @block.scalar
            def _(e):
                def window(j, par, i):
                    for g in range(4):
                        e.wait_ge(s_t, 4 * j + g + 1)
                        wait(e, s_h, 4 * j + g - 1)
                        nc.scalar.activation(EAT[:, g % 2, :], ps[:, g % 2, 0:P], ACT.Copy).then_inc(s_tc, 1)
                        e.wait_ge(s_h, 4 * j + g + 1)
                        wait(e, s_w, 4 * j + g - 1)
                        nc.scalar.activation(H1T[0:MLP, g % 2, :], ps[0:MLP, 2 + g % 2, :], ACT.Relu,
                                             bias=b1_sb[:, :]).then_inc(s_hr, 1)
                        if g == 1:
                            e.wait_ge(s_gath[par], GW * i + GW)
                            wait(e, s_cf, j - 1)
                            wait(e, s_pr, 4 * j - 4)
                            for q in range(4):
                                nc.scalar.activation(XC[:, par, 4 * q:4 * q + 4, :], ring[:, par, q:CH:4, 0:C], ACT.Copy).then_inc(s_xc, 1)
                            e.wait_ge(s_xc, 5 * j + 4)
                            nc.scalar.activation(COEF[:, par, :, 2, :], XC[:, par, :, 0:MUL], ACT.Copy).then_inc(s_xc, 1)
                pairs(e, window)

            @block.vector
            def _(e):
                v = nc.vector
                ch = Chain(e, s_c)
                v.memset(H1T[MLP:MLP + 1, :, :], 1.0).then_inc(s_ones, 1)
                for par in range(2):
                    v.tensor_copy(stage[:, par, 0:CH], src_jc[:, par, :]).then_inc(s_ready[par], 1)

                def window(j, par, i):
                    at = bass.ds(j, 1) if not first(j) else slice(j, j + 1)
                    sh = ea4[:, :, :].rearrange("p (c j) k -> p j c k", j=J)[:, at, :, :].rearrange("p a c k -> p (a c) k")
                    sh1 = sh[:, :, None, 1:4].to_broadcast([P, CH, MUL, 3])
                    cf = COEF[:, par, :, :, :]
                    e.wait_ge(s_xc, 5 * j + 5)
                    xv = XC[:, par, :, MUL:C].rearrange("p c (i m) -> p c i m", m=3)
                    done = ch.value()
                    ch.mark(v.tensor_tensor(cf[:, :, 0, :], XC[:, par, :, 0:MUL], sh[:, :, 0:1].to_broadcast([P, CH, MUL]), ALU.mult))
                    wait(e, s_c, done)
                    terms = ch.mark(v.tensor_tensor(TMP[:, :, :, :], xv, sh1, ALU.mult))
                    ch.mark(v.tensor_tensor(cf[:, :, 3:6, :], xv.rearrange("p c i m -> p c m i"),
                                            sh[:, :, 0:1, None].to_broadcast([P, CH, 3, MUL]), ALU.mult))
                    e.wait_ge(s_c, terms)
                    ch.link(v.tensor_reduce(cf[:, :, 1, :], TMP[:, :, :, :], AX.X, ALU.add))
                    if not (first(j) and j + 2 >= J):
                        e.wait_ge(s_gate, j + 1)
                        v.tensor_copy(stage[:, par, 0:CH], src_next[:, at, :].rearrange("p a c -> p (a c)")).then_inc(s_ready[par], 1)
                    def products(g):
                        e.wait_ge(s_w, 4 * j + g + 1)
                        if g == 3:
                            e.wait_ge(s_red, 4 * j + 1)
                        W = ps[:, 4 + 2 * (g % 2):6 + 2 * (g % 2), :].rearrange("p a (t r) -> p (a t) r", t=2)
                        pr = PROD[:, g % 3, :, :]
                        c4 = cf[:, 4 * g:4 * g + 4, :, :].rearrange("p t r i -> p t (r i)")
                        first_three = v.tensor_tensor(pr[:, :, 0:192].rearrange("p t (k o) -> p t k o", o=MUL),
                                                      W[:, :, 0:192].rearrange("p t (k o) -> p t k o", o=MUL),
                                                      c4[:, :, 0:24, None].to_broadcast([P, 4, 24, MUL]), ALU.mult)
                        if g == 0:
                            first_three.then_inc(s_cf, 1)
                        for m in range(3):
                            last = v.tensor_tensor(pr[:, :, 192 + 64 * m:256 + 64 * m].rearrange("p t (k o) -> p t k o", o=MUL),
                                                   W[:, :, 192:256].rearrange("p t (k o) -> p t k o", o=MUL),
                                                   c4[:, :, 24 + 8 * m:32 + 8 * m, None].to_broadcast([P, 4, MUL, MUL]), ALU.mult)
                        last.then_inc(s_pr, 1)

                    def sums(g):
                        e.wait_ge(s_pr, 4 * j + g + 1)
                        v.tensor_reduce(RED[:, 4 * g:4 * g + 4, :, :].rearrange("p t r o -> p (t r) o"),
                                        PROD[:, g % 3, :, :].rearrange("p t (r i o) -> p (t r) o i", i=MUL, o=MUL), AX.X, ALU.add).then_inc(s_red, 1)
                    products(0)
                    for g in range(1, 4):
                        products(g)
                        sums(g - 1)
                    sums(3)
                    e.wait_ge(s_red, 4 * j + 4)
                    msg = xsr[:, :, :].rearrange("p (c j) k -> p j c k", j=J)[:, at, :, :].rearrange("p a c k -> p (a c) k")
                    terms = ch.mark(v.tensor_tensor(TMP[:, :, :, :], RED[:, :, 2, :, None].to_broadcast([P, CH, MUL, 3]), sh1, ALU.mult))
                    ch.mark(v.tensor_tensor(msg[:, :, 0:MUL], RED[:, :, 0, :], RED[:, :, 1, :], ALU.add))
                    e.wait_ge(s_c, terms)
                    ch.mark(v.tensor_tensor(msg[:, :, MUL:C].rearrange("p c (o m) -> p c o m", m=3), TMP[:, :, :, :],
                                            RED[:, :, 3:6, :].rearrange("p c m o -> p c o m"), ALU.add))

                pairs(e, window, [(ch, 2 * 7)])

        def walk(table, k, n, most):
            at = slice(k, k + n) if first(k) else bass.ds(k, n)
            return list(nc.values_load_multi_w_load_instructions(
                table[0:1, at], engines=(mybir.EngineType.DVE,), min_val=0, max_val=most,
                skip_runtime_bounds_check_because="the walk is made on the chip and ends at the last tile and block")[1])

        def load_edge_weights(e, l, sem):
            Wl, Wr, bl, br = (A["L1_gnn_" + n][l] for n in ("Wl", "Wr", "bl", "br"))
            att = A["L1_gnn_att"][l].rearrange("h c -> (h c)")
            loads = [(wst[k * C:(k + 1) * C, :], w) for k, w in enumerate((Wl, Wr, Wl, Wr))]
            for to, w, b in ((wl_aug, Wl, bl), (wr_aug, Wr, br)):
                loads += [(to[0:C, :], w), (to[C:C + 1, :], b.rearrange("(a n) -> a n", a=1))]
            loads += [(attb[:, :], row_bcast(att)), (attc[:, :], att.rearrange("(k p) -> p k", p=P)),
                      (bz[:, 0:2], bl.rearrange("(k p) -> p k", p=P)), (bz[:, 2:4], br.rearrange("(k p) -> p k", p=P))]
            for to, a in loads:
                e.dma_start(to, a).then_inc(sem, 16)
            return len(loads)

        def load_node_weights(e, l, sem):
            Wl = A["L1_gnn_Wl"][l]
            loads = [(wlr[(h % 4) * C:(h % 4 + 1) * C, h // 4, :], Wl[:, h * C:(h + 1) * C]) for h in range(H)]
            loads.append((vecs[:, 0, :], row_bcast(A["L1_gnn_bl"][l])))
            loads += [(vecs[:, 1 + k, 0:C], row_bcast(A["L1_gnn_" + n][l])) for k, n in enumerate(("conv_bias", "bn_gamma", "bn_beta"))]
            for to, a in loads:
                e.dma_start(to, a).then_inc(sem, 16)
            return len(loads)

        def segment_sums(width, edge_values, layer, on_dve=0, turned=False):
            with Phase() as ph:
                s_v, s_o, s_mm, s_acc, s_ap, s_in = (ph.sem(n) for n in ("values", "selected", "sums", "added", "apart", "weights_in"))
                block = ph.block()
                s_zero = ph.sem("zeroed")
                on_act = ST - on_dve
                zeros = pm[:, 0:T // 4, :].rearrange("p t k -> p (t k)")

                @block.gpsimd
                def _(e):
                    if layer < 0:
                        e.memset(zeros, 0.0)
                    e.memset(accT[:, :, :] if turned else acc[:, :, :], 0.0).then_inc(s_zero, 1)

                @block.sync
                def _(e):
                    n = 0
                    if layer < 0:
                        e.wait_ge(s_zero, 1)
                        parts = T * C // zeros.shape[-1]
                        rows = first_rows[0:EP, :].rearrange("(p k t) c -> p k (t c)", p=P, k=parts)
                        for k in range(parts):
                            e.dma_start(rows[:, k, :], zeros).then_inc(s_in, 16)
                        n += parts
                    if layer >= 0:
                        n += load_node_weights(e, layer, s_in)
                    if layer + 1 < L:
                        n += load_edge_weights(e, layer + 1, s_in)
                    e.wait_ge(s_in, 16 * n)

                @block.vector
                def _(e):
                    v = nc.vector

                    def make(k, slot, t4):
                        if on_dve:
                            item = slice(k, k + 1) if first(k) else bass.ds(k, 1)
                            v.tensor_tensor(apart[:, item, :].rearrange("p a t -> p (a t)"), base128[:, item].to_broadcast([P, ST]),
                                            dstf[:, bass.ds(t4, ST)], ALU.subtract).then_inc(s_ap, 1)
                        wait(e, s_mm, k - SLOTS + 1)
                        if on_dve:
                            e.wait_ge(s_ap, k + 1)
                            for t in range(on_act, ST):
                                v.tensor_scalar(slotO[:, slot, t, :], iota_f[:, :], apart[:, item, t:t + 1].rearrange("p a t -> p (a t)"),
                                                0.0, ALU.add, ALU.is_equal)
                        edge_values(v, slot, t4).then_inc(s_v, 1)

                    def add(k, slot, b):
                        e.wait_ge(s_mm, k + 1)
                        if first(k) and k == 0:
                            e.wait_ge(s_zero, 1)
                        wait(e, s_acc, k)
                        if turned:
                            row = accT[:, bass.ds(b, 1), :].rearrange("w a n -> w (a n)")
                            v.tensor_tensor(row, row, ps[0:width, slot, 0:P], ALU.add).then_inc(s_acc, 1)
                        else:
                            row = acc[:, bass.ds(b, 1), 0:width].rearrange("p a w -> p (a w)")
                            v.tensor_tensor(row, row, ps[:, slot, 0:width], ALU.add).then_inc(s_acc, 1)

                    def round_of(k, before, n=4):
                        t4 = walk(walk_t, k, n, T - ST)
                        b = walk(walk_b, k - 2, n, NB - 1) if before else [None, None] + walk(walk_b, k, 2, NB - 1)
                        for u in range(n):
                            make(k + u, u, t4[u])
                            if b[u] is not None:
                                add(k + u - 2, (u - 2) % 4, b[u])
                    round_of(0, False)
                    with e.Fori(1, ROUNDS) as i:
                        round_of(4 * i, True)
                    if ITEMS % 4:
                        round_of(4 * ROUNDS, True, ITEMS % 4)
                    for u, b in enumerate(walk(walk_b, ITEMS - 2, 2, NB - 1)):
                        add(ITEMS - 2 + u, (ITEMS - 2 + u) % 4, b)

                @block.scalar
                def _(e):
                    def select(k, slot):
                        wait(e, s_mm, k - SLOTS + 1)
                        item = slice(k, k + 1) if first(k) else bass.ds(k, 1)
                        if on_dve:
                            e.wait_ge(s_ap, k + 1)
                        for t in range(on_act):
                            nc.scalar.activation(slotO[:, slot, t, :], iota_f[:, :], ACT.Abs,
                                                 bias=apart[:, item, t:t + 1].rearrange("p a t -> p (a t)")).then_inc(s_o, 1)
                        e.wait_ge(s_o, k * (on_act + 1) + on_act)
                        nc.scalar.activation(slotO[:, slot, 0:on_act, :], slotO[:, slot, 0:on_act, :], ACT.Relu, scale=-1.0, bias=1.0).then_inc(s_o, 1)
                    for k in range(4):
                        select(k, k)
                    with e.Fori(1, ROUNDS) as i:
                        for u in range(4):
                            select(4 * i + u, u)
                    for k in range(4 * ROUNDS, ITEMS):
                        select(k, k % 4)

                @block.tensor
                def _(e):
                    def item(k, slot):
                        e.wait_ge(s_v, k + 1)
                        e.wait_ge(s_o, (k + 1) * (on_act + 1))
                        wait(e, s_acc, k - SLOTS + 1)
                        for t in range(ST):
                            select, values = slotO[:, slot, t, :], slotV[:, slot, t, 0:width]
                            if turned:
                                last = nc.tensor.matmul(ps[0:width, slot, 0:P], values, select, start=(t == 0), stop=(t == ST - 1))
                            else:
                                last = nc.tensor.matmul(ps[:, slot, 0:width], select, values, start=(t == 0), stop=(t == ST - 1))
                        last.then_inc(s_mm, 1)
                    for k in range(4):
                        item(k, k)
                    with e.Fori(1, ROUNDS) as i:
                        for u in range(4):
                            item(4 * i + u, u)
                    for k in range(4 * ROUNDS, ITEMS):
                        item(k, k % 4)

        def message_values(v, slot, t4):
            return v.tensor_copy(slotV[:, slot, :, 0:MW], xsr[:, bass.ds(t4, ST), :])

        segment_sums(MW, message_values, -1, on_dve=1, turned=True)
        turn_features()

        with Phase() as ph:
            s_m, s_c = ph.sem("self"), ph.sem("dve_step")
            s_w = ph.sem("scaled")
            s_i, s_b = ph.sem("own_rows"), ph.sem("sums_turned")
            block = ph.block()

            @block.gpsimd
            def _(e):
                e.iota(small[:, 64:64 + NB].bitcast(I32), pattern=[[P, NB]], base=EP, channel_multiplier=1).then_inc(s_i, 1)

            def sums(lo, hi):
                return [(a, b, psf[:, 1024 + (a // 15) * 512:][:, 0:(b - a) * MW].rearrange("p (b w) -> p b w", w=MW)[:, :, lo:hi])
                        for a, b in ((0, 15), (15, NB))]

            @block.vector
            def _(e):
                v = nc.vector
                ch = Chain(e, s_c)
                e.wait_ge(s_i, 1)
                v.tensor_scalar(siw[:, :], siw[:, :], SI, None, ALU.mult).then_inc(s_w, 1)
                e.wait_ge(s_b, 1)
                for a, b, z in sums(C, C + 2):
                    ch.mark(v.tensor_copy(count[:, a:b], z[:, :, 0]))
                    ch.mark(v.tensor_copy(small[:, 96 + a:96 + b], z[:, :, 1]))
                ch.link(v.tensor_copy(small[:, 32:32 + NB], small[:, 64:64 + NB].bitcast(I32)))
                ch.link(v.tensor_scalar(small[:, 0:NB], count[:, :], -1.0, -1.0, ALU.add, ALU.mult))
                ch.link(v.tensor_tensor(small[:, 0:NB], small[:, 0:NB], small[:, 32:32 + NB], ALU.mult))
                ch.link(v.tensor_tensor(small[:, 0:NB], small[:, 0:NB], small[:, 96:96 + NB], ALU.add))
                ch.link(v.tensor_tensor(small[:, 0:NB], small[:, 0:NB], small[:, 32:32 + NB], ALU.min))
                ch.link(v.tensor_copy(first_at[:, :], small[:, 0:NB]))
                for a, b, z in sums(0, C):
                    ch.link(v.tensor_tensor(xres[:, a:b, :], xres[:, a:b, :], z, ALU.add))
                e.wait_ge(s_m, 1)
                ch.link(v.tensor_tensor(xres[:, 0:16, :], xres[:, 0:16, :], ps[:, 0, :].rearrange("p (b c) -> p b c", c=C), ALU.add))
                ch.link(v.tensor_tensor(xres[:, 16:NB, :], xres[:, 16:NB, :],
                                        ps[:, 1, 0:(NB - 16) * C].rearrange("p (b c) -> p b c", c=C), ALU.add))

            @block.tensor
            def _(e):
                for a, b, z in sums(0, MW):
                    for k in range(a, b):
                        last = nc.tensor.transpose(z[:, k - a, :], accT[:, k, :], ident[0:MW, 0:MW])
                last.then_inc(s_b, 1)
                e.wait_ge(s_w, 1)
                for b in range(NB):
                    last = nc.tensor.matmul(psf[:, b * C:(b + 1) * C], featT[0:C, b * P:(b + 1) * P], siw[:, :], start=True, stop=True)
                last.then_inc(s_m, 1)
        layer_norm_relu(xres, feat)

        for l in range(L):
            with Phase() as ph:
                s_f, s_sc, s_init, s_ft, s_fe, s_sz, s_sr, s_se, s_sp, s_sl = (ph.sem(n) for n in (
                    "table_out", "first_rows_put", "weights_set", "features_turned", "features_copied", "self_z",
                    "self_copied", "self_leaky", "self_products", "self_logits"))
                self_z = work[:, 7168:7680].rearrange("p (s n) -> p s n", s=2)
                node_groups = [(g, min(4, NB - g)) for g in range(0, NB, 4)]
                s_ready = [ph.sem("staged0"), ph.sem("staged1")]
                s_gath = [ph.sem("gathered0"), ph.sem("gathered1")]
                s_last = [ph.sem("last_gathered0"), ph.sem("last_gathered1")]
                GW = (CH - 1) * GATHER
                s_v = [ph.sem("first0"), ph.sem("first1")]
                s_gate = ph.sem("gate_passed")
                s_tr, s_xt, s_z, s_r, s_e, s_q, s_xs, s_lge, s_st, s_so, s_c = (ph.sem(n) for n in (
                    "turned", "filled", "z", "z_copied", "leaky", "logits", "src_kept", "logits_out", "start_rows_in",
                    "start_rows_out", "dve_step"))
                block = ph.block()

                @block.gpsimd
                def _(e):
                    for b in range(NB):
                        e.indirect_dma_start(out=first_rows[:, :], out_offset=bass.IndirectOffsetOnAxis(ap=first_at[:, b:b + 1], axis=0),
                                             in_=feat[:, b, :], in_offset=None).then_inc(s_sc, 16)
                    e.wait_ge(s_f, 16)
                    e.indirect_dma_start(out=start_row[:, :], out_offset=None, in_=table[:, :],
                                         in_offset=bass.IndirectOffsetOnAxis(ap=start_dst[:, 0:1], axis=0)).then_inc(s_st, 16)
                    gather_program(e, s_ready, s_gath, s_gate, s_last)

                @block.sync
                def _(e):
                    e.dma_start(table.rearrange("(b p) c -> p b c", p=P), feat[:, :, :]).then_inc(s_f, 16)
                    e.wait_ge(s_sc, 16 * NB)
                    e.wait_ge(s_st, 16)
                    e.dma_start(first_rows[0:EP:CE, :], start_row[:, :]).then_inc(s_so, 16)
                    e.wait_ge(s_so, 16)
                    fr = first_rows[0:EP, :].rearrange("(c j p) r -> j p c r", c=CH, p=P)
                    sd = same_d.rearrange("(r s q) (j e) -> j s q r e", r=2, s=2, e=P)

                    def window(j, par, i, padding=False):
                        wait(e, s_tr, j - 1)
                        wait(e, s_xt, 8 * j - 8)
                        for q in range(4):
                            src = fr[j] if first(j) else fr[bass.ds(j, 1)].rearrange("a p c r -> (a p) c r")
                            e.dma_start(ring[:, par, 4 * q:4 * q + 4, C:], src[:, q:CH:4, :]).then_inc(s_v[par], 16)
                            for s in range(2):
                                if q == 3 and s == 1 and not padding:
                                    e.wait_ge(s_last[par], GATHER * i + GATHER)
                                m = sd[j] if first(j) else sd[bass.ds(j, 1)].rearrange("a s q r e -> (a s) q r e")
                                e.dma_start(SAME[(2 * s + 1) * C:(2 * s + 2) * C, par, 2 * q:2 * q + 2, :],
                                            m[s, q].partition_broadcast(C)).then_inc(s_v[par], 16)

                    def late(j, par, i):
                        window(j, par, i, padding=True)
                    pairs(e, window, late=late)
                VW1 = 12 * 16

                def loaded(e, j, par, i):
                    e.wait_ge(s_v[par], VW1 * i + VW1)

                @block.tensor
                def _(e):
                    def z(j, par, q):
                        wait(e, s_r, 8 * j + 2 * q - 2)
                        e.wait_ge(s_xt, 8 * j + 2 * q + 2)
                        for half in range(2):
                            for side in range(2):
                                last = nc.tensor.matmul(ps[:, 2 + 2 * (q % 2) + side, half * 256:(half + 1) * 256],
                                                        wst[64 * side:64 * side + 64, half * P:(half + 1) * P],
                                                        XT[64 * side:64 * side + 64, par, 2 * q:2 * q + 2, :],
                                                        start=True, stop=True)
                        last.then_inc(s_z, 1)

                    def logits(j, par, q):
                        e.wait_ge(s_e, 4 * j + q + 1)
                        for half in range(2):
                            for g in range(4):
                                last = nc.tensor.matmul(ps[32 * g:32 * g + 32, 6 + par, 0:P], attp[:, half, 32 * q:32 * q + 32],
                                                        RE[:, q, half, (g % 2) * 256 + (g // 2) * P:(g % 2) * 256 + (g // 2) * P + P],
                                                        start=(q == 0 and half == 0), stop=(q == 3 and half == 1), skip_group_check=True)
                        last.then_inc(s_q, 1)

                    def turn(j, par, i):
                        e.wait_ge(s_gath[par], GW * i + GW)
                        loaded(e, j, par, i)
                        wait(e, s_xt, 8 * j)
                        for k in range(8):
                            last = nc.tensor.transpose(psf[:, k * P:(k + 1) * P],
                                                       ring[:, par, 2 * k:2 * k + 2, :].rearrange("p g r -> p (g r)"), ident[:, :])
                        last.then_inc(s_tr, 1)

                    def window(j, par, i):
                        z(j, par, 0)
                        z(j, par, 1)
                        z(j, par, 2)
                        wait(e, s_lge, j - 1)
                        logits(j, par, 0)
                        z(j, par, 3)
                        logits(j, par, 1)
                        if not (first(j) and j == J - 1):
                            turn(j + 1, 1 - par, i + par)
                        logits(j, par, 2)
                        logits(j, par, 3)
                    for g, w in node_groups:
                        for b in range(w):
                            last = nc.tensor.transpose(ps[0:C, g // 4, b * P:(b + 1) * P], feat[:, g + b, :], ident[:, :])
                        last.then_inc(s_ft, 1)
                    e.wait_ge(s_init, 1)
                    for b in range(NB):
                        e.wait_ge(s_fe, max(2, b // 4 + 1))
                        wait(e, s_sr, b - 1)
                        nc.tensor.matmul(ps[:, b % 2, 0:HC], featT[:, b * P:(b + 1) * P], wz[:, :], start=True, stop=True).then_inc(s_sz, 1)
                    e.wait_ge(s_sr, NB)
                    turn(0, 0, 0)
                    pairs(e, window)

                @block.scalar
                def _(e):
                    for g, w in node_groups:
                        e.wait_ge(s_ft, g // 4 + 1)
                        nc.scalar.activation(featT[0:C, g * P:(g + w) * P], ps[0:C, g // 4, 0:w * P], ACT.Copy).then_inc(s_fe, 1)
                    for b in range(NB):
                        e.wait_ge(s_sz, b + 1)
                        wait(e, s_sl, b - 1)
                        nc.scalar.activation(self_z[:, b % 2, :], ps[:, b % 2, 0:HC], ACT.Copy).then_inc(s_sr, 1)

                    def window(j, par, i):
                        at = bass.ds(j, 1) if not first(j) else slice(j, j + 1)
                        e.wait_ge(s_gath[par], GW * i + GW)
                        loaded(e, j, par, i)
                        for g in range(4):
                            kept = xsr[:, 4 * g * J:4 * (g + 1) * J, :].rearrange("p (c j) k -> p j c k", j=J)[:, at, :, 0:C].rearrange("p a c k -> p (a c) k")
                            nc.scalar.activation(kept, ring[:, par, g:CH:4, 0:C], ACT.Copy).then_inc(s_xs, 1)
                        for q in range(4):
                            e.wait_ge(s_z, 4 * j + q + 1)
                            wait(e, s_q, 4 * j + q - 3)
                            for half in range(2):
                                nc.scalar.activation(RE[:, q, half, :].rearrange("p (s e) -> p s e", s=2),
                                                     ps[:, 2 + 2 * (q % 2):4 + 2 * (q % 2), half * 256:(half + 1) * 256],
                                                     ACT.Identity, bias=bz[:, half:half + 1]).then_inc(s_r, 1)
                        e.wait_ge(s_q, 4 * j + 4)
                        col = bass.ds(j * P, P) if not first(j) else slice(j * P, j * P + P)
                        nc.scalar.activation(logit[:, col], ps[:, 6 + par, 0:P], ACT.Copy).then_inc(s_lge, 1)
                    pairs(e, window)

                @block.vector
                def _(e):
                    v = nc.vector
                    for par in range(2):
                        v.tensor_copy(stage[:, par, 0:CH], src_jc[:, par, :]).then_inc(s_ready[par], 1)
                    v.memset(SAME[0:C, :, :, :], 0.0)
                    v.memset(SAME[2 * C:3 * C, :, :, :], 0.0)
                    ch = Chain(e, s_c)
                    ch.mark(v.tensor_tensor(bz[:, 0:2], bz[:, 0:2], bz[:, 2:4], ALU.add))
                    ch.link(v.memset(attp[:, :, :], 0.0))
                    for h in range(H):
                        a, half = h % 4, h // 4
                        v.tensor_copy(attp[a * C:(a + 1) * C, half, h:P:40], attc[a * C:(a + 1) * C, half:half + 1].to_broadcast([C, 4]))
                    v.memset(featT[C:C + 1, :], 1.0)
                    v.tensor_tensor(wz[:, :], wl_aug[:, :], wr_aug[:, :], ALU.add).then_inc(s_init, 1)
                    for b in range(NB):
                        z = self_z[:, b % 2, :]
                        e.wait_ge(s_sr, b + 1)
                        v.scalar_tensor_tensor(z, z, 0.2, z, ALU.mult, ALU.max).then_inc(s_se, 1)
                        e.wait_ge(s_se, b + 1)
                        v.tensor_tensor(z, z, attb[:, :], ALU.mult).then_inc(s_sp, 1)
                        e.wait_ge(s_sp, b + 1)
                        v.tensor_reduce(lself[:, b, :], z.rearrange("p (h c) -> p h c", c=C), AX.X, ALU.add).then_inc(s_sl, 1)

                    def window(j, par, i):
                        e.wait_ge(s_tr, j + 1)
                        loaded(e, j, par, i)
                        wait(e, s_q, 4 * j - 4)
                        wait(e, s_xt, 8 * j)
                        for k in range(8):
                            v.tensor_tensor_scan(XT[:, par, k, :], SAME[:, par, k, :], psf[:, k * P:(k + 1) * P],
                                                 0.0 if first(j) and j == 0 else XT[:, 1 - par, k, P - 1:P],
                                                 ALU.mult, ALU.add).then_inc(s_xt, 1)
                        if not (first(j) and j + 2 >= J):
                            e.wait_ge(s_gate, j + 1)
                            e.wait_ge(s_xs, 4 * j + 4)
                            at = bass.ds(j, 1) if not first(j) else slice(j, j + 1)
                            v.tensor_copy(stage[:, par, 0:CH], src_next[:, at, :].rearrange("p a c -> p (a c)")).then_inc(s_ready[par], 1)
                        for q in range(4):
                            e.wait_ge(s_r, 8 * j + 2 * q + 2)
                            zc = RE[:, q, :, :].rearrange("p h e -> p (h e)")
                            v.scalar_tensor_tensor(zc, zc, 0.2, zc, ALU.mult, ALU.max).then_inc(s_e, 1)
                    pairs(e, window)

            with Phase() as ph:
                s_c, s_d, s_e, s_t, s_m, s_p = (ph.sem(n) for n in ("dve_step", "turned_ends", "exp", "turned", "maxima_kept", "probs_kept"))
                block = ph.block()
                ends = small[:, 0:2 * CH].rearrange("p (k c) -> p k c", k=2)
                left, right = small[0:H, 64:64 + CH + 1], small[0:H, 96:96 + CH + 1]
                own = small[:, 128:128 + 2 * CH].rearrange("p (k c) -> p k c", k=2)
                carry = small[:, 192:194]
                groups = [(g, min(4, J - g)) for g in range(0, J, 4)]

                def bank_view(bank, w):
                    return ps[:, bank, 0:w * P].rearrange("p (j c h) -> p j c h", c=CH, h=H)

                def kept(lo, g, w):
                    return pm[:, :, :].rearrange("p (c j) k -> p j c k", j=J)[:, g:g + w, :, lo:lo + H]

                @block.vector
                def _(e):
                    v = nc.vector
                    ch = Chain(e, s_c)
                    ch.mark(v.memset(small[0:H, 64:64 + 64], -BIG))
                    ch.mark(v.tensor_tensor_scan(SCAN_F, start_pen[:, :], logit[:, :], -BIG, ALU.add, ALU.max))
                    ch.link(v.tensor_tensor_scan(SCAN_B[:, ::-1], end_pen[:, ::-1], logit[:, ::-1], -BIG, ALU.add, ALU.max))
                    ch.mark(v.tensor_scalar(ends[:, 0, :], of_chunk[:, :], SCAN_F[:, CE - 1:CE], None, ALU.mult))
                    ch.mark(v.tensor_scalar(ends[:, 1, :], of_chunk[:, :], SCAN_B[:, 0:1], None, ALU.mult))
                    e.wait_ge(s_d, 1)
                    ch.mark(v.tensor_tensor_scan(left[:, 1:CH + 1], pens[:, 0, :], ps[0:H, 0, 0:CH], -BIG, ALU.add, ALU.max))
                    ch.mark(v.tensor_tensor_scan(right[:, 0:CH][:, ::-1], pens[:, 1, ::-1], ps[0:H, 0, CH:2 * CH][:, ::-1], -BIG, ALU.add, ALU.max))
                    e.wait_ge(s_d, 2)
                    ch.link(v.tensor_tensor(own, ps[:, 1, 0:2 * CH].rearrange("p (k c) -> p k c", k=2),
                                            of_chunk[:, None, :].to_broadcast([P, 2, CH]), ALU.mult))
                    ch.link(v.tensor_reduce(carry, own, AX.X, ALU.add))
                    ch.mark(v.tensor_tensor_scan(SCAN_F, start_pen[:, :], logit[:, :], carry[:, 0:1], ALU.add, ALU.max))
                    ch.link(v.tensor_tensor_scan(SCAN_B[:, ::-1], end_pen[:, ::-1], logit[:, ::-1], carry[:, 1:2], ALU.add, ALU.max))
                    ch.link(v.tensor_tensor(SCAN_F, SCAN_F, SCAN_B, ALU.max))
                    ch.link(v.tensor_tensor(logit[:, :], logit[:, :], SCAN_F, ALU.subtract))
                    for k, (g, w) in enumerate(groups):
                        e.wait_ge(s_t, k + 1)
                        lj = lastf[:, :].rearrange("p (c j) -> p j c", j=J)[:, g:g + w, :, None].to_broadcast([P, w, CH, H])
                        v.tensor_tensor(kept(H, g, w), bank_view(k, w), lj, ALU.mult).then_inc(s_m, 1)

                @block.scalar
                def _(e):
                    e.wait_ge(s_c, 13)
                    nc.scalar.activation(logit[:, :], logit[:, :], ACT.Exp).then_inc(s_e, 1)
                    for k, (g, w) in enumerate(groups):
                        e.wait_ge(s_t, len(groups) + k + 1)
                        nc.scalar.activation(kept(0, g, w), bank_view((k - 1) % 8, w), ACT.Copy).then_inc(s_p, 1)

                @block.tensor
                def _(e):
                    e.wait_ge(s_c, 5)
                    nc.tensor.matmul(ps[0:H, 0, 0:2 * CH], of_head[:, :], ends.rearrange("p k c -> p (k c)"), start=True, stop=True).then_inc(s_d, 1)
                    e.wait_ge(s_c, 7)
                    nc.tensor.matmul(ps[:, 1, 0:CH], of_headT[:, :], left[:, 0:CH], start=True, stop=True)
                    nc.tensor.matmul(ps[:, 1, CH:2 * CH], of_headT[:, :], right[:, 1:CH + 1], start=True, stop=True).then_inc(s_d, 1)
                    e.wait_ge(s_c, 12)
                    for k, (g, w) in enumerate(groups):
                        for t in range(w):
                            last = nc.tensor.transpose(ps[:, k, t * P:(t + 1) * P], SCAN_F[:, (g + t) * P:(g + t + 1) * P], ident[:, :])
                        last.then_inc(s_t, 1)
                    e.wait_ge(s_e, 1)
                    for k, (g, w) in enumerate(groups):
                        wait(e, s_m, k)
                        for t in range(w):
                            last = nc.tensor.transpose(ps[:, (k - 1) % 8, t * P:(t + 1) * P], logit[:, (g + t) * P:(g + t + 1) * P], ident[:, :])
                        last.then_inc(s_t, 1)

            def attention_values(v, slot, t4):
                v.tensor_copy(slotV[:, slot, :, HC:], pm[:, bass.ds(t4, ST), :])
                return v.tensor_tensor(slotV[:, slot, :, 0:HC].rearrange("p t (h c) -> p t h c", c=C),
                                pm[:, bass.ds(t4, ST), 0:H, None].to_broadcast([P, ST, H, C]),
                                xsr[:, bass.ds(t4, ST), None, 0:C].to_broadcast([P, ST, H, C]), ALU.mult)

            segment_sums(VW, attention_values, l)

            with Phase() as ph:
                s_c, s_x = ph.sem("dve_step"), ph.sem("exps")
                s_g, s_t, s_a, s_m = (ph.sem(n) for n in ("means", "turned", "turned_copied", "heads"))
                block = ph.block()
                G = 5
                NH = NB * H
                m1 = small[:, 0:NH].rearrange("p (b h) -> p b h", h=H)
                m2 = small[:, NH:2 * NH].rearrange("p (b h) -> p b h", h=H)
                w12 = small[:, 0:2 * NH]
                mx = small[:, 2 * NH:3 * NH].rearrange("p (b h) -> p b h", h=H)
                cb = small[:, 3 * NH:3 * NH + NB]
                bl_sum = small[:, 640:640 + C]
                own = work[:, 0:G * HC].rearrange("p (b h c) -> p b h c", h=H, c=C)
                AT = work[:, G * HC:3 * G * HC].rearrange("p (s b k n) -> p s b k n", s=2, b=G, k=2)

                @block.vector
                def _(e):
                    v = nc.vector
                    ch = Chain(e, s_c)
                    ch.mark(v.tensor_scalar(wlr[:, :, :], wlr[:, :, :], 1.0 / H, None, ALU.mult))
                    ch.link(v.tensor_reduce(bl_sum, vecs[:, 0, :].rearrange("p (h c) -> p c h", c=C), AX.X, ALU.add))
                    ch.mark(v.scalar_tensor_tensor(vecs[:, 1, 0:C], bl_sum, 1.0 / H, vecs[:, 1, 0:C], ALU.mult, ALU.add))
                    ch.link(v.tensor_scalar(cb, count[:, :], -1.0, BIG, ALU.add, ALU.mult))
                    ch.link(v.tensor_tensor(m1, acc[:, :, HC + H:], cb[:, :, None].to_broadcast([P, NB, H]), ALU.add))
                    ch.link(v.tensor_tensor(mx, m1, lself[:, :, :], ALU.max))
                    ch.link(v.tensor_tensor(m1, m1, mx, ALU.subtract))
                    ch.link(v.tensor_tensor(m2, lself[:, :, :], mx, ALU.subtract))
                    e.wait_ge(s_x, 1)
                    ch.link(v.tensor_tensor(mx, acc[:, :, HC:HC + H], m1, ALU.mult))
                    ch.link(v.tensor_tensor(mx, mx, m2, ALU.add))
                    ch.link(v.tensor_scalar(mx, mx, 1e-16, None, ALU.add))
                    ch.link(v.reciprocal(mx, mx))
                    ch.mark(v.tensor_tensor(m1, m1, mx, ALU.mult))
                    ch.link(v.tensor_tensor(m2, m2, mx, ALU.mult))

                    for g in range(NB // G):
                        lo, hi = g * G, (g + 1) * G
                        a = acc[:, lo:hi, 0:HC].rearrange("p b (h c) -> p b h c", c=C)
                        ch.mark(v.tensor_tensor(a, a, m1[:, lo:hi, :, None].to_broadcast([P, G, H, C]), ALU.mult))
                        ch.link(v.tensor_tensor(own, feat[:, lo:hi, None, :].to_broadcast([P, G, H, C]),
                                                m2[:, lo:hi, :, None].to_broadcast([P, G, H, C]), ALU.mult))
                        v.tensor_tensor(a, a, own, ALU.add).then_inc(s_g, 1)
                        e.wait_ge(s_g, g + 1)
                    for g in (0, 3):
                        n = min(3, NB // G - g)
                        e.wait_ge(s_m, g + n)
                        v.tensor_tensor(conv[:, g * G:(g + n) * G, :], ps[:, 6 + g // 3, 0:n * G * C].rearrange("p (b c) -> p b c", c=C),
                                        vecs[:, 1, None, 0:C].to_broadcast([P, n * G, C]), ALU.add)

                @block.tensor
                def _(e):
                    def heads(g):
                        e.wait_ge(s_a, g + 1)
                        for b in range(G):
                            at = (g % 3) * G * C + b * C
                            for k in range(2):
                                last = nc.tensor.matmul(ps[:, 6 + g // 3, at:at + C], AT[:, g % 2, b, k, :], wlr[:, k, :],
                                                        start=(k == 0), stop=(k == 1))
                        last.then_inc(s_m, 1)
                    for g in range(NB // G):
                        e.wait_ge(s_g, g + 1)
                        wait(e, s_a, g - 1)
                        for b in range(G):
                            for k in range(2):
                                n = (g % 2) * 3 * 512 + (2 * b + k) * P
                                last = nc.tensor.transpose(psf[:, n:n + P], acc[:, g * G + b, k * P:(k + 1) * P], ident[:, :])
                        last.then_inc(s_t, 1)
                        if g:
                            heads(g - 1)
                    heads(NB // G - 1)

                @block.scalar
                def _(e):
                    e.wait_ge(s_c, 8)
                    nc.scalar.activation(w12, w12, ACT.Exp).then_inc(s_x, 1)
                    for g in range(NB // G):
                        e.wait_ge(s_t, g + 1)
                        wait(e, s_m, g - 1)
                        nc.scalar.activation(AT[:, g % 2, :, :, :].rearrange("p b k n -> p (b k n)"),
                                             psf[:, (g % 2) * 3 * 512:(g % 2) * 3 * 512 + 2 * G * P], ACT.Copy).then_inc(s_a, 1)

            with Phase() as ph:
                s_c, s_m, s_q = (ph.sem(n) for n in ("dve_step", "node_sums", "root"))
                block = ph.block()
                flat = work[:, 0:NB * C].rearrange("p (b c) -> p b c", c=C)
                part = small[:, 0:C]
                mean, var, rstd = (small[:, 32 * k:32 * k + C] for k in range(1, 4))

                @block.vector
                def _(e):
                    v = nc.vector
                    ch = Chain(e, s_c)
                    def masked(a):
                        return v.tensor_scalar(a[:, NB - 1, :], a[:, NB - 1, :], nodemask[:, 0:1], None, ALU.mult)
                    if l < L - 1:
                        ch.link(v.scalar_tensor_tensor(conv[:, :, :], conv[:, :, :], 0.01, conv[:, :, :], ALU.mult, ALU.max))
                    ch.link(v.tensor_tensor(feat[:, :, :], feat[:, :, :], conv[:, :, :], ALU.add))
                    ch.link(masked(feat))
                    ch.link(v.tensor_reduce(part, feat[:, :, :].rearrange("p b c -> p c b"), AX.X, ALU.add))
                    e.wait_ge(s_m, 1)
                    ch.link(v.tensor_scalar(mean, ps[:, 0, 0:C], 1.0 / N, None, ALU.mult))
                    ch.link(v.tensor_tensor(feat[:, :, :], feat[:, :, :], mean[:, None, :].to_broadcast([P, NB, C]), ALU.subtract))
                    ch.link(v.tensor_tensor(flat, feat[:, :, :], feat[:, :, :], ALU.mult))
                    ch.link(masked(flat))
                    ch.link(v.tensor_reduce(part, flat.rearrange("p b c -> p c b"), AX.X, ALU.add))
                    e.wait_ge(s_m, 2)
                    ch.link(v.tensor_scalar(var, ps[:, 1, 0:C], 1.0 / N, EPS, ALU.mult, ALU.add))
                    e.wait_ge(s_q, 1)
                    ch.link(v.reciprocal(rstd, rstd))
                    ch.link(v.tensor_tensor(rstd, rstd, vecs[:, 2, 0:C], ALU.mult))
                    ch.link(v.tensor_tensor(feat[:, :, :], feat[:, :, :], rstd[:, None, :].to_broadcast([P, NB, C]), ALU.mult))
                    ch.link(v.tensor_tensor(feat[:, :, :], feat[:, :, :], vecs[:, 3, None, 0:C].to_broadcast([P, NB, C]), ALU.add))
                    if l == L - 1:
                        ch.link(v.tensor_tensor(xres[:, :, :], xres[:, :, :], feat[:, :, :], ALU.add))
                base = 4 if l < L - 1 else 3

                @block.tensor
                def _(e):
                    e.wait_ge(s_c, base)
                    nc.tensor.matmul(ps[:, 0, 0:C], ones[:, :], part, start=True, stop=True).then_inc(s_m, 1)
                    e.wait_ge(s_c, base + 5)
                    nc.tensor.matmul(ps[:, 1, 0:C], ones[:, :], part, start=True, stop=True).then_inc(s_m, 1)

                @block.scalar
                def _(e):
                    e.wait_ge(s_c, base + 6)
                    nc.scalar.activation(rstd, var, ACT.Sqrt).then_inc(s_q, 1)

        with Phase() as ph:
            s_o = ph.sem("out_written")
            block = ph.block()

            @block.sync
            def _(e):
                e.dma_start(out[0:(NB - 1) * P, :].rearrange("(b p) c -> p b c", p=P), xres[:, 0:NB - 1, :]).then_inc(s_o, 16)
                e.dma_start(out[(NB - 1) * P:N, :], xres[0:REAL, NB - 1, :]).then_inc(s_o, 16)
                e.wait_ge(s_o, 32)


NAMES = ("x", "src", "dst", "edge_attr_32", "edge_attr_4", "L0_gnn_W1", "L0_gnn_b1", "L0_gnn_W2", "L0_gnn_b2",
         "L0_gnn_si_w0", "L0_gnn_si_w1", "L1_gnn_Wl", "L1_gnn_bl", "L1_gnn_Wr", "L1_gnn_br", "L1_gnn_att",
         "L1_gnn_conv_bias", "L1_gnn_bn_gamma", "L1_gnn_bn_beta")


def kernel(**inputs):
    import numpy as np
    import concourse.bacc as bacc
    from concourse.bass_utils import run_bass_kernel_spmd as run

    nc = bacc.Bacc("TRN2", target_bir_lowering=False, num_devices=1)
    arrays, aps = {}, {}
    for name in NAMES:
        a = np.ascontiguousarray(inputs[name])
        arrays[name + "_in"] = a
        aps[name] = nc.dram_tensor(name + "_in", a.shape, mybir.dt.from_np(a.dtype), kind="ExternalInput").ap()
    out = nc.dram_tensor("out", (N, C), F32, kind="ExternalOutput").ap()
    build(nc, aps, out)
    return run(nc, [arrays], core_ids=[0]).results[0]["out"]
```
